# Optimizing a Trainium2 kernel written in Bass

```python
import numpy as np
import jax
import jax.numpy as jnp

def _softmax(x, axis=-1):
    return jax.nn.softmax(x, axis=axis)

def _gelu(x):
    return jax.nn.gelu(x, approximate=True)

def _silu(x):
    return jax.nn.silu(x)

def _sigmoid(x):
    return jax.nn.sigmoid(x)

def _layernorm(x, axis=-1, eps=1e-05):
    m = jnp.mean(x, axis=axis, keepdims=True)
    v = jnp.var(x, axis=axis, keepdims=True)
    return (x - m) / jnp.sqrt(v + eps)

def _scatter_add(tgt, idx, src, axis=0):
    return tgt.at[idx].add(src)

def _segment_sum(src, seg, n):
    return jax.ops.segment_sum(src, seg, n)
kernel_name = 'mk_perceiver_d2_seqx_r4_884669'

def setup_inputs(seed: int=0):
    np.random.seed(seed)
    _w = jnp.asarray

    def _rec_inputs():
        import jax
        import jax.numpy as jnp
        _rk = jax.random.key(seed)
        x = -0.0002928 + 1 * jax.random.normal(jax.random.fold_in(_rk, 1), (1, 128, 256), jnp.float32)
        _lenS = 128 - jax.random.randint(jax.random.fold_in(_rk, 7), (1,), 0, max(1, 128 // 4) + 1, jnp.int32)
        _lenS2 = 12544 - jax.random.randint(jax.random.fold_in(_rk, 8), (1,), 0, max(1, 12544 // 4) + 1, jnp.int32)
        _ctx_1024P = jax.random.normal(jax.random.fold_in(_rk, 11), (1, 16, 256), jnp.float32)
        _ctx_1024c = jax.random.dirichlet(jax.random.fold_in(_rk, 511), 0.3 * jnp.ones((16,), jnp.float32), (1, 12544))
        _ctx_1024t = jnp.einsum('bsk,bkd->bsd', _ctx_1024c, _ctx_1024P)
        _ctx_1024t = _ctx_1024t * jax.lax.rsqrt(jnp.mean(jnp.square(_ctx_1024t)) + 1e-12) * 0.953939
        ctx_1024 = 4.13588e-05 + 0.999923 * (_ctx_1024t + 0.3 * jax.random.normal(jax.random.fold_in(_rk, 611), (1, 12544, 256), jnp.float32))
        fside_Bx16xSxS2_0 = -6.00028e-06 + 0.100001 * jax.random.normal(jax.random.fold_in(_rk, 12), (1, 16, 128, 12544), jnp.float32)
        return (x, ctx_1024, fside_Bx16xSxS2_0)
    x, ctx_1024, fside_Bx16xSxS2_0 = _rec_inputs()

    def _L0_xattn_setup():
        import jax, jax.numpy as jnp
        import numpy as np
        B, S, T = (4, 256, 512)
        HID = 256
        NH = 16
        NKV = 4
        HD = HID // NH
        key = jax.random.key(seed)
        ks = jax.random.split(key, 6)
        scale = 1.0 / np.sqrt(HID)
        return {'x': jax.random.normal(ks[0], (B, S, HID), dtype=jnp.float32), 'context': jax.random.normal(ks[1], (B, T, HID), dtype=jnp.float32), 'Wq': jax.random.normal(ks[2], (NH * HD, HID), dtype=jnp.float32) * scale, 'Wk': jax.random.normal(ks[3], (NKV * HD, HID), dtype=jnp.float32) * scale, 'Wv': jax.random.normal(ks[4], (NKV * HD, HID), dtype=jnp.float32) * scale, 'Wo': jax.random.normal(ks[5], (HID, NH * HD), dtype=jnp.float32) * scale}
    _L0_xattn_all = _L0_xattn_setup()
    _L0_xattn_in = {k: v for k, v in _L0_xattn_all.items() if k in ('Wq', 'Wk', 'Wv', 'Wo')}
    del _L0_xattn_all

    def _L0_attn_setup():
        import jax, jax.numpy as jnp
        import numpy as np
        EMBED_DIM = 256
        NUM_HEADS = 16
        HEAD_DIM = EMBED_DIM // NUM_HEADS
        SEQ_LEN = 256
        BATCH = 4
        MAX_REL_POS = 2

        def _rel_index(length_q, length_k):
            q = jnp.arange(length_q)[:, None]
            k = jnp.arange(length_k)[None, :]
            return jnp.clip(k - q, -MAX_REL_POS, MAX_REL_POS) + MAX_REL_POS
        key = jax.random.key(seed)
        ks = jax.random.split(key, 12)
        s = 1.0 / np.sqrt(EMBED_DIM)
        x = jax.random.normal(ks[0], (BATCH, SEQ_LEN, EMBED_DIM), dtype=jnp.float32)
        W_q = jax.random.normal(ks[1], (EMBED_DIM, EMBED_DIM), dtype=jnp.float32) * s
        b_q = jnp.zeros((EMBED_DIM,), dtype=jnp.float32)
        W_k = jax.random.normal(ks[2], (EMBED_DIM, EMBED_DIM), dtype=jnp.float32) * s
        b_k = jnp.zeros((EMBED_DIM,), dtype=jnp.float32)
        W_v = jax.random.normal(ks[3], (EMBED_DIM, EMBED_DIM), dtype=jnp.float32) * s
        b_v = jnp.zeros((EMBED_DIM,), dtype=jnp.float32)
        W_o = jax.random.normal(ks[4], (EMBED_DIM, EMBED_DIM), dtype=jnp.float32) * s
        b_o = jnp.zeros((EMBED_DIM,), dtype=jnp.float32)
        lim = float(np.sqrt(6.0 / (2 * MAX_REL_POS + 1 + HEAD_DIM)))
        rel_k_table = jax.random.uniform(ks[5], (2 * MAX_REL_POS + 1, HEAD_DIM), jnp.float32, -lim, lim)
        rel_v_table = jax.random.uniform(ks[6], (2 * MAX_REL_POS + 1, HEAD_DIM), jnp.float32, -lim, lim)
        return {'x': x, 'W_q': W_q, 'b_q': b_q, 'W_k': W_k, 'b_k': b_k, 'W_v': W_v, 'b_v': b_v, 'W_o': W_o, 'b_o': b_o, 'rel_k_table': rel_k_table, 'rel_v_table': rel_v_table}
    _L0_attn_all = _L0_attn_setup()
    _L0_attn_in = {k: v for k, v in _L0_attn_all.items() if k in ('W_q', 'b_q', 'W_k', 'b_k', 'W_v', 'b_v', 'W_o', 'b_o', 'rel_k_table', 'rel_v_table')}
    del _L0_attn_all

    def _L0_ffn_setup():
        import jax, jax.numpy as jnp
        import numpy as np
        DIM = 256
        DEPTH = 6
        HEADS = 16
        DIM_HEAD = 64
        WINDOW = 64
        INNER = HEADS * DIM_HEAD
        DIM_INNER = int(DIM * 4 * 2 / 3)
        QK_SCALE = 8.0

        def shift_tokens(t):
            a, s = jnp.split(t, 2, -1)
            s = jnp.pad(s, ((0, 0), (1, 0), (0, 0)))[:, :-1]
            return jnp.concatenate([a, s], -1)

        def l2norm(t):
            return t / jnp.maximum(jnp.linalg.norm(t, axis=-1, keepdims=True), 1e-12)

        def rotate_half(x):
            x1, x2 = jnp.split(x, 2, -1)
            return jnp.concatenate([-x2, x1], -1)

        def rotary_tables(n):
            half = jnp.arange(0, DIM_HEAD, 2, dtype=jnp.float32)
            inv_freq = 1.0 / 10000.0 ** (half / DIM_HEAD)
            t = jnp.arange(n, dtype=jnp.float32)
            freqs = t[:, None] * inv_freq[None, :]
            freqs = jnp.concatenate([freqs, freqs], -1)
            base_scale = (half + 0.4 * DIM_HEAD) / (1.4 * DIM_HEAD)
            power = (t - n // 2) / (WINDOW // 2)
            scale = base_scale[None, :] ** power[:, None]
            scale = jnp.concatenate([scale, scale], -1)
            return (freqs, scale)

        def local_attention(q, k, v):
            b, h, n, d = q.shape
            w = WINDOW
            nw = n // w
            bq = q.reshape(b, h, nw, w, d)
            bk = k.reshape(b, h, nw, w, d)
            bv = v.reshape(b, h, nw, w, d)

            def look(t):
                p = jnp.pad(t, ((0, 0), (0, 0), (1, 0), (0, 0), (0, 0)))
                return jnp.concatenate([p[:, :, :nw], p[:, :, 1:]], axis=3)
            bk2, bv2 = (look(bk), look(bv))
            seq = jnp.arange(n).reshape(nw, w)
            seq_p = jnp.pad(seq, ((1, 0), (0, 0)), constant_values=-1)
            jt = jnp.concatenate([seq_p[:nw], seq_p[1:]], axis=1)
            it = seq[:, :, None]
            jb = jt[:, None, :]
            mask = (it < jb) | (it > jb + w) | (jb == -1)
            sim = jnp.einsum('bhwie,bhwje->bhwij', bq, bk2) * QK_SCALE
            sim = jnp.where(mask, -jnp.finfo(sim.dtype).max, sim)
            attn = jax.nn.softmax(sim, -1)
            out = jnp.einsum('bhwij,bhwje->bhwie', attn, bv2)
            return out.reshape(b, h, n, d)

        def attn_layer(x, Wqkv, qs, ksc, Wo):
            b, n, _ = x.shape
            qkv = x @ Wqkv
            q, k, v = jnp.split(qkv, 3, -1)
            sh = lambda t: t.reshape(b, n, HEADS, DIM_HEAD).transpose(0, 2, 1, 3)
            q, k, v = (sh(q), sh(k), sh(v))
            q = l2norm(q) * qs
            k = l2norm(k) * ksc
            freqs, scale = rotary_tables(n)
            cos, sin = (jnp.cos(freqs), jnp.sin(freqs))
            q = q * cos * scale + rotate_half(q) * sin * scale
            inv = 1.0 / scale
            k = k * cos * inv + rotate_half(k) * sin * inv
            out = local_attention(q, k, v)
            out = out.transpose(0, 2, 1, 3).reshape(b, n, INNER)
            return out @ Wo

        def ffn_layer(x, g, bln, W1, b1, W2, b2):
            mu = x.mean(-1, keepdims=True)
            var = ((x - mu) ** 2).mean(-1, keepdims=True)
            xn = (x - mu) / jnp.sqrt(var + 1e-05) * g + bln
            hg = xn @ W1 + b1
            a, gate = jnp.split(hg, 2, -1)
            return a * jax.nn.gelu(gate, approximate=False) @ W2 + b2
        key = jax.random.key(seed)
        ks = jax.random.split(key, 8)
        B, N = (2, 512)
        init = lambda k, shape: jax.random.normal(k, shape, jnp.float32) * 0.02
        return {'x': jax.random.normal(ks[0], (B, N, DIM), jnp.float32), 'Wqkv': init(ks[1], (DEPTH, DIM, 3 * INNER)), 'q_scale': jnp.ones((DEPTH, DIM_HEAD), jnp.float32), 'k_scale': jnp.ones((DEPTH, DIM_HEAD), jnp.float32), 'Wo': init(ks[2], (DEPTH, INNER, DIM)), 'ln_g': jnp.ones((DEPTH, DIM), jnp.float32), 'ln_b': jnp.zeros((DEPTH, DIM), jnp.float32), 'W1': init(ks[3], (DEPTH, DIM, 2 * DIM_INNER)), 'b1': jnp.zeros((DEPTH, 2 * DIM_INNER), jnp.float32), 'W2': init(ks[4], (DEPTH, DIM_INNER, DIM)), 'b2': jnp.zeros((DEPTH, DIM), jnp.float32)}
    _L0_ffn_all = _L0_ffn_setup()
    _L0_ffn_in = {k: v for k, v in _L0_ffn_all.items() if k in ('Wqkv', 'q_scale', 'k_scale', 'Wo', 'ln_g', 'ln_b', 'W1', 'b1', 'W2', 'b2')}
    del _L0_ffn_all

    def _L1_xattn_setup():
        import jax, jax.numpy as jnp
        import numpy as np
        import math
        H = 16
        D = 256
        FF = 1024
        DK = D // H
        EPS = 1e-05

        def layer_norm(x, g, b):
            mu = jnp.mean(x, axis=-1, keepdims=True)
            var = jnp.var(x, axis=-1, keepdims=True)
            return (x - mu) * jax.lax.rsqrt(var + EPS) * g + b
        key = jax.random.key(seed)
        ks = jax.random.split(key, 16)
        B, S = (2, 512)
        s = 1.0 / math.sqrt(D)
        return {'x_q': jax.random.normal(ks[0], (B, S, D), jnp.float32), 'x_kv': jax.random.normal(ks[1], (B, S, D), jnp.float32), 'bias': jax.random.normal(ks[2], (B, H, S, S), jnp.float32) * 0.1, 'Wq': jax.random.normal(ks[3], (D, D), jnp.float32) * s, 'Wk': jax.random.normal(ks[4], (D, D), jnp.float32) * s, 'Wv': jax.random.normal(ks[5], (D, D), jnp.float32) * s, 'Wo': jax.random.normal(ks[6], (D, D), jnp.float32) * s, 'W1': jax.random.normal(ks[7], (FF, D), jnp.float32) * s, 'b1': jnp.zeros((FF,), jnp.float32), 'W2': jax.random.normal(ks[8], (D, FF), jnp.float32) * (1.0 / math.sqrt(FF)), 'b2': jnp.zeros((D,), jnp.float32), 'g1': jnp.ones((D,), jnp.float32), 'be1': jnp.zeros((D,), jnp.float32), 'g2': jnp.ones((D,), jnp.float32), 'be2': jnp.zeros((D,), jnp.float32)}
    _L1_xattn_all = _L1_xattn_setup()
    _L1_xattn_in = {k: v for k, v in _L1_xattn_all.items() if k in ('Wq', 'Wk', 'Wv', 'Wo', 'W1', 'b1', 'W2', 'b2', 'g1', 'be1', 'g2', 'be2')}
    del _L1_xattn_all

    def _L1_attn_setup():
        import jax, jax.numpy as jnp
        import numpy as np
        B, T, D, H = (8, 512, 256, 2)
        DK = D // H
        GAMMA_INIT, LAMBDA_INIT = (0.9, 0.1)
        key = jax.random.key(seed)
        ks = jax.random.split(key, 8)
        xav = float(np.sqrt(6.0 / (D + D)))

        def lin(k):
            return jax.random.uniform(k, (D, D), jnp.float32, -xav, xav)
        logit_g = float(np.log(GAMMA_INIT / (1.0 - GAMMA_INIT)))
        logit_l = float(np.log(LAMBDA_INIT / (1.0 - LAMBDA_INIT)))
        return {'x': jax.random.normal(ks[0], (B, T, D), jnp.float32), 'Wq': lin(ks[1]), 'Wk': lin(ks[2]), 'Wv': lin(ks[3]), 'Wo': lin(ks[4]), 'W_gamma': 0.02 * jax.random.normal(ks[5], (H, DK), jnp.float32), 'b_gamma': jnp.full((H, DK), logit_g, jnp.float32), 'W_lambda': 0.02 * jax.random.normal(ks[6], (H, DK), jnp.float32), 'b_lambda': jnp.full((H, DK), logit_l, jnp.float32)}
    _L1_attn_all = _L1_attn_setup()
    _L1_attn_in = {k: v for k, v in _L1_attn_all.items() if k in ('Wq', 'Wk', 'Wv', 'Wo', 'W_gamma', 'b_gamma', 'W_lambda', 'b_lambda')}
    del _L1_attn_all

    def _L1_ffn_setup():
        import jax, jax.numpy as jnp
        import numpy as np
        H = 256
        E = 8
        F = 1024
        K = 2
        key = jax.random.key(seed)
        ks = jax.random.split(key, 6)
        s_in = 1.0 / np.sqrt(H)
        s_ff = 1.0 / np.sqrt(F)
        return {'hidden_states': jax.random.normal(ks[0], (4, 512, H), dtype=jnp.float32), 'gate_w': jax.random.uniform(ks[1], (H, E), jnp.float32, -s_in, s_in), 'W1': jax.random.uniform(ks[2], (E, H, F), jnp.float32, -s_in, s_in), 'b1': jax.random.uniform(ks[3], (E, F), jnp.float32, -s_in, s_in), 'W2': jax.random.uniform(ks[4], (E, F, H), jnp.float32, -s_ff, s_ff), 'b2': jax.random.uniform(ks[5], (E, H), jnp.float32, -s_ff, s_ff)}
    _L1_ffn_all = _L1_ffn_setup()
    _L1_ffn_in = {k: v for k, v in _L1_ffn_all.items() if k in ('gate_w', 'W1', 'b1', 'W2', 'b2')}
    del _L1_ffn_all
    return {'x': x, 'ctx_1024': ctx_1024, 'fside_Bx16xSxS2_0': fside_Bx16xSxS2_0, 'L0_xattn_Wq': _L0_xattn_in['Wq'], 'L0_xattn_Wk': _L0_xattn_in['Wk'], 'L0_xattn_Wv': _L0_xattn_in['Wv'], 'L0_xattn_Wo': _L0_xattn_in['Wo'], 'L0_attn_W_q': _L0_attn_in['W_q'], 'L0_attn_b_q': _L0_attn_in['b_q'], 'L0_attn_W_k': _L0_attn_in['W_k'], 'L0_attn_b_k': _L0_attn_in['b_k'], 'L0_attn_W_v': _L0_attn_in['W_v'], 'L0_attn_b_v': _L0_attn_in['b_v'], 'L0_attn_W_o': _L0_attn_in['W_o'], 'L0_attn_b_o': _L0_attn_in['b_o'], 'L0_attn_rel_k_table': _L0_attn_in['rel_k_table'], 'L0_attn_rel_v_table': _L0_attn_in['rel_v_table'], 'L0_ffn_Wqkv': _L0_ffn_in['Wqkv'], 'L0_ffn_q_scale': _L0_ffn_in['q_scale'], 'L0_ffn_k_scale': _L0_ffn_in['k_scale'], 'L0_ffn_Wo': _L0_ffn_in['Wo'], 'L0_ffn_ln_g': _L0_ffn_in['ln_g'], 'L0_ffn_ln_b': _L0_ffn_in['ln_b'], 'L0_ffn_W1': _L0_ffn_in['W1'], 'L0_ffn_b1': _L0_ffn_in['b1'], 'L0_ffn_W2': _L0_ffn_in['W2'], 'L0_ffn_b2': _L0_ffn_in['b2'], 'L1_xattn_Wq': _L1_xattn_in['Wq'], 'L1_xattn_Wk': _L1_xattn_in['Wk'], 'L1_xattn_Wv': _L1_xattn_in['Wv'], 'L1_xattn_Wo': _L1_xattn_in['Wo'], 'L1_xattn_W1': _L1_xattn_in['W1'], 'L1_xattn_b1': _L1_xattn_in['b1'], 'L1_xattn_W2': _L1_xattn_in['W2'], 'L1_xattn_b2': _L1_xattn_in['b2'], 'L1_xattn_g1': _L1_xattn_in['g1'], 'L1_xattn_be1': _L1_xattn_in['be1'], 'L1_xattn_g2': _L1_xattn_in['g2'], 'L1_xattn_be2': _L1_xattn_in['be2'], 'L1_attn_Wq': _L1_attn_in['Wq'], 'L1_attn_Wk': _L1_attn_in['Wk'], 'L1_attn_Wv': _L1_attn_in['Wv'], 'L1_attn_Wo': _L1_attn_in['Wo'], 'L1_attn_W_gamma': _L1_attn_in['W_gamma'], 'L1_attn_b_gamma': _L1_attn_in['b_gamma'], 'L1_attn_W_lambda': _L1_attn_in['W_lambda'], 'L1_attn_b_lambda': _L1_attn_in['b_lambda'], 'L1_ffn_gate_w': _L1_ffn_in['gate_w'], 'L1_ffn_W1': _L1_ffn_in['W1'], 'L1_ffn_b1': _L1_ffn_in['b1'], 'L1_ffn_W2': _L1_ffn_in['W2'], 'L1_ffn_b2': _L1_ffn_in['b2']}

def reference(x, ctx_1024, fside_Bx16xSxS2_0, L0_xattn_Wq, L0_xattn_Wk, L0_xattn_Wv, L0_xattn_Wo, L0_attn_W_q, L0_attn_b_q, L0_attn_W_k, L0_attn_b_k, L0_attn_W_v, L0_attn_b_v, L0_attn_W_o, L0_attn_b_o, L0_attn_rel_k_table, L0_attn_rel_v_table, L0_ffn_Wqkv, L0_ffn_q_scale, L0_ffn_k_scale, L0_ffn_Wo, L0_ffn_ln_g, L0_ffn_ln_b, L0_ffn_W1, L0_ffn_b1, L0_ffn_W2, L0_ffn_b2, L1_xattn_Wq, L1_xattn_Wk, L1_xattn_Wv, L1_xattn_Wo, L1_xattn_W1, L1_xattn_b1, L1_xattn_W2, L1_xattn_b2, L1_xattn_g1, L1_xattn_be1, L1_xattn_g2, L1_xattn_be2, L1_attn_Wq, L1_attn_Wk, L1_attn_Wv, L1_attn_Wo, L1_attn_W_gamma, L1_attn_b_gamma, L1_attn_W_lambda, L1_attn_b_lambda, L1_ffn_gate_w, L1_ffn_W1, L1_ffn_b1, L1_ffn_W2, L1_ffn_b2):
    import jax
    import jax.numpy as jnp

    def _L0_xattn_ref(x, context, Wq, Wk, Wv, Wo):
        import jax, jax.numpy as jnp
        import numpy as np
        B, S, T = (4, 256, 512)
        HID = 256
        NH = 16
        NKV = 4
        HD = HID // NH
        Bx, Sx, _ = x.shape
        Tx = context.shape[1]
        rep = NH // NKV
        q = (x @ Wq.T).reshape(Bx, Sx, NKV, rep, HD)
        k = (context @ Wk.T).reshape(Bx, Tx, NKV, HD)
        v = (context @ Wv.T).reshape(Bx, Tx, NKV, HD)
        scale = 1.0 / jnp.sqrt(jnp.asarray(HD, dtype=q.dtype))
        scores = jnp.einsum('bsgrd,btgd->bgrst', q, k) * scale
        attn = jax.nn.softmax(scores, axis=-1)
        out = jnp.einsum('bgrst,btgd->bsgrd', attn, v)
        out = out.reshape(Bx, Sx, NH * HD)
        return out @ Wo.T

    def _L0_attn_ref(x, W_q, b_q, W_k, b_k, W_v, b_v, W_o, b_o, rel_k_table, rel_v_table):
        import jax, jax.numpy as jnp
        import numpy as np
        EMBED_DIM = 256
        NUM_HEADS = 16
        HEAD_DIM = EMBED_DIM // NUM_HEADS
        SEQ_LEN = 256
        BATCH = 4
        MAX_REL_POS = 2

        def _rel_index(length_q, length_k):
            q = jnp.arange(length_q)[:, None]
            k = jnp.arange(length_k)[None, :]
            return jnp.clip(k - q, -MAX_REL_POS, MAX_REL_POS) + MAX_REL_POS
        B, S, E = x.shape
        H, D = (NUM_HEADS, HEAD_DIM)
        scale = jnp.sqrt(jnp.asarray(D, x.dtype))
        Q = x @ W_q + b_q
        K = x @ W_k + b_k
        V = x @ W_v + b_v
        Qh = Q.reshape(B, S, H, D).transpose(0, 2, 1, 3)
        Kh = K.reshape(B, S, H, D).transpose(0, 2, 1, 3)
        Vh = V.reshape(B, S, H, D).transpose(0, 2, 1, 3)
        scores = jnp.einsum('bhqd,bhkd->bhqk', Qh, Kh)
        idx = _rel_index(S, S)
        rel_k = rel_k_table[idx]
        scores = (scores + jnp.einsum('bhqd,qkd->bhqk', Qh, rel_k)) / scale
        causal = jnp.tril(jnp.ones((S, S), dtype=bool))
        scores = jnp.where(causal[None, None], scores, jnp.asarray(-1000000000.0, scores.dtype))
        attn = jax.nn.softmax(scores, axis=-1)
        out = jnp.einsum('bhqk,bhkd->bhqd', attn, Vh)
        rel_v = rel_v_table[idx]
        out = out + jnp.einsum('bhqk,qkd->bhqd', attn, rel_v)
        out = out.transpose(0, 2, 1, 3).reshape(B, S, E)
        return out @ W_o + b_o

    def _L0_ffn_ref(x, Wqkv, q_scale, k_scale, Wo, ln_g, ln_b, W1, b1, W2, b2):
        import jax, jax.numpy as jnp
        import numpy as np
        DIM = 256
        DEPTH = 6
        HEADS = 16
        DIM_HEAD = 64
        WINDOW = 64
        INNER = HEADS * DIM_HEAD
        DIM_INNER = int(DIM * 4 * 2 / 3)
        QK_SCALE = 8.0

        def shift_tokens(t):
            a, s = jnp.split(t, 2, -1)
            s = jnp.pad(s, ((0, 0), (1, 0), (0, 0)))[:, :-1]
            return jnp.concatenate([a, s], -1)

        def l2norm(t):
            return t / jnp.maximum(jnp.linalg.norm(t, axis=-1, keepdims=True), 1e-12)

        def rotate_half(x):
            x1, x2 = jnp.split(x, 2, -1)
            return jnp.concatenate([-x2, x1], -1)

        def rotary_tables(n):
            half = jnp.arange(0, DIM_HEAD, 2, dtype=jnp.float32)
            inv_freq = 1.0 / 10000.0 ** (half / DIM_HEAD)
            t = jnp.arange(n, dtype=jnp.float32)
            freqs = t[:, None] * inv_freq[None, :]
            freqs = jnp.concatenate([freqs, freqs], -1)
            base_scale = (half + 0.4 * DIM_HEAD) / (1.4 * DIM_HEAD)
            power = (t - n // 2) / (WINDOW // 2)
            scale = base_scale[None, :] ** power[:, None]
            scale = jnp.concatenate([scale, scale], -1)
            return (freqs, scale)

        def local_attention(q, k, v):
            b, h, n, d = q.shape
            w = WINDOW
            nw = n // w
            bq = q.reshape(b, h, nw, w, d)
            bk = k.reshape(b, h, nw, w, d)
            bv = v.reshape(b, h, nw, w, d)

            def look(t):
                p = jnp.pad(t, ((0, 0), (0, 0), (1, 0), (0, 0), (0, 0)))
                return jnp.concatenate([p[:, :, :nw], p[:, :, 1:]], axis=3)
            bk2, bv2 = (look(bk), look(bv))
            seq = jnp.arange(n).reshape(nw, w)
            seq_p = jnp.pad(seq, ((1, 0), (0, 0)), constant_values=-1)
            jt = jnp.concatenate([seq_p[:nw], seq_p[1:]], axis=1)
            it = seq[:, :, None]
            jb = jt[:, None, :]
            mask = (it < jb) | (it > jb + w) | (jb == -1)
            sim = jnp.einsum('bhwie,bhwje->bhwij', bq, bk2) * QK_SCALE
            sim = jnp.where(mask, -jnp.finfo(sim.dtype).max, sim)
            attn = jax.nn.softmax(sim, -1)
            out = jnp.einsum('bhwij,bhwje->bhwie', attn, bv2)
            return out.reshape(b, h, n, d)

        def attn_layer(x, Wqkv, qs, ksc, Wo):
            b, n, _ = x.shape
            qkv = x @ Wqkv
            q, k, v = jnp.split(qkv, 3, -1)
            sh = lambda t: t.reshape(b, n, HEADS, DIM_HEAD).transpose(0, 2, 1, 3)
            q, k, v = (sh(q), sh(k), sh(v))
            q = l2norm(q) * qs
            k = l2norm(k) * ksc
            freqs, scale = rotary_tables(n)
            cos, sin = (jnp.cos(freqs), jnp.sin(freqs))
            q = q * cos * scale + rotate_half(q) * sin * scale
            inv = 1.0 / scale
            k = k * cos * inv + rotate_half(k) * sin * inv
            out = local_attention(q, k, v)
            out = out.transpose(0, 2, 1, 3).reshape(b, n, INNER)
            return out @ Wo

        def ffn_layer(x, g, bln, W1, b1, W2, b2):
            mu = x.mean(-1, keepdims=True)
            var = ((x - mu) ** 2).mean(-1, keepdims=True)
            xn = (x - mu) / jnp.sqrt(var + 1e-05) * g + bln
            hg = xn @ W1 + b1
            a, gate = jnp.split(hg, 2, -1)
            return a * jax.nn.gelu(gate, approximate=False) @ W2 + b2
        for i in range(DEPTH):
            x = attn_layer(shift_tokens(x), Wqkv[i], q_scale[i], k_scale[i], Wo[i]) + x
            x = ffn_layer(shift_tokens(x), ln_g[i], ln_b[i], W1[i], b1[i], W2[i], b2[i]) + x
        return x

    def _L1_xattn_ref(x_q, x_kv, bias, Wq, Wk, Wv, Wo, W1, b1, W2, b2, g1, be1, g2, be2):
        import jax, jax.numpy as jnp
        import numpy as np
        import math
        H = 16
        D = 256
        FF = 1024
        DK = D // H
        EPS = 1e-05

        def layer_norm(x, g, b):
            mu = jnp.mean(x, axis=-1, keepdims=True)
            var = jnp.var(x, axis=-1, keepdims=True)
            return (x - mu) * jax.lax.rsqrt(var + EPS) * g + b
        B, S, _ = x_q.shape

        def split(x):
            return x.reshape(B, -1, H, DK).transpose(0, 2, 1, 3)
        q = split(x_q @ Wq.T)
        k = split(x_kv @ Wk.T)
        v = split(x_kv @ Wv.T)
        scores = jnp.einsum('bhqd,bhkd->bhqk', q, k) / math.sqrt(DK) + bias
        p = jax.nn.softmax(scores, axis=-1)
        o = jnp.einsum('bhqk,bhkd->bhqd', p, v)
        o = o.transpose(0, 2, 1, 3).reshape(B, S, D)
        x = x_q + o @ Wo.T
        h = jax.nn.gelu(layer_norm(x, g1, be1) @ W1.T + b1, approximate=False)
        x = x + h @ W2.T + b2
        return layer_norm(x, g2, be2)

    def _L1_attn_ref(x, Wq, Wk, Wv, Wo, W_gamma, b_gamma, W_lambda, b_lambda):
        import jax, jax.numpy as jnp
        import numpy as np
        B, T, D, H = (8, 512, 256, 2)
        DK = D // H
        GAMMA_INIT, LAMBDA_INIT = (0.9, 0.1)
        Bn, Tn, Dn = x.shape

        def heads(w):
            return (x @ w.T).reshape(Bn, Tn, H, DK).transpose(0, 2, 1, 3)
        q, k, v = (heads(Wq), heads(Wk), heads(Wv))
        k = k / jnp.maximum(jnp.linalg.norm(k, axis=-1, keepdims=True), 1e-12)
        Wg = W_gamma[None, :, None, :]
        bg = b_gamma[None, :, None, :]
        Wl = W_lambda[None, :, None, :]
        bl = b_lambda[None, :, None, :]
        gamma = jax.nn.sigmoid(Wg * k + bg)
        lam = jax.nn.sigmoid(Wl * k + bl)
        rho = (1.0 - lam) * gamma
        qs = q.transpose(2, 0, 1, 3)
        ks_ = k.transpose(2, 0, 1, 3)
        vs = v.transpose(2, 0, 1, 3)
        rs = rho.transpose(2, 0, 1, 3)
        S0 = jnp.zeros((Bn, H, DK, DK), x.dtype)

        def step(S, inp):
            q_t, k_t, v_t, r_t = inp
            rho_col = r_t[:, :, None, :]
            outer = v_t[:, :, :, None] * k_t[:, :, None, :]
            S = rho_col * S + (1.0 - rho_col) * outer
            y_t = jnp.einsum('bhv,bhvk->bhk', q_t, S)
            return (S, y_t)
        _, ys = jax.lax.scan(step, S0, (qs, ks_, vs, rs))
        out = ys.transpose(1, 0, 2, 3).reshape(Bn, Tn, Dn)
        return out @ Wo.T

    def _L1_ffn_ref(hidden_states, gate_w, W1, b1, W2, b2):
        import jax, jax.numpy as jnp
        import numpy as np
        H = 256
        E = 8
        F = 1024
        K = 2
        B, S, D = hidden_states.shape
        x = hidden_states.reshape(-1, D)
        N = x.shape[0]
        gate_logits = x @ gate_w
        topk_logits, topk_idx = jax.lax.top_k(gate_logits, K)
        topk_w = jax.nn.softmax(topk_logits, axis=-1)
        combine = jnp.zeros((N, E), x.dtype).at[jnp.arange(N)[:, None], topk_idx].add(topk_w)
        h = jax.nn.gelu(jnp.einsum('nd,edf->nef', x, W1) + b1[None], approximate=False)
        expert_out = jnp.einsum('nef,efd->ned', h, W2) + b2[None]
        out = jnp.einsum('ne,ned->nd', combine, expert_out)
        return out.reshape(B, S, D)
    x = x + _L0_xattn_ref(_layernorm(x, axis=-1), ctx_1024, L0_xattn_Wq, L0_xattn_Wk, L0_xattn_Wv, L0_xattn_Wo)
    x = x + _L0_attn_ref(_layernorm(x, axis=-1), L0_attn_W_q, L0_attn_b_q, L0_attn_W_k, L0_attn_b_k, L0_attn_W_v, L0_attn_b_v, L0_attn_W_o, L0_attn_b_o, L0_attn_rel_k_table, L0_attn_rel_v_table)
    x = x + _L0_ffn_ref(_layernorm(x, axis=-1), L0_ffn_Wqkv, L0_ffn_q_scale, L0_ffn_k_scale, L0_ffn_Wo, L0_ffn_ln_g, L0_ffn_ln_b, L0_ffn_W1, L0_ffn_b1, L0_ffn_W2, L0_ffn_b2)
    x = x + _L1_xattn_ref(_layernorm(x, axis=-1), ctx_1024, fside_Bx16xSxS2_0, L1_xattn_Wq, L1_xattn_Wk, L1_xattn_Wv, L1_xattn_Wo, L1_xattn_W1, L1_xattn_b1, L1_xattn_W2, L1_xattn_b2, L1_xattn_g1, L1_xattn_be1, L1_xattn_g2, L1_xattn_be2)
    x = x + _L1_attn_ref(_layernorm(x, axis=-1), L1_attn_Wq, L1_attn_Wk, L1_attn_Wv, L1_attn_Wo, L1_attn_W_gamma, L1_attn_b_gamma, L1_attn_W_lambda, L1_attn_b_lambda)
    x = x + _L1_ffn_ref(_layernorm(x, axis=-1), L1_ffn_gate_w, L1_ffn_W1, L1_ffn_b1, L1_ffn_W2, L1_ffn_b2)
    return x

_drawn_inputs = setup_inputs


def setup_inputs(seed=0):
    import zlib

    import numpy as np

    out = dict(_drawn_inputs(seed))
    spreads = {'L0_attn_b_q': (0.0, 0.547),
     'L0_attn_b_k': (0.0, 2.0),
     'L0_attn_b_v': (0.0, 0.1),
     'L0_attn_b_o': (0.0, 0.1),
     'L0_ffn_q_scale': (1.0, 0.6),
     'L0_ffn_k_scale': (1.0, 0.6),
     'L0_ffn_ln_g': (1.0, 0.6),
     'L0_ffn_ln_b': (0.0, 0.8),
     'L0_ffn_b1': (0.0, 0.493),
     'L0_ffn_b2': (0.0, 0.1),
     'L1_xattn_b1': (0.0, 0.417),
     'L1_xattn_b2': (0.0, 0.309),
     'L1_xattn_g1': (1.0, 0.2),
     'L1_xattn_be1': (0.0, 0.376),
     'L1_xattn_g2': (1.0, 0.2),
     'L1_xattn_be2': (0.0, 0.1),
     'L1_attn_b_gamma': (2.1972246170043945, 0.6),
     'L1_attn_b_lambda': (-2.1972246170043945, 0.6)}
    factors = {'fside_Bx16xSxS2_0': 64.0,
     'L1_attn_W_gamma': 200.0,
     'L1_attn_W_lambda': 200.0,
     'L1_ffn_b1': 8.0,
     'L1_ffn_b2': 8.0}
    for name, (base, spread) in spreads.items():
        noise = np.random.default_rng([zlib.crc32(name.encode()), seed]).standard_normal(out[name].shape)
        drawn = base * np.exp(spread * noise) if base else spread * noise
        out[name] = jnp.asarray(drawn.astype(out[name].dtype))
    for name, factor in factors.items():
        out[name] = (out[name] * factor).astype(out[name].dtype)
    return out
```

```python
from contextlib import ExitStack

import concourse.bass as bass
from concourse import mybir

F32 = mybir.dt.float32
ALU = mybir.AluOpType
ACT = mybir.ActivationFunctionType
AX_X = mybir.AxisListType.X

P = 128
S = 128
D = 256
KT = D // P
NH = 16
HD = D // NH
NKV = 4
GRP = NH // NKV
KVA = NKV * HD
BLK = 7
CH = BLK * P
HC = CH // 2
PA = 4
LOWEST = -3.0e38
HPT = P // HD
LN_EPS = 1e-5


class Core:

    def __init__(self, nc, ctx):
        self.nc, self.ctx, self.sems = nc, ctx, []
        self.ps = self.psum("banks", [P, 8, 512])
        self.sc = [self.ps[:, 2 * i:2 * i + 2, :] for i in range(2)]
        self.single = [self.ps[:, 4 + i, :] for i in range(4)]

    def sb(self, name, shape, dt=F32):
        return self.ctx.enter_context(self.nc.sbuf_tensor(name, shape, dt))

    def psum(self, name, shape, dt=F32):
        return self.ctx.enter_context(self.nc.psum_tensor(name, shape, dt))

    def sem(self, name):
        self.sems.append(self.nc.alloc_semaphore(name))
        return self.sems[-1]

    def run(self, stage, *args):
        stage(self.nc, self, *args)
        self.nc.clear_and_free_semaphores(self.sems)
        self.nc.all_engine_barrier()
        self.sems = []

    def bank(self, i):
        return self.ps[:, i, :]


class Chain:

    def __init__(self, eng, sem, base=0):
        self.eng, self.sem, self.base, self.n = eng, sem, base, 0

    def __call__(self, ins):
        ins.then_inc(self.sem, 1)
        self.n += 1
        self.eng.wait_ge(self.sem, self.base + self.n)


def consts(nc, c):
    c.ident = c.sb("ident", [P, P])
    c.headmask = c.sb("headmask", [P, HPT])
    c.eps = c.sb("eps", [P, 1])
    c.x = c.sb("x_rows", [S, D])
    c.xn = c.sb("x_normed", [S, D])
    c.xT = c.sb("x_normedT", [P, KT, S])
    c.gate, c.gates = c.sb("gate", [S, 16]), 0
    c.stats = c.sb("ln_stats", [S, 6])
    c.mv = c.sb("ln_mean_var", [S, 2])
    c.std = c.sb("ln_std", [S, 1])
    c.rstd = c.sb("ln_rstd", [S, 1])
    filled, selected, loaded = c.sem("const_filled"), c.sem("const_selected"), c.sem("x_loaded")
    with nc.Block() as block:
        @block.sync
        def _(sp):
            sp.dma_start(c.x[:, :], c.x_dram).then_inc(loaded, 16)
            sp.wait_ge(loaded, 16)

        @block.gpsimd
        def _(pool):
            pool.memset(c.ident[:, :], 0.0).then_inc(filled, 1)
            pool.memset(c.headmask[:, :], 1.0).then_inc(filled, 1)
            pool.memset(c.eps[:, :], LN_EPS).then_inc(filled, 1)
            pool.wait_ge(filled, 3)
            pool.affine_select(out=c.ident[:, :], in_=c.ident[:, :], compare_op=ALU.not_equal, fill=1.0,
                               base=0, pattern=[[-1, P]], channel_multiplier=1).then_inc(selected, 1)
            pool.affine_select(out=c.headmask[:, :], in_=c.headmask[:, :], compare_op=ALU.is_ge, fill=0.0,
                               base=0, pattern=[[-HD, HPT]], channel_multiplier=1).then_inc(selected, 1)
            pool.wait_ge(selected, 2)
            pool.affine_select(out=c.headmask[:, :], in_=c.headmask[:, :], compare_op=ALU.is_ge, fill=0.0,
                               base=HD - 1, pattern=[[HD, HPT]], channel_multiplier=-1).then_inc(selected, 1)
            pool.wait_ge(selected, 3)


class Norm:

    def __init__(self, c, name):
        self.c = c
        self.gate = c.gate[:, c.gates:c.gates + 1]
        c.gates += 1
        self.gated = c.sem(f"{name}_gated")
        self.stats = c.sem(f"{name}_stats")
        self.var = c.sem(f"{name}_var")
        self.std = c.sem(f"{name}_std")
        self.rstd = c.sem(f"{name}_rstd")
        self.out = c.sem(f"{name}_out")
        self.turned = c.sem(f"{name}_turned")
        self.outT = c.sem(f"{name}_outT")

    def vector(self, dve, n, x, out):
        c = self.c
        dve.bn_stats(c.stats[:, :], x).then_inc(self.stats, 1)
        dve.wait_ge(self.stats, n + 1)
        if not (isinstance(n, int) and n == 0):
            dve.wait_ge(self.gated, n)
        dve.memset(self.gate, 0.0).then_inc(self.gated, 1)
        dve.bn_aggr(c.mv[:, :], c.stats[:, :]).then_inc(self.var, 1)
        dve.wait_ge(self.std, n + 1)
        dve.reciprocal(c.rstd[:, :], c.std[:, :]).then_inc(self.rstd, 1)
        dve.wait_ge(self.rstd, n + 1)
        dve.tensor_scalar(out, x, c.mv[:, 0:1], c.rstd[:, 0:1], ALU.subtract, ALU.mult).then_inc(self.out, 1)

    def scalar(self, act, n):
        c = self.c
        act.wait_ge(self.var, n + 1)
        act.activation(c.std[:, :], c.mv[:, 1:2], ACT.Sqrt, bias=c.eps[:, 0:1]).then_inc(self.std, 1)

    def turn(self, pe, n, src, bank):
        pe.wait_ge(self.out, n + 1)
        for k in range(KT):
            mm = pe.transpose(bank[:, k * S:(k + 1) * S], src[:, k * P:(k + 1) * P], self.c.ident[:, :])
        mm.then_inc(self.turned, 1)

    def keep(self, dve, n, bank, dst):
        dve.wait_ge(self.turned, n + 1)
        dve.tensor_copy(dst, bank[:, 0:KT * S].rearrange("p (k s) -> p k s", k=KT)).then_inc(self.outT, 1)


def context_products(nc, c):
    T = c.T
    n_chunks = T // CH
    W = KVA + D
    with ExitStack() as ctx:
        def sb(name, shape):
            return ctx.enter_context(nc.sbuf_tensor(name, shape, F32))

        ctx_tile = [sb(f"ctx_tile{i}", [P, KT, CH]) for i in range(2)]
        wk, wv = sb("wk_both", [P, KT, W]), sb("wv_both", [P, KT, W])
        keys2 = [sb(f"keys2_{i}", [P, KT, CH]) for i in range(2)]
        vals1 = [sb(f"vals1_{i}", [P, NKV, BLK, HD]) for i in range(2)]
        vals2 = [sb(f"vals2_{i}", [P, NH, BLK, HD]) for i in range(2)]
        w_in = c.sem("kv_weights_in")
        ctx_in = [c.sem(f"ctx_in{i}") for i in range(2)]
        stored = [c.sem(f"kv_stored{i}") for i in range(2)]
        k_made = c.sem("k_made")
        k_kept = c.sem("k_kept")
        v_made = c.sem("v_made")
        v_kept = c.sem("v_kept")
        k_units = [(KVA, 0, n) for n in range(2)] + [(P, KVA + m * P, n) for m in range(KT) for n in range(2)]
        KU = len(k_units)
        block = ctx.enter_context(nc.Block())

        @block.sync
        def _(sp):
            sp.dma_start(wk[:, :, 0:KVA], c.wkA).then_inc(w_in, 16)
            sp.dma_start(wk[:, :, KVA:W], c.wkD).then_inc(w_in, 16)
            sp.dma_start(wv[:, :, 0:KVA], c.wvA).then_inc(w_in, 16)
            sp.dma_start(wv[:, :, KVA:W], c.wvD).then_inc(w_in, 16)
            ctx_v = c.ctxT.rearrange("(k p) t -> p k t", p=P)
            for par in range(2):
                sp.dma_start(ctx_tile[par][:, :, :], ctx_v[:, :, par * CH:(par + 1) * CH]).then_inc(ctx_in[par], 16)

            def store(i, par):
                ch = 2 * i + par
                sp.wait_ge(k_kept, KU * (2 * i + par + 1))
                sp.dma_start(c.k2_dram.rearrange("m p t -> p m t")[:, :, bass.ds(ch * CH, CH)], keys2[par][:, :, :]).then_inc(stored[par], 16)
                sp.wait_ge(v_kept, BLK * (2 * i + par + 1))
                sp.dma_start(c.v1_dram.rearrange("h p n d -> p h n d")[:, :, bass.ds(ch * BLK, BLK), :], vals1[par][:, :, :, :]).then_inc(stored[par], 16)
                sp.dma_start(c.v2_dram.rearrange("h p n d -> p h n d")[:, :, bass.ds(ch * BLK, BLK), :], vals2[par][:, :, :, :]).then_inc(stored[par], 16)

            def load(i, par):
                sp.wait_ge(v_made, BLK * (2 * i + par - 1))
                sp.dma_start(ctx_tile[par][:, :, :], ctx_v[:, :, bass.ds((2 * i + par) * CH, CH)]).then_inc(ctx_in[par], 16)

            if n_chunks > 2:
                with sp.Fori(1, n_chunks // 2) as i:
                    for par in range(2):
                        load(i, par)
                        store(i - 1, par)
            for par in range(2):
                store(n_chunks // 2 - 1, par)
            for par in range(2):
                sp.wait_ge(stored[par], 48 * (n_chunks // 2))

        def each_chunk(eng, body):
            for par in range(2):
                body(0, par)
            if n_chunks > 2:
                with eng.Fori(1, n_chunks // 2) as i:
                    for par in range(2):
                        body(i, par)

        @block.tensor
        def _(pe):
            pe.wait_ge(w_in, 64)

            def body(i, par):
                ch, first = 2 * i + par, isinstance(i, int) and i == 0
                pe.wait_ge(ctx_in[par], 16 * (i + 1))
                for u, (m, w0, n) in enumerate(k_units):
                    if not (first and par == 0):
                        pe.wait_ge(k_kept, KU * (ch - 1) + u + 1)
                    for k in range(KT):
                        mm = pe.matmul(c.bank(u)[0:m, 0:HC], wk[:, k, w0:w0 + m], ctx_tile[par][:, k, n * HC:(n + 1) * HC],
                                       start=(k == 0), stop=(k == KT - 1))
                    mm.then_inc(k_made, 1)
                for b in range(BLK):
                    u = BLK * par + b
                    if not (first and u < 2):
                        pe.wait_ge(v_kept, BLK * ch + b - 1)
                    for k in range(KT):
                        mm = pe.matmul(c.bank(6 + u % 2)[:, 0:W], ctx_tile[par][:, k, b * P:(b + 1) * P], wv[:, k, :],
                                       start=(k == 0), stop=(k == KT - 1))
                    mm.then_inc(v_made, 1)
            each_chunk(pe, body)

        @block.scalar
        def _(act):
            def body(i, par):
                ch = 2 * i + par
                if not (isinstance(i, int) and i == 0):
                    act.wait_ge(stored[par], 48 * i)
                for u, (m, w0, n) in enumerate(k_units):
                    act.wait_ge(k_made, KU * ch + u + 1)
                    dst = (c.keys[0:KVA, bass.ds(ch * CH + n * HC, HC)] if w0 == 0
                           else keys2[par][:, (w0 - KVA) // P, n * HC:(n + 1) * HC])
                    act.copy(dst, c.bank(u)[0:m, 0:HC]).then_inc(k_kept, 1)
            each_chunk(act, body)

        @block.vector
        def _(dve):
            def body(i, par):
                ch = 2 * i + par
                if not (isinstance(i, int) and i == 0):
                    dve.wait_ge(stored[par], 48 * i)
                for b in range(BLK):
                    bank = c.bank(6 + (BLK * par + b) % 2)
                    dve.wait_ge(v_made, BLK * ch + b + 1)
                    dve.tensor_copy(vals1[par][:, :, b, :], bank[:, 0:KVA].rearrange("p (h d) -> p h d", d=HD))
                    dve.tensor_copy(vals2[par][:, :, b, :], bank[:, KVA:W].rearrange("p (h d) -> p h d", d=HD)).then_inc(v_kept, 1)
            each_chunk(dve, body)


def queries(nc, c, name, w_dram, rows, groups):
    tiles = D // rows
    with ExitStack() as ctx:
        wq = ctx.enter_context(nc.sbuf_tensor(f"{name}_wq", [P, KT, D], F32))
        w_in = c.sem(f"{name}_wq_in")
        made = c.sem(f"{name}_q_made")
        norm = Norm(c, f"{name}_norm")
        block = ctx.enter_context(nc.Block())

        @block.sync
        def _(sp):
            sp.dma_start(wq[:, :, :], w_dram).then_inc(w_in, 16)
            sp.wait_ge(w_in, 16)

        @block.scalar
        def _(act):
            norm.scalar(act, 0)

        @block.tensor
        def _(pe):
            norm.turn(pe, 0, c.xn, c.bank(4))
            pe.wait_ge(norm.outT, 1)
            pe.wait_ge(w_in, 16)
            for t in range(tiles):
                for k in range(KT):
                    mm = pe.matmul(c.bank(t)[0:rows, 0:S], wq[:, k, t * rows:(t + 1) * rows], c.xT[:, k, :],
                                   start=(k == 0), stop=(k == KT - 1))
                mm.then_inc(made, 1)

        @block.vector
        def _(dve):
            norm.vector(dve, 0, c.x[:, :], c.xn[:, :])
            norm.keep(dve, 0, c.bank(4), c.xT[:, :, :])
            for t in range(tiles):
                dve.wait_ge(made, t + 1)
                for g in range(rows // HD):
                    h = GRP * g + t if groups else t * HPT + g
                    dve.tensor_scalar(c.qm[0:rows, h, :], c.bank(t)[0:rows, 0:S], c.headmask[0:rows, g:g + 1],
                                      float(HD) ** -0.5, ALU.mult, ALU.mult)


def attention(nc, c, name, rows, v_dram, heads_per_v, bias, keys_dram):
    T = c.T
    NC = T // CH
    NB = T // P
    HALF = NC // 2
    HB = HALF * CH
    with ExitStack() as ctx:
        def sb(nm, shape):
            return ctx.enter_context(nc.sbuf_tensor(f"{name}_{nm}", shape, F32))

        def sem(nm):
            return c.sem(f"{name}_{nm}")

        q_head = [sb(f"q_head{i}", [P, S]) for i in range(2)]
        v_head = [sb(f"v_head{i}", [P, NB, HD]) for i in range(2)]
        s = [c.scores[i] for i in range(2)]
        probT = [sb(f"probT{i}", [P, BLK, S]) for i in range(2)]
        chunk_max = [sb(f"chunk_max{i}", [S, NC]) for i in range(2)]
        neg_max = [sb(f"neg_max{i}", [S, 1]) for i in range(2)]
        chunk_sum = [sb(f"chunk_sum{i}", [S, NC]) for i in range(2)]
        total = sb("total", [S, 1])
        gate = sb("gate", [S, 1])
        inv_total = sb("inv_total", [S, 1])
        outT = [sb(f"outT{i}", [HD, S]) for i in range(2)]
        q_staged = sem("q_staged")
        v_in = [sem(f"v_in{i}") for i in range(2)]
        bias_in = [[sem(f"bias_in{i}{j}") for j in range(2)] for i in range(2)]
        keys_in = [sem(f"keys_in{j}") for j in range(2)]
        made = sem("scores_made")
        kept = sem("scores_kept")
        max_ready = sem("max_ready")
        exp_ready = sem("exp_ready")
        turned = [sem("turned_a"), sem("turned_b")]
        copied = [sem("copied_a"), sem("copied_b")]
        pv_done = sem("pv_done")
        outT_kept = sem("outT_kept")
        out_ready = sem("out_ready")
        head_done = sem("head_done")
        step = sem("small_step")
        gated = sem("gated")
        block = ctx.enter_context(nc.Block())
        units = [(0, PA), (PA, BLK)]
        last = NH // 2 - 1

        def pairs(eng, body):
            body(0)
            if keys_dram is not None:
                with eng.Fori(1, last // 2) as it:
                    body(it)
                body(last // 2)
                with eng.Fori(last // 2 + 1, last) as it:
                    body(it)
            else:
                with eng.Fori(1, last) as it:
                    body(it)
            body(last)

        @block.sync
        def _(sp):
            def load_v(h, par):
                src = v_dram[bass.ds(h // heads_per_v, 1), :, :, :] if not isinstance(h, int) else v_dram[h // heads_per_v:h // heads_per_v + 1, :, :, :]
                sp.dma_start(v_head[par][:, :, :], src.rearrange("o p n d -> (o p) n d")).then_inc(v_in[par], 16)

            def load_bias(h, par, j):
                src = bias[bass.ds(h, 1), :, j * HB:(j + 1) * HB] if not isinstance(h, int) else bias[h:h + 1, :, j * HB:(j + 1) * HB]
                sp.dma_start(s[par][:, j * HB:(j + 1) * HB], src.rearrange("o q t -> (o q) t")).then_inc(bias_in[par][j], 16)

            def load_keys(m, j):
                sp.dma_start(c.keys[:, j * HB:(j + 1) * HB], keys_dram[m, :, j * HB:(j + 1) * HB]).then_inc(keys_in[j], 16)

            if keys_dram is not None:
                for j in range(2):
                    load_keys(0, j)
            for par in range(2):
                if bias is not None:
                    for j in range(2):
                        load_bias(par, par, j)
                load_v(par, par)

            def body(it):
                for par in range(2):
                    h = 2 * it + par
                    if keys_dram is not None and isinstance(it, int) and h == HPT - 2:
                        for j in range(2):
                            sp.wait_ge(made, (h + 1) * NC + HALF * (j + 1))
                            load_keys(1, j)
                    if isinstance(it, int) and it == last:
                        continue
                    for j in range(2):
                        if bias is not None:
                            sp.wait_ge(turned[1], h * NC + HALF * (j + 1))
                            load_bias(h + 2, par, j)
                    sp.wait_ge(pv_done, (h + 1) * NC)
                    load_v(h + 2, par)
            pairs(sp, body)

        @block.gpsimd
        def _(pool):
            def stage(h, par):
                src = c.qm[0:rows, bass.ds(h, 1), :].rearrange("p o s -> p (o s)") if not isinstance(h, int) else c.qm[0:rows, h, :]
                pool.tensor_copy(q_head[par][0:rows, :], src).then_inc(q_staged, 1)

            for par in range(2):
                stage(par, par)

            def body(it):
                if isinstance(it, int) and it == last:
                    return
                for par in range(2):
                    h = 2 * it + par
                    pool.wait_ge(made, (h + 1) * NC)
                    stage(h + 2, par)
            pairs(pool, body)

        @block.tensor
        def _(pe):
            def scores(h, par, ch):
                n = h * NC + ch
                if ch == 0:
                    pe.wait_ge(q_staged, h + 1)
                if keys_dram is not None and ch % HALF == 0 and isinstance(h, int) and h in (0, HPT):
                    pe.wait_ge(keys_in[ch // HALF], 16 * (h // HPT + 1))
                if not (isinstance(h, int) and n < 2):
                    pe.wait_ge(kept, n - 1)
                for k in range(2):
                    mm = pe.matmul(c.sc[ch % 2][:, k, 0:HC], q_head[par][0:rows, :],
                                   c.keys[0:rows, ch * CH + k * HC:ch * CH + (k + 1) * HC], start=True, stop=True)
                mm.then_inc(made, 1)

            def turn(h, par, ch):
                n = h * NC + ch
                pe.wait_ge(exp_ready, n + 1)
                for u, (b0, b1) in enumerate(units):
                    if not (isinstance(h, int) and n == 0):
                        pe.wait_ge(copied[u], n)
                    for b in range(b0, b1):
                        col = ch * CH + b * P
                        mm = pe.transpose(c.single[u][:, (b - b0) * S:(b - b0 + 1) * S], s[par][:, col:col + P], c.ident[:, :])
                    mm.then_inc(turned[u], 1)

            def weigh(h, par, ch, it):
                if ch == 0:
                    pe.wait_ge(v_in[par], 16 * (it + 1))
                    if not (isinstance(h, int) and h < 2):
                        pe.wait_ge(head_done, h - 1)
                for u, (b0, b1) in enumerate(units):
                    pe.wait_ge(copied[u], h * NC + ch + 1)
                    for b in range(b0, b1):
                        mm = pe.matmul(c.single[2 + par][0:HD, 0:S], v_head[par][:, ch * BLK + b, :], probT[ch % 2][:, b, :],
                                       start=(ch == 0 and b == 0), stop=(ch == NC - 1 and b == BLK - 1))
                mm.then_inc(pv_done, 1)

            for ch in range(NC):
                scores(0, 0, ch)

            def body(it):
                for par in range(2):
                    h = 2 * it + par
                    for ch in range(NC):
                        if not (isinstance(h, int) and h == NH - 1):
                            scores(h + 1, 1 - par, ch)
                        turn(h, par, ch)
                        if ch >= 1:
                            weigh(h, par, ch - 1, it)
                    weigh(h, par, NC - 1, it)
                    pe.wait_ge(outT_kept, h + 1)
                    pe.matmul(c.single[2 + par][:, 2 * P:2 * P + HD], outT[par][:, :], c.ident[0:HD, 0:HD],
                              start=True, stop=True).then_inc(out_ready, 1)
            pairs(pe, body)

        @block.scalar
        def _(act):
            def exp(h, par, ch):
                if ch == 0:
                    act.wait_ge(max_ready, h + 1)
                    if not (isinstance(h, int) and h < 2):
                        act.wait_ge(head_done, h - 1)
                part = s[par][:, ch * CH:(ch + 1) * CH]
                act.activation(part, part, ACT.Exp, bias=neg_max[par][:, 0:1],
                               accum_out=chunk_sum[par][:, ch:ch + 1]).then_inc(exp_ready, 1)

            def body(it):
                for par in range(2):
                    h = 2 * it + par
                    exp(h, par, 0)
                    exp(h, par, 1)
                    for ch in range(NC):
                        n = h * NC + ch
                        act.wait_ge(turned[1], n + 1)
                        if not (isinstance(h, int) and n < 2):
                            act.wait_ge(pv_done, n - 1)
                        act.copy(probT[ch % 2][:, PA:BLK, :], c.single[1][:, 0:(BLK - PA) * S].rearrange("p (b s) -> p b s", s=S)).then_inc(copied[1], 1)
                        if ch + 2 < NC:
                            exp(h, par, ch + 2)
                    act.wait_ge(pv_done, (h + 1) * NC)
                    act.copy(outT[par][:, :], c.single[2 + par][0:HD, 0:S]).then_inc(outT_kept, 1)
            pairs(act, body)

        @block.vector
        def _(dve):
            def keep(h, par, ch, it_in):
                n = h * NC + ch
                dve.wait_ge(made, n + 1)
                src = c.sc[ch % 2][:, :, 0:HC]
                dst = s[par][:, ch * CH:(ch + 1) * CH].rearrange("p (k n) -> p k n", k=2)
                if bias is None:
                    if not (isinstance(h, int) and h < 2):
                        dve.wait_ge(turned[1], (h - 2) * NC + ch + 1)
                    dve.tensor_scalar(dst, src, 1.0, LOWEST, ALU.mult, ALU.max,
                                      accum_out=chunk_max[par][:, ch:ch + 1]).then_inc(kept, 1)
                else:
                    if ch % HALF == 0:
                        dve.wait_ge(bias_in[par][ch // HALF], 16 * (it_in + 1))
                    if not (isinstance(h, int) and n == 0):
                        dve.wait_ge(gated, n)
                    dve.memset(gate[:, :], 0.0).then_inc(gated, 1)
                    dve.tensor_tensor_reduce(dst, src, dst, 1.0, LOWEST, ALU.add, ALU.max,
                                             chunk_max[par][:, ch:ch + 1]).then_inc(kept, 1)

            def head_max(h, par):
                dve.wait_ge(kept, (h + 1) * NC)
                if not (isinstance(h, int) and h < 2):
                    dve.wait_ge(exp_ready, (h - 1) * NC)
                dve.tensor_reduce(neg_max[par][:, :], chunk_max[par][:, :], AX_X, ALU.max, negate=True).then_inc(max_ready, 1)

            for ch in range(NC):
                keep(0, 0, ch, 0)
            head_max(0, 0)

            def body(it):
                for par in range(2):
                    h = 2 * it + par
                    for ch in range(NC):
                        n = h * NC + ch
                        if not (isinstance(h, int) and h == NH - 1):
                            keep(h + 1, 1 - par, ch, it + par)
                        dve.wait_ge(turned[0], n + 1)
                        if not (isinstance(h, int) and n < 2):
                            dve.wait_ge(pv_done, n - 1)
                        dve.tensor_copy(probT[ch % 2][:, 0:PA, :], c.single[0][:, :].rearrange("p (b s) -> p b s", s=S)).then_inc(copied[0], 1)
                    if not (isinstance(h, int) and h == NH - 1):
                        head_max(h + 1, 1 - par)
                    dve.wait_ge(exp_ready, (h + 1) * NC)
                    dve.reduce_sum(total[:, :], chunk_sum[par][:, :], AX_X).then_inc(step, 1)
                    dve.wait_ge(step, 2 * h + 1)
                    dve.reciprocal(inv_total[:, :], total[:, :]).then_inc(step, 1)
                    dve.wait_ge(step, 2 * h + 2)
                    dve.wait_ge(out_ready, h + 1)
                    dst = c.attn[:, bass.ds(h * HD, HD)]
                    dve.tensor_scalar(dst, c.single[2 + par][:, 2 * P:2 * P + HD], inv_total[:, 0:1], None, ALU.mult).then_inc(head_done, 1)
            pairs(dve, body)


def project_out(nc, c, name, w_dram, base, dst):
    with ExitStack() as ctx:
        w = ctx.enter_context(nc.sbuf_tensor(f"{name}_wo", [P, KT, D], F32))
        w_in = c.sem(f"{name}_wo_in")
        turned = c.sem(f"{name}_attn_turned")
        attnT = c.sem(f"{name}_attnT_kept")
        made = c.sem(f"{name}_out_made")
        added = c.sem(f"{name}_x_added")
        block = ctx.enter_context(nc.Block())

        @block.sync
        def _(sp):
            sp.dma_start(w[:, :, :], w_dram).then_inc(w_in, 16)

        @block.tensor
        def _(pe):
            for k in range(KT):
                mm = pe.transpose(c.bank(4)[:, k * S:(k + 1) * S], c.attn[:, k * P:(k + 1) * P], c.ident[:, :])
            mm.then_inc(turned, 1)
            pe.wait_ge(attnT, 1)
            pe.wait_ge(w_in, 16)
            for k in range(KT):
                mm = pe.matmul(c.bank(5)[:, 0:D], c.xT[:, k, :], w[:, k, :], start=(k == 0), stop=(k == KT - 1))
            mm.then_inc(made, 1)

        @block.vector
        def _(dve):
            dve.wait_ge(turned, 1)
            dve.tensor_copy(c.xT[:, :, :], c.bank(4)[:, 0:KT * S].rearrange("p (k s) -> p k s", k=KT)).then_inc(attnT, 1)
            dve.wait_ge(made, 1)
            dve.tensor_tensor(dst[:, :], base[:, :], c.bank(5)[:, 0:D], ALU.add).then_inc(added, 1)
            dve.wait_ge(added, 1)


def relative_attention(nc, c):
    R = 5
    BAND = 3
    with ExitStack() as ctx:
        def sb(nm, shape):
            return ctx.enter_context(nc.sbuf_tensor(f"rel_{nm}", shape, F32))

        def sem(nm):
            return c.sem(f"rel_{nm}")

        w = {n: sb(f"w{n}", [P, KT, D]) for n in "qkvo"}
        bcol = {n: sb(f"bcol_{n}", [P, KT]) for n in "qk"}
        brow = {n: sb(f"brow_{n}", [S, D]) for n in "vo"}
        relk = sb("relk", [P, R])
        relk_heads = sb("relk_heads", [P, HPT, R])
        relv = sb("relv", [S, R, HD])
        band = sb("band", [S, BAND, S])
        qT, kT, v = sb("qT", [P, KT, S]), sb("kT", [P, KT, S]), sb("v", [S, D])
        qm = sb("qm", [P, NH, S])
        r = sb("r", [S, NH, R])
        sc, t = sb("scores", [S, NH, S]), sb("t", [S, NH, S])
        pT = sb("pT", [S, NH, S])
        mx, total, wgt = sb("mx", [S, NH]), sb("total", [S, NH]), sb("wgt", [S, BAND, NH])
        o, ot = sb("o", [S, NH, HD]), sb("ot", [S, NH, HD])
        norm = Norm(c, "rel_norm")
        w_in, band_step, band_made = sem("w_in"), sem("band_step"), sem("band_made")
        proj_made, q_ready, scores_made, r_made = sem("proj_made"), sem("q_ready"), sem("scores_made"), sem("r_made")
        rel_added, masked, max_ready, exp_ready = sem("rel_added"), sem("masked"), sem("max_ready"), sem("exp_ready")
        p_turned, pT_ready, pv_made, o_ready = sem("p_turned"), sem("pT_ready"), sem("pv_made"), sem("o_ready")
        o_turned, oT_ready, out_made, steps = sem("o_turned"), sem("oT_ready"), sem("out_made"), sem("steps")
        LOADS = 4 + 2 + 2 + HPT + 1
        block = ctx.enter_context(nc.Block())

        @block.sync
        def _(sp):
            for n in "qkvo":
                sp.dma_start(w[n][:, :, :], c.rel[f"W_{n}"]).then_inc(w_in, 16)
            for n in "qk":
                sp.dma_start(bcol[n][:, :], c.rel[f"b_{n}"]).then_inc(w_in, 16)
            for n in "vo":
                sp.dma_start(brow[n][:, :], c.rel[f"b_{n}"].rearrange("(o d) -> o d", o=1).broadcast_to((S, D))).then_inc(w_in, 16)
            for h in range(HPT):
                sp.dma_start(relk[h * HD:(h + 1) * HD, :], c.rel["rel_kT"]).then_inc(w_in, 16)
            sp.dma_start(relv[:, :, :].rearrange("p r d -> p (r d)"),
                         c.rel["rel_v_table"].rearrange("(o r) d -> o (r d)", o=1).broadcast_to((S, R * HD))).then_inc(w_in, 16)
            sp.wait_ge(w_in, 16 * LOADS)

        @block.gpsimd
        def _(pool):
            pool.memset(band[:, 0, :], 1.0).then_inc(band_step, 1)
            pool.memset(band[:, 1, :], 0.0).then_inc(band_step, 1)
            pool.tensor_copy(band[:, 2, :], c.ident[:, :]).then_inc(band_step, 1)
            pool.wait_ge(band_step, 3)
            pool.affine_select(out=band[:, 0, :], in_=band[:, 0, :], compare_op=ALU.is_ge, fill=0.0,
                               base=-2, pattern=[[-1, S]], channel_multiplier=1).then_inc(band_made, 1)
            pool.affine_select(out=band[:, 1, :], in_=band[:, 1, :], compare_op=ALU.not_equal, fill=1.0,
                               base=-1, pattern=[[-1, S]], channel_multiplier=1).then_inc(band_made, 1)
            pool.wait_ge(rel_added, 1)
            pool.affine_select(out=sc[:, :, :], in_=sc[:, :, :], compare_op=ALU.is_ge, fill=-1.0e9 * HD ** 0.5,
                               base=0, pattern=[[0, NH], [-1, S]], channel_multiplier=1).then_inc(masked, 1)

        @block.scalar
        def _(act):
            norm.scalar(act, 0)
            act.wait_ge(max_ready, 1)
            for h in range(NH):
                act.activation(sc[:, h, :], sc[:, h, :], ACT.Exp, bias=mx[:, h:h + 1], scale=HD ** -0.5,
                               accum_out=total[:, h:h + 1]).then_inc(exp_ready, 1)

        @block.tensor
        def _(pe):
            norm.turn(pe, 0, c.xn, c.bank(4))
            pe.wait_ge(norm.outT, 1)
            pe.wait_ge(w_in, 16 * LOADS)
            for i, n in enumerate("qk"):
                for m in range(KT):
                    for k in range(KT):
                        mm = pe.matmul(c.bank(i)[:, m * S:(m + 1) * S], w[n][:, k, m * P:(m + 1) * P], c.xT[:, k, :],
                                       start=(k == 0), stop=(k == KT - 1))
                mm.then_inc(proj_made, 1)
            for k in range(KT):
                mm = pe.matmul(c.bank(2)[:, 0:D], c.xT[:, k, :], w["v"][:, k, :], start=(k == 0), stop=(k == KT - 1))
            mm.then_inc(proj_made, 1)
            pe.wait_ge(q_ready, 1)
            for m in range(KT):
                mm = pe.matmul(c.bank(5)[:, m * HPT * R:(m + 1) * HPT * R], qT[:, m, :],
                               relk_heads[:, :, :].rearrange("p h r -> p (h r)"), start=True, stop=True)
            mm.then_inc(r_made, 1)
            pe.wait_ge(q_ready, 2)
            for h in range(NH):
                mm = pe.matmul(c.bank(h // 4)[:, (h % 4) * S:(h % 4 + 1) * S], qm[:, h, :], kT[:, h // HPT, :], start=True, stop=True)
            mm.then_inc(scores_made, 1)
            for h in range(NH):
                pe.wait_ge(exp_ready, h + 1)
                mm = pe.transpose(c.bank(h // 4)[:, (h % 4) * S:(h % 4 + 1) * S], sc[:, h, :], c.ident[:, :])
            mm.then_inc(p_turned, 1)
            pe.wait_ge(pT_ready, 1)
            for h in range(NH):
                mm = pe.matmul(c.bank(6)[:, h * HD:(h + 1) * HD], pT[:, h, :], v[:, h * HD:(h + 1) * HD], start=True, stop=True)
            mm.then_inc(pv_made, 1)
            pe.wait_ge(o_ready, 1)
            for k in range(KT):
                mm = pe.transpose(c.bank(4)[:, k * S:(k + 1) * S], o[:, k * HPT:(k + 1) * HPT, :].rearrange("p h d -> p (h d)"), c.ident[:, :])
            mm.then_inc(o_turned, 1)
            pe.wait_ge(oT_ready, 1)
            for k in range(KT):
                mm = pe.matmul(c.bank(7)[:, 0:D], c.xT[:, k, :], w["o"][:, k, :], start=(k == 0), stop=(k == KT - 1))
            mm.then_inc(out_made, 1)

        @block.vector
        def _(dve):
            chain = Chain(dve, steps)
            dve.wait_ge(w_in, 16 * LOADS)
            chain(dve.tensor_tensor(relk_heads[:, :, :], relk[:, :].unsqueeze(1).broadcast_to((P, HPT, R)),
                                    c.headmask[:, :].unsqueeze(2).broadcast_to((P, HPT, R)), ALU.mult))
            norm.vector(dve, 0, c.x[:, :], c.xn[:, :])
            norm.keep(dve, 0, c.bank(4), c.xT[:, :, :])
            dve.wait_ge(proj_made, 1)
            for m in range(KT):
                chain(dve.tensor_scalar(qT[:, m, :], c.bank(0)[:, m * S:(m + 1) * S], bcol["q"][:, m:m + 1], None, ALU.add))
            dve.sem_inc(q_ready, 1)
            dve.wait_ge(proj_made, 2)
            for m in range(KT):
                chain(dve.tensor_scalar(kT[:, m, :], c.bank(1)[:, m * S:(m + 1) * S], bcol["k"][:, m:m + 1], None, ALU.add))
            for h in range(NH):
                ins = dve.tensor_scalar(qm[:, h, :], qT[:, h // HPT, :], c.headmask[:, h % HPT:h % HPT + 1], None, ALU.mult)
            chain(ins)
            dve.wait_ge(proj_made, 3)
            chain(dve.tensor_tensor(v[:, :], c.bank(2)[:, 0:D], brow["v"][:, :], ALU.add))
            dve.sem_inc(q_ready, 1)
            dve.wait_ge(r_made, 1)
            chain(dve.tensor_copy(r[:, :, :].rearrange("p h r -> p (h r)"), c.bank(5)[:, 0:NH * R]))
            dve.wait_ge(band_made, 2)
            dve.wait_ge(scores_made, 1)
            for j in range(BAND):
                chain(dve.tensor_tensor(t[:, :, :], band[:, j, :].unsqueeze(1).broadcast_to((S, NH, S)),
                                        r[:, :, j:j + 1].broadcast_to((S, NH, S)), ALU.mult))
                acc = c.ps[:, 0:4, :].rearrange("p b (h s) -> p (b h) s", s=S) if j == 0 else sc[:, :, :]
                ins = dve.tensor_tensor(sc[:, :, :], acc, t[:, :, :], ALU.add)
                if j < BAND - 1:
                    chain(ins)
            ins.then_inc(rel_added, 1)
            dve.wait_ge(masked, 1)
            chain(dve.tensor_reduce(mx[:, :], sc[:, :, :], AX_X, ALU.max, negate=True))
            dve.tensor_scalar(mx[:, :], mx[:, :], HD ** -0.5, None, ALU.mult).then_inc(max_ready, 1)
            dve.wait_ge(p_turned, 1)
            dve.tensor_copy(pT[:, :, :], c.ps[:, 0:4, :].rearrange("p b (h s) -> p (b h) s", s=S)).then_inc(pT_ready, 1)
            dve.wait_ge(exp_ready, NH)
            for j in range(BAND):
                chain(dve.tensor_tensor(t[:, :, :], sc[:, :, :], band[:, j, :].unsqueeze(1).broadcast_to((S, NH, S)), ALU.mult))
                chain(dve.reduce_sum(wgt[:, j, :], t[:, :, :], AX_X))
            dve.wait_ge(pv_made, 1)
            for j in range(BAND):
                chain(dve.tensor_tensor(ot[:, :, :], wgt[:, j, :].unsqueeze(2).broadcast_to((S, NH, HD)),
                                        relv[:, j, :].unsqueeze(1).broadcast_to((S, NH, HD)), ALU.mult))
                acc = c.bank(6)[:, 0:D].rearrange("p (h d) -> p h d", d=HD) if j == 0 else o[:, :, :]
                chain(dve.tensor_tensor(o[:, :, :], acc, ot[:, :, :], ALU.add))
            chain(dve.reciprocal(total[:, :], total[:, :]))
            dve.tensor_tensor(o[:, :, :], o[:, :, :], total[:, :].unsqueeze(2).broadcast_to((S, NH, HD)), ALU.mult).then_inc(o_ready, 1)
            chain(dve.tensor_tensor(c.x[:, :], c.x[:, :], brow["o"][:, :], ALU.add))
            dve.wait_ge(o_turned, 1)
            dve.tensor_copy(c.xT[:, :, :], c.bank(4)[:, 0:KT * S].rearrange("p (k s) -> p k s", k=KT)).then_inc(oT_ready, 1)
            dve.wait_ge(out_made, 1)
            chain(dve.tensor_tensor(c.x[:, :], c.x[:, :], c.bank(7)[:, 0:D], ALU.add))


def tiled(w):
    return w.rearrange("(k p) n -> p k n", p=P)


def store_x(nc, c, out):
    stored = c.sem("x_stored")
    with nc.Block() as block:
        @block.sync
        def _(sp):
            sp.dma_start(out.rearrange("o s d -> (o s) d"), c.x[:, :]).then_inc(stored, 16)
            sp.wait_ge(stored, 16)


LH, LD = 16, 64
INNER = LH * LD
WINDOW = 64
QK_SCALE = 8.0
DEPTH = 6
FF = int(D * 4 * 2 / 3)
FT = -(-FF // P)
FLAST = FF - (FT - 1) * P
MASKED = -1.0e30


def rotary_tables():
    import numpy as np
    f = np.float32
    half = np.arange(0, LD, 2, dtype=f)
    inv_freq = (f(1.0) / f(10000.0) ** (half / f(LD))).astype(f)
    t = np.arange(S, dtype=f)
    freqs = np.concatenate([t[:, None] * inv_freq[None, :]] * 2, -1)
    base = (half + f(0.4 * LD)) / f(1.4 * LD)
    scale = base[None, :] ** ((t - S // 2) / f(WINDOW // 2))[:, None]
    scale = np.concatenate([scale, scale], -1)
    sign = np.where(np.arange(LD) < LD // 2, f(-1), f(1))
    cos, sin = np.cos(freqs), np.sin(freqs) * sign
    return np.stack([cos * scale, sin * scale, cos / scale, sin / scale], 1).astype(f)


def local_transformer(nc, c):
    with ExitStack() as ctx:
        def sb(nm, shape):
            return ctx.enter_context(nc.sbuf_tensor(f"loc_{nm}", shape, F32))

        def sem(nm):
            return c.sem(f"loc_{nm}")

        wqkv, wo = sb("wqkv", [P, KT, 3 * INNER]), sb("wo", [P, INNER // P, D])
        w1, w2 = sb("w1", [P, KT, 2 * FF]), sb("w2", [P, FT, D])
        cols_all, rows_all = sb("cols_all", [P, DEPTH, 2 * KT + 2 * FT]), sb("rows_all", [S, DEPTH, 2 * LD + D])
        cols, rows = sb("cols", [P, 2 * KT + 2 * FT]), sb("rows", [S, 2 * LD + D])
        rot_all, rot = sb("rot_all", [S, 4, LD]), sb("rot", [S, 4, LD])
        shift, mask = sb("shift", [S, S]), sb("mask", [S, S])
        y, shifted = sb("y", [S, D]), sb("shifted", [S, D])
        tT, hT = sb("tT", [P, KT, S]), sb("hT", [P, FT, S])
        v, sq = sb("v", [S, INNER]), sb("sq", [S, 2 * INNER])
        norms = sb("norms", [S, 2 * LH])
        qk = [sb(f"qk{i}", [S, LH, LD]) for i in range(2)]
        qa, qb = sb("qa", [S, LH, LD]), sb("qb", [S, LH, LD])
        qkT = [sb(f"qkT{i}", [P, LH // 2, S]) for i in range(2)]
        sc, pT = sb("sc", [S, LH, S]), sb("pT", [S, LH, S])
        mx, total, inv = sb("mx", [S, LH]), sb("total", [S, LH]), sb("inv", [S, LH // 2, 2])
        o, oT = sb("o", [S, LH, LD]), sb("oT", [P, INNER // P, S])
        gate = sb("gate", [P, FT, S])

        norm0, norm = Norm(c, "loc_in"), Norm(c, "loc_norm")
        small_in, made_mask, mask_step = sem("small_in"), sem("mask_made"), sem("mask_step")
        w_in = {n: sem(f"{n}_in") for n in ("wqkv", "wo", "w1", "w2")}
        y_ready, y_turned, tT_ready = sem("y_ready"), sem("y_turned"), sem("tT_ready")
        qkv_made, squared, normed = sem("qkv_made"), sem("squared"), sem("sums_ready")
        rooted, v_kept = sem("norms_rooted"), sem("v_kept")
        rotated, qk_turned, qkT_ready = sem("qk_rotated"), sem("qk_turned"), sem("qkT_ready")
        rot_ready, rot_step = sem("rot_ready"), sem("rot_step")
        scores_made, max_ready, exp_ready = sem("scores_made"), sem("max_ready"), sem("exp_ready")
        p_turned, pT_ready, pv_made, o_ready = sem("p_turned"), sem("pT_ready"), sem("pv_made"), sem("o_ready")
        o_turned, oT_ready, wo_made, mid_ready = sem("o_turned"), sem("oT_ready"), sem("wo_made"), sem("mid_ready")
        shift_made, h_made, gelu_ready, hT_ready, w2_made = sem("shift_made"), sem("h_made"), sem("gelu_ready"), sem("hT_ready"), sem("w2_made")
        steps, layer_done, cols_ready = sem("steps"), sem("layer_done"), sem("cols_ready")
        block = ctx.enter_context(nc.Block())
        QO, KO = 0, LD
        B2 = 2 * LD

        def h_tile(u, m):
            t = u % FT
            return c.bank(((3, 4), (5, 7))[u // FT][t // 4])[0:m, (t % 4) * S:(t % 4 + 1) * S]

        def h_signals(u):
            return 2 * (u // FT) + (u % FT) // 4 + 1

        def tile_rows(t):
            return P if t % FT < FT - 1 else FLAST

        @block.sync
        def _(sp):
            sp.dma_start(cols_all[:, :, :], c.loc["cols"]).then_inc(small_in, 16)
            sp.dma_start(rows_all[:, :, :].rearrange("s l n -> s (l n)"),
                         c.loc["rows"].rearrange("(o l) n -> o (l n)", o=1).broadcast_to((S, DEPTH * (2 * LD + D)))).then_inc(small_in, 16)
            sp.dma_start(rot_all[:, :, :], c.loc["rotary"]).then_inc(small_in, 16)

            def load_w(i, name, dst, src, free_sem, free_at):
                if not (isinstance(i, int) and i == 0):
                    sp.wait_ge(free_sem, free_at)
                sp.dma_start(dst, src).then_inc(w_in[name], 16)

            def body(i):
                def layer(w):
                    return w[bass.ds(i, 1)].rearrange("o r n -> (o r) n")
                load_w(i, "wqkv", wqkv[:, :, :], tiled(layer(c.loc["Wqkv"])), qkv_made, 6 * i)
                load_w(i, "wo", wo[:, :, :], tiled(layer(c.loc["Wo"])), wo_made, i)
                load_w(i, "w1", w1[:, :, :], tiled(layer(c.loc["W1"])), h_made, 4 * i)
                src = layer(c.loc["W2"])
                load_w(i, "w2", w2[:, 0:FT - 1, :], tiled(src[0:(FT - 1) * P, :]), w2_made, i)
                sp.dma_start(w2[0:FLAST, FT - 1, :], src[(FT - 1) * P:FF, :]).then_inc(w_in["w2"], 16)
            body(0)
            with sp.Fori(1, DEPTH) as i:
                body(i)
            sp.wait_ge(w_in["w2"], 32 * DEPTH)

        @block.gpsimd
        def _(pool):
            pool.memset(shift[:, :], 0.0).then_inc(mask_step, 1)
            pool.memset(mask[:, :], 0.0).then_inc(mask_step, 1)
            pool.wait_ge(mask_step, 2)
            pool.affine_select(out=shift[:, :], in_=shift[:, :], compare_op=ALU.not_equal, fill=1.0,
                               base=-1, pattern=[[1, S]], channel_multiplier=-1).then_inc(made_mask, 1)
            pool.affine_select(out=mask[:, :], in_=mask[:, :], compare_op=ALU.is_ge, fill=MASKED,
                               base=0, pattern=[[-1, S]], channel_multiplier=1).then_inc(made_mask, 1)
            pool.wait_ge(made_mask, 2)
            pool.affine_select(out=mask[:, :], in_=mask[:, :], compare_op=ALU.is_ge, fill=MASKED,
                               base=WINDOW, pattern=[[1, S]], channel_multiplier=-1).then_inc(made_mask, 1)
            pool.wait_ge(small_in, 48)

            def body(i):
                if not (isinstance(i, int) and i == 0):
                    pool.wait_ge(layer_done, i)
                pool.tensor_copy(cols[:, :], cols_all[:, bass.ds(i, 1), :].rearrange("p o n -> p (o n)")).then_inc(cols_ready, 1)
                pool.tensor_copy(rows[:, :], rows_all[:, bass.ds(i, 1), :].rearrange("p o n -> p (o n)")).then_inc(cols_ready, 1)
                pool.wait_ge(cols_ready, 2 * i + 2)
                H = LD // 2
                for j, off in enumerate((QO, KO)):
                    pool.tensor_tensor(rot[:, 2 * j, :], rot_all[:, 2 * j, :], rows[:, off:off + LD], ALU.mult).then_inc(rot_ready, 1)
                    pool.tensor_tensor(rot[:, 2 * j + 1, 0:H], rot_all[:, 2 * j + 1, 0:H], rows[:, off + H:off + LD], ALU.mult).then_inc(rot_ready, 1)
                    pool.tensor_tensor(rot[:, 2 * j + 1, H:LD], rot_all[:, 2 * j + 1, H:LD], rows[:, off:off + H], ALU.mult).then_inc(rot_ready, 1)
            body(0)
            with pool.Fori(1, DEPTH) as i:
                body(i)

        @block.tensor
        def _(pe):
            pe.wait_ge(made_mask, 3)

            def body(i):
                pe.wait_ge(y_ready, i + 1)
                for k in range(KT):
                    mm = pe.transpose(c.bank(4)[:, k * S:(k + 1) * S], y[:, k * P:(k + 1) * P], c.ident[:, :])
                mm.then_inc(y_turned, 1)
                pe.wait_ge(tT_ready, i + 1)
                pe.wait_ge(w_in["wqkv"], 16 * i + 16)
                for u, b in enumerate((0, 1, 2, 3, 6, 7)):
                    for k in range(KT):
                        mm = pe.matmul(c.bank(b), tT[:, k, :], wqkv[:, k, u * 512:(u + 1) * 512], start=(k == 0), stop=(k == KT - 1))
                    mm.then_inc(qkv_made, 1)
                for j in range(2):
                    pe.wait_ge(rotated, 2 * i + j + 1)
                    for t in range(LH // 2):
                        mm = pe.transpose(c.bank(2 * j + t // 4)[:, (t % 4) * S:(t % 4 + 1) * S],
                                          qk[j][:, 2 * t:2 * t + 2, :].rearrange("s h d -> s (h d)"), c.ident[:, :])
                    mm.then_inc(qk_turned, 1)
                pe.wait_ge(qkT_ready, 2 * i + 2)
                pe.wait_ge(v_kept, i + 1)
                for par in range(2):
                    for t in range(LH // 2):
                        lo = par * LD
                        mm = pe.matmul(c.bank(4 + 2 * par + t // 4)[:, (t % 4) * S:(t % 4 + 1) * S],
                                       qkT[0][lo:lo + LD, t, :], qkT[1][lo:lo + LD, t, :], start=True, stop=True)
                mm.then_inc(scores_made, 1)
                for hh in range(LH):
                    pe.wait_ge(exp_ready, LH * i + hh + 1)
                    mm = pe.transpose(c.bank(hh // 4)[:, (hh % 4) * S:(hh % 4 + 1) * S], sc[:, hh, :], c.ident[:, :])
                    if hh % 8 == 7:
                        mm.then_inc(p_turned, 1)
                for hh in range(LH):
                    if hh % 8 == 0:
                        pe.wait_ge(pT_ready, 2 * i + hh // 8 + 1)
                    h = 2 * (hh % 8) + hh // 8
                    mm = pe.matmul(c.bank(4 + h // 8)[:, (h % 8) * LD:(h % 8 + 1) * LD], pT[:, hh, :], v[:, h * LD:(h + 1) * LD], start=True, stop=True)
                mm.then_inc(pv_made, 1)
                pe.wait_ge(o_ready, i + 1)
                for t in range(INNER // P):
                    mm = pe.transpose(c.bank(6 + t // 4)[:, (t % 4) * S:(t % 4 + 1) * S],
                                      o[:, 2 * t:2 * t + 2, :].rearrange("s h d -> s (h d)"), c.ident[:, :])
                mm.then_inc(o_turned, 1)
                pe.wait_ge(oT_ready, i + 1)
                pe.wait_ge(w_in["wo"], 16 * i + 16)
                for t in range(INNER // P):
                    mm = pe.matmul(c.bank(0)[:, 0:D], oT[:, t, :], wo[:, t, :], start=(t == 0), stop=(t == INNER // P - 1))
                mm.then_inc(wo_made, 1)
                pe.wait_ge(mid_ready, i + 1)
                pe.matmul(c.bank(1)[:, 0:P], shift[:, :], y[:, P:D], start=True, stop=True).then_inc(shift_made, 1)
                norm.turn(pe, i, c.xn, c.bank(2))
                pe.wait_ge(norm.outT, i + 1)
                pe.wait_ge(w_in["w1"], 16 * i + 16)
                for u in range(2 * FT):
                    t = u % FT
                    w0 = t * P + (FF if u < FT else 0)
                    m = tile_rows(u)
                    for k in range(KT):
                        mm = pe.matmul(h_tile(u, m), w1[:, k, w0:w0 + m], c.xT[:, k, :],
                                       start=(k == 0), stop=(k == KT - 1))
                    if u % FT in (3, FT - 1):
                        mm.then_inc(h_made, 1)
                pe.wait_ge(hT_ready, i + 1)
                pe.wait_ge(w_in["w2"], 32 * i + 32)
                for t in range(FT):
                    m = tile_rows(t)
                    mm = pe.matmul(c.bank(6)[:, 0:D], hT[0:m, t, :], w2[0:m, t, :], start=(t == 0), stop=(t == FT - 1))
                mm.then_inc(w2_made, 1)
            body(0)
            with pe.Fori(1, DEPTH) as i:
                body(i)

        @block.scalar
        def _(act):
            norm0.scalar(act, 0)

            def body(i):
                for j in range(2):
                    act.wait_ge(qkv_made, 6 * i + 2 * j + 2)
                    act.activation(sq[:, j * INNER:(j + 1) * INNER].rearrange("s (b n) -> s b n", b=2), c.ps[:, 2 * j:2 * j + 2, :],
                                   ACT.Square).then_inc(squared, 1)
                act.wait_ge(normed, i + 1)
                act.activation(norms[:, :], norms[:, :], ACT.Sqrt).then_inc(rooted, 1)
                act.wait_ge(qkv_made, 6 * i + 6)
                act.copy(v[:, :].rearrange("s (b n) -> s b n", b=2), c.ps[:, 6:8, :]).then_inc(v_kept, 1)
                act.wait_ge(max_ready, i + 1)
                for hh in range(LH):
                    act.activation(sc[:, hh, :], sc[:, hh, :], ACT.Exp, bias=mx[:, hh:hh + 1], scale=QK_SCALE,
                                   accum_out=total[:, hh:hh + 1]).then_inc(exp_ready, 1)
                norm.scalar(act, i)
                for t in range(FT):
                    m = tile_rows(t)
                    act.wait_ge(h_made, 4 * i + h_signals(t))
                    act.activation(gate[0:m, t, :], h_tile(t, m), ACT.Gelu,
                                   bias=cols[0:m, 2 * KT + t:2 * KT + t + 1]).then_inc(gelu_ready, 1)
            body(0)
            with act.Fori(1, DEPTH) as i:
                body(i)

        @block.vector
        def _(dve):
            STEPS = 18
            first = Chain(dve, steps)
            first(dve.memset(tT[:, 1, 0:1], 0.0))
            dve.wait_ge(made_mask, 3)
            first(dve.memset(shifted[:, :], 0.0))
            norm0.vector(dve, 0, c.x[:, :], y[:, :])
            dve.wait_ge(norm0.out, 1)
            dve.sem_inc(y_ready, 1)

            def body(i):
                chain = Chain(dve, steps, STEPS * i + 2)
                dve.wait_ge(y_turned, i + 1)
                dve.tensor_copy(tT[:, 0, :], c.bank(4)[:, 0:S]).then_inc(steps, 1)
                chain.n += 1
                dve.tensor_copy(tT[:, 1, 1:S], c.bank(4)[:, S:2 * S - 1]).then_inc(tT_ready, 1)
                for j in range(2):
                    dve.wait_ge(squared, 2 * i + j + 1)
                    chain(dve.reduce_sum(norms[:, j * LH:(j + 1) * LH], sq[:, j * INNER:(j + 1) * INNER].rearrange("s (h d) -> s h d", d=LD), AX_X))
                dve.sem_inc(normed, 1)
                dve.wait_ge(rooted, i + 1)
                chain(dve.tensor_scalar(norms[:, :], norms[:, :], 1e-12, None, ALU.max))
                chain(dve.reciprocal(norms[:, :], norms[:, :]))
                dve.wait_ge(rot_ready, 6 * i + 6)
                H = LD // 2
                for j in range(2):
                    src = c.ps[:, 2 * j:2 * j + 2, :].rearrange("s b (h d) -> s (b h) d", d=LD)
                    chain(dve.tensor_tensor(qa[:, :, :], src, norms[:, j * LH:(j + 1) * LH].unsqueeze(2).broadcast_to((S, LH, LD)), ALU.mult))
                    dve.tensor_tensor(qb[:, :, 0:H], qa[:, :, H:LD], rot[:, 2 * j + 1, 0:H].unsqueeze(1).broadcast_to((S, LH, H)), ALU.mult)
                    chain(dve.tensor_tensor(qb[:, :, H:LD], qa[:, :, 0:H], rot[:, 2 * j + 1, H:LD].unsqueeze(1).broadcast_to((S, LH, H)), ALU.mult))
                    chain(dve.tensor_tensor(qa[:, :, :], qa[:, :, :], rot[:, 2 * j, :].unsqueeze(1).broadcast_to((S, LH, LD)), ALU.mult))
                    dve.tensor_tensor(qk[j][:, :, :], qa[:, :, :], qb[:, :, :], ALU.add).then_inc(rotated, 1)
                    dve.wait_ge(rotated, 2 * i + j + 1)
                for j in range(2):
                    dve.wait_ge(qk_turned, 2 * i + j + 1)
                    dve.tensor_copy(qkT[j][:, :, :], c.ps[:, 2 * j:2 * j + 2, :].rearrange("p b (t s) -> p (b t) s", s=S)).then_inc(qkT_ready, 1)
                dve.wait_ge(scores_made, i + 1)
                chain(dve.tensor_tensor(sc[:, :, :], c.ps[:, 4:8, :].rearrange("p b (t s) -> p (b t) s", s=S),
                                        mask[:, :].unsqueeze(1).broadcast_to((S, LH, S)), ALU.add))
                chain(dve.tensor_reduce(mx[:, :], sc[:, :, :], AX_X, ALU.max, negate=True))
                dve.tensor_scalar(mx[:, :], mx[:, :], QK_SCALE, None, ALU.mult).then_inc(max_ready, 1)
                for half in range(2):
                    dve.wait_ge(p_turned, 2 * i + half + 1)
                    dve.tensor_copy(pT[:, 8 * half:8 * half + 8, :], c.ps[:, 2 * half:2 * half + 2, :].rearrange("p b (t s) -> p (b t) s", s=S)).then_inc(pT_ready, 1)
                dve.wait_ge(exp_ready, LH * i + LH)
                chain(dve.reciprocal(inv[:, :, :], total[:, :].rearrange("s (a t) -> s t a", a=2)))
                dve.wait_ge(pv_made, i + 1)
                dve.tensor_tensor(o[:, :, :], c.ps[:, 4:6, :].rearrange("s b (h d) -> s (b h) d", d=LD),
                                  inv[:, :, :].rearrange("s t a -> s (t a)").unsqueeze(2).broadcast_to((S, LH, LD)), ALU.mult).then_inc(o_ready, 1)
                dve.wait_ge(o_turned, i + 1)
                dve.tensor_copy(oT[:, :, :], c.ps[:, 6:8, :].rearrange("p b (t s) -> p (b t) s", s=S)).then_inc(oT_ready, 1)
                dve.wait_ge(wo_made, i + 1)
                chain(dve.tensor_tensor(y[:, :], y[:, :], c.bank(0)[:, 0:D], ALU.add))
                dve.sem_inc(mid_ready, 1)
                dve.tensor_copy(shifted[:, 0:P], y[:, 0:P])
                dve.wait_ge(shift_made, i + 1)
                chain(dve.tensor_copy(shifted[:, P:D], c.bank(1)[:, 0:P]))
                norm.vector(dve, i, shifted[:, :], c.xn[:, :])
                dve.wait_ge(norm.turned, i + 1)
                for k in range(KT):
                    ins = dve.tensor_scalar(c.xT[:, k, :], c.bank(2)[:, k * S:(k + 1) * S], cols[:, k:k + 1], cols[:, KT + k:KT + k + 1], ALU.mult, ALU.add)
                    if k == KT - 1:
                        ins.then_inc(norm.outT, 1)
                for t in range(FT):
                    m = tile_rows(t)
                    u = FT + t
                    dve.wait_ge(h_made, 4 * i + h_signals(u))
                    dve.wait_ge(gelu_ready, FT * i + t + 1)
                    ins = dve.scalar_tensor_tensor(out=hT[0:m, t, :], in0=h_tile(u, m),
                                                   scalar=cols[0:m, 2 * KT + u:2 * KT + u + 1], in1=gate[0:m, t, :], op0=ALU.add, op1=ALU.mult)
                ins.then_inc(hT_ready, 1)
                chain(dve.tensor_tensor(y[:, :], y[:, :], rows[:, B2:B2 + D], ALU.add))
                dve.wait_ge(w2_made, i + 1)
                chain(dve.tensor_tensor(y[:, :], y[:, :], c.bank(6)[:, 0:D], ALU.add))
                dve.sem_inc(y_ready, 1)
                dve.sem_inc(layer_done, 1)
                assert chain.n == STEPS, chain.n
            body(0)
            with dve.Fori(1, DEPTH) as i:
                body(i)
            dve.tensor_tensor(c.x[:, :], c.x[:, :], y[:, :], ALU.add).then_inc(layer_done, 1)
            dve.wait_ge(layer_done, DEPTH + 1)



def lay_out_local(t):
    import numpy as _np
    b1 = _np.zeros((2, FT * P, DEPTH), t["b1"].dtype)
    b1[0, 0:FF] = t["b1"][:, FF:].T
    b1[1, 0:FF] = t["b1"][:, :FF].T
    cols = [t[n].reshape(DEPTH, KT, P).transpose(2, 0, 1) for n in ("ln_g", "ln_b")]
    cols.append(b1.reshape(2 * FT, P, DEPTH).transpose(1, 2, 0))
    return {"Wqkv": t["Wqkv"], "Wo": t["Wo"], "W1": t["W1"], "W2": t["W2"], "rotary": rotary_tables(),
            "cols": _np.concatenate(cols, 2), "rows": _np.concatenate([t["q_scale"], t["k_scale"], t["b2"]], 1)}


RH = 2
LEVELS = S.bit_length() - 1


def level_masks():
    import numpy as np
    i = np.arange(S)
    out = [((i[None, :] >> l) == (i[:, None] >> l) + 1) & (((i[None, :] >> l) & 1) == 1) for l in range(LEVELS)]
    out.append(np.eye(S, dtype=bool))
    return np.stack(out, 1).astype(np.float32)


def gated_recurrence(nc, c):
    with ExitStack() as ctx:
        def sb(nm, shape):
            return ctx.enter_context(nc.sbuf_tensor(f"rec_{nm}", shape, F32))

        def sem(nm):
            return c.sem(f"rec_{nm}")

        w = {n: sb(f"w{n}", [P, KT, D]) for n in "qkvo"}
        gates = sb("gates", [P, 4, RH])
        masks = sb("masks", [S, LEVELS + 1, S])
        qT, vT = sb("qT", [P, RH, S]), sb("vT", [P, RH, S])
        kn, kT = sb("kn", [S, D]), sb("kT", [P, RH, S])
        ksum, sq = sb("ksum", [S, RH]), sb("sq", [S, D])
        gamma, lam = sb("gamma", [P, RH, S]), sb("lam", [P, RH, S])
        decay = [sb(f"decay{l}", [P, RH * S]) for l in range(LEVELS)]
        wk = [sb(f"wk{l}", [P, RH * S]) for l in range(LEVELS)]
        am = sb("am", [S, RH, LEVELS + 1, S])
        wkN = [sb(f"wkN{l}", [S, RH, P]) for l in range(LEVELS)]
        yT, t = sb("yT", [P, RH, S]), sb("t", [P, RH, S])
        norm = Norm(c, "rec_norm")
        w_in, proj_made, qv_kept, squared = sem("w_in"), sem("proj_made"), sem("qv_kept"), sem("squared")
        rooted, kn_ready, k_turned, kT_ready = sem("rooted"), sem("kn_ready"), sem("k_turned"), sem("kT_ready")
        gated, steps, a_made = sem("gates_ready"), sem("steps"), sem("a_made")
        decay_ready, wk_step, wk_ready = sem("decay_ready"), sem("wk_step"), sem("wk_ready")
        wk_turned, wkN_ready, am_ready, level_made, level_used = sem("wk_turned"), sem("wkN_ready"), sem("am_ready"), sem("level_made"), sem("level_used")
        yT_ready, out_made = sem("yT_ready"), sem("out_made")
        block = ctx.enter_context(nc.Block())

        def pair(ap, l):
            return ap.rearrange("p (b a r) -> p b a r", a=2, r=1 << l)

        @block.sync
        def _(sp):
            for n in "kqvo":
                sp.dma_start(w[n][:, :, :], c.rec[f"W{n}"]).then_inc(w_in, 16)
            sp.dma_start(gates[:, :, :], c.rec["gates"]).then_inc(w_in, 16)
            sp.dma_start(masks[:, :, :], c.rec["masks"]).then_inc(w_in, 16)
            sp.wait_ge(w_in, 96)

        @block.tensor
        def _(pe):
            norm.turn(pe, 0, c.xn, c.bank(4))
            pe.wait_ge(norm.outT, 1)
            pe.wait_ge(w_in, 96)
            for k in range(KT):
                mm = pe.matmul(c.bank(0)[:, 0:D], c.xT[:, k, :], w["k"][:, k, :], start=(k == 0), stop=(k == KT - 1))
            mm.then_inc(proj_made, 1)
            for i, n in enumerate("qv"):
                for h in range(RH):
                    for k in range(KT):
                        mm = pe.matmul(c.bank(1 + i)[:, h * S:(h + 1) * S], w[n][:, k, h * P:(h + 1) * P], c.xT[:, k, :],
                                       start=(k == 0), stop=(k == KT - 1))
                mm.then_inc(proj_made, 1)
            pe.wait_ge(qv_kept, 2)
            for h in range(RH):
                mm = pe.matmul(c.bank(3)[:, h * S:(h + 1) * S], vT[:, h, :], qT[:, h, :], start=True, stop=True)
            mm.then_inc(a_made, 1)
            pe.wait_ge(kn_ready, RH)
            for h in range(RH):
                mm = pe.transpose(c.bank(4)[:, h * S:(h + 1) * S], kn[:, h * P:(h + 1) * P], c.ident[:, :])
            mm.then_inc(k_turned, 1)

            def turn(l):
                pe.wait_ge(wk_ready, l + 1)
                if l >= 2:
                    pe.wait_ge(wkN_ready, l - 1)
                for h in range(RH):
                    mm = pe.transpose(c.bank(l % 2)[:, h * P:(h + 1) * P], wk[l][:, h * S:(h + 1) * S], c.ident[:, :])
                mm.then_inc(wk_turned, 1)

            def level(n, l, j):
                if l == 0:
                    pe.wait_ge(am_ready, RH)
                pe.wait_ge(wkN_ready, l + 1)
                if n >= 2:
                    pe.wait_ge(level_used, n - 1)
                for h in range(RH):
                    mm = pe.matmul(c.bank(6 + n % 2)[:, h * S:(h + 1) * S], wkN[l][:, h, :], am[:, h, j, :], start=True, stop=True)
                mm.then_inc(level_made, 1)

            turn(0)
            turn(1)
            level(0, 0, LEVELS)
            for l in range(LEVELS):
                if l + 2 < LEVELS:
                    turn(l + 2)
                level(l + 1, l, l)
            pe.wait_ge(yT_ready, 1)
            for k in range(KT):
                mm = pe.matmul(c.bank(5)[:, 0:D], yT[:, k, :], w["o"][:, k, :], start=(k == 0), stop=(k == KT - 1))
            mm.then_inc(out_made, 1)

        @block.scalar
        def _(act):
            norm.scalar(act, 0)
            act.wait_ge(proj_made, 1)
            for h in range(RH):
                act.activation(sq[:, h * P:(h + 1) * P], c.bank(0)[:, h * P:(h + 1) * P], ACT.Square, accum_out=ksum[:, h:h + 1]).then_inc(squared, 1)
            act.wait_ge(squared, RH)
            act.activation(ksum[:, :], ksum[:, :], ACT.Sqrt).then_inc(rooted, 1)
            act.wait_ge(w_in, 96)
            act.wait_ge(kT_ready, 1)
            for h in range(RH):
                act.activation(gamma[:, h, :], kT[:, h, :], ACT.Sigmoid, bias=gates[:, 1, h:h + 1], scale=gates[:, 0, h:h + 1]).then_inc(gated, 1)
                act.activation(lam[:, h, :], kT[:, h, :], ACT.Sigmoid, bias=gates[:, 3, h:h + 1], scale=gates[:, 2, h:h + 1]).then_inc(gated, 1)
            for l in range(LEVELS):
                act.wait_ge(wk_turned, l + 1)
                act.copy(wkN[l][:, :, :].rearrange("s h k -> s (h k)"), c.bank(l % 2)[:, 0:RH * P]).then_inc(wkN_ready, 1)

        @block.gpsimd
        def _(pool):
            for l in range(1, LEVELS):
                pool.wait_ge(decay_ready, l)
                pool.wait_ge(wk_ready, l)
                old, new, d = pair(wk[l - 1][:, :], l - 1), pair(wk[l][:, :], l - 1), pair(decay[l - 1][:, :], l - 1)
                r = 1 << (l - 1)
                pool.tensor_copy(new[:, :, 1, :], old[:, :, 1, :]).then_inc(wk_step, 1)
                pool.wait_ge(wk_step, l)
                pool.tensor_tensor(new[:, :, 0, :], old[:, :, 0, :], d[:, :, 1, r - 1:r].broadcast_to((P, S // r, r)), ALU.mult).then_inc(wk_ready, 1)

        @block.vector
        def _(dve):
            chain = Chain(dve, steps)
            norm.vector(dve, 0, c.x[:, :], c.xn[:, :])
            norm.keep(dve, 0, c.bank(4), c.xT[:, :, :])
            dve.wait_ge(rooted, 1)
            chain(dve.tensor_scalar(ksum[:, :], ksum[:, :], 1e-12, None, ALU.max))
            chain(dve.reciprocal(ksum[:, :], ksum[:, :]))
            for h in range(RH):
                dve.tensor_scalar(kn[:, h * P:(h + 1) * P], c.bank(0)[:, h * P:(h + 1) * P], ksum[:, h:h + 1], None, ALU.mult).then_inc(kn_ready, 1)
            for i, dst in enumerate((qT, vT)):
                dve.wait_ge(proj_made, 2 + i)
                dve.tensor_copy(dst[:, :, :].rearrange("p h s -> p (h s)"), c.bank(1 + i)[:, 0:RH * S]).then_inc(qv_kept, 1)
            dve.wait_ge(k_turned, 1)
            dve.tensor_copy(kT[:, :, :].rearrange("p h s -> p (h s)"), c.bank(4)[:, 0:RH * S]).then_inc(kT_ready, 1)
            dve.wait_ge(a_made, 1)
            for h in range(RH):
                dve.tensor_tensor(am[:, h, :, :], c.bank(3)[:, h * S:(h + 1) * S].unsqueeze(1).broadcast_to((S, LEVELS + 1, S)), masks[:, :, :], ALU.mult).then_inc(am_ready, 1)
            dve.wait_ge(gated, 2 * RH)
            flat = [g[:, :, :].rearrange("p h s -> p (h s)") for g in (gamma, lam, kT)]
            chain(dve.tensor_scalar(flat[1], flat[1], -1.0, 1.0, ALU.mult, ALU.add))
            dve.tensor_tensor(decay[0][:, :], flat[1], flat[0], ALU.mult).then_inc(decay_ready, 1)
            dve.wait_ge(decay_ready, 1)
            chain(dve.tensor_scalar(flat[0], decay[0][:, :], -1.0, 1.0, ALU.mult, ALU.add))
            dve.tensor_tensor(wk[0][:, :], flat[0], flat[2], ALU.mult).then_inc(wk_ready, 1)
            for l in range(1, LEVELS):
                old, new = pair(decay[l - 1][:, :], l - 1), pair(decay[l][:, :], l - 1)
                r = 1 << (l - 1)
                dve.tensor_copy(new[:, :, 0, :], old[:, :, 0, :])
                dve.tensor_tensor(new[:, :, 1, :], old[:, :, 1, :], old[:, :, 0, r - 1:r].broadcast_to((P, S // r, r)), ALU.mult).then_inc(decay_ready, 1)
                dve.wait_ge(decay_ready, l + 1)
            dve.wait_ge(level_made, 1)
            y = yT[:, :, :].rearrange("p h s -> p (h s)")
            tf = t[:, :, :].rearrange("p h s -> p (h s)")
            dve.tensor_copy(y, c.bank(6)[:, 0:RH * S]).then_inc(level_used, 1)
            for l in range(LEVELS):
                dve.wait_ge(level_made, l + 2)
                dve.tensor_tensor(tf, c.bank(6 + (l + 1) % 2)[:, 0:RH * S], decay[l][:, :], ALU.mult).then_inc(level_used, 1)
                dve.wait_ge(level_used, l + 2)
                ins = dve.tensor_tensor(y, y, tf, ALU.add)
                if l < LEVELS - 1:
                    chain(ins)
            ins.then_inc(yT_ready, 1)
            dve.wait_ge(out_made, 1)
            chain(dve.tensor_tensor(c.x[:, :], c.x[:, :], c.bank(5)[:, 0:D], ALU.add))



def lay_out_recurrence(t):
    import numpy as _np
    return {**{f"W{n}": t[f"W{n}"].T for n in "qkvo"}, "masks": level_masks(),
            "gates": _np.stack([t[n].T for n in ("W_gamma", "b_gamma", "W_lambda", "b_lambda")], 1)}


NE = 8
EF = 1024
ET = EF // P
TOP = 2


def experts(nc, c):
    with ExitStack() as ctx:
        def sb(nm, shape):
            return ctx.enter_context(nc.sbuf_tensor(f"moe_{nm}", shape, F32))

        def sem(nm):
            return c.sem(f"moe_{nm}")

        gw, b2 = sb("gate_w", [P, KT, NE]), sb("b2", [NE, D])
        w1 = [sb(f"w1_{i}", [P, KT, EF]) for i in range(2)]
        w2 = [sb(f"w2_{i}", [P, ET, D]) for i in range(2)]
        b1 = [sb(f"b1_{i}", [P, ET]) for i in range(2)]
        hT = [sb(f"hT{i}", [P, ET, S]) for i in range(2)]
        earlier = sb("earlier", [S, NE, NE])
        logit, ex = sb("logit", [S, NE]), sb("ex", [S, NE])
        beats, ties = sb("beats", [S, NE, NE]), sb("ties", [S, NE, NE])
        rank, neg_max, total = sb("rank", [S, NE]), sb("neg_max", [S, 1]), sb("total", [S, 1])
        combine, combT = sb("combine", [S, NE]), sb("combT", [NE, S])
        share = [sb(f"share{i}", [S, 1]) for i in range(2)]
        norm = Norm(c, "moe_norm")
        small_in, filled, earlier_made = sem("small_in"), sem("filled"), sem("earlier_made")
        up_in, down_in = [sem(f"up_in{i}") for i in range(2)], [sem(f"down_in{i}") for i in range(2)]
        logits_made, max_ready, ex_ready, steps = sem("logits_made"), sem("max_ready"), sem("ex_ready"), sem("steps")
        combine_ready, comb_turned, combT_ready, bias_made = sem("combine_ready"), sem("comb_turned"), sem("combT_ready"), sem("bias_made")
        up_made, h_ready, down_made, added, shared = sem("up_made"), sem("h_ready"), sem("down_made"), sem("added"), sem("shared")
        block = ctx.enter_context(nc.Block())

        @block.sync
        def _(sp):
            sp.dma_start(gw[:, :, :], c.moe["gate_w"]).then_inc(small_in, 16)
            sp.dma_start(b2[:, :], c.moe["b2"]).then_inc(small_in, 16)

            def load(e, par):
                def one(w):
                    return w[bass.ds(e, 1)].rearrange("o r n -> (o r) n")
                first = isinstance(e, int) and e < 2
                if not first:
                    sp.wait_ge(h_ready, ET * (e - 1))
                sp.dma_start(w1[par][:, :, :], tiled(one(c.moe["W1"]))).then_inc(up_in[par], 16)
                sp.dma_start(b1[par][:, :], one(c.moe["b1"])).then_inc(up_in[par], 16)
                if not first:
                    sp.wait_ge(down_made, e - 1)
                sp.dma_start(w2[par][:, :, :], tiled(one(c.moe["W2"]))).then_inc(down_in[par], 16)
            for par in range(2):
                load(par, par)
            with sp.Fori(1, NE // 2) as i:
                for par in range(2):
                    load(2 * i + par, par)

        @block.gpsimd
        def _(pool):
            pool.memset(earlier[:, :, :], 1.0).then_inc(filled, 1)
            pool.wait_ge(filled, 1)
            pool.affine_select(out=earlier[:, :, :], in_=earlier[:, :, :], compare_op=ALU.is_gt, fill=0.0,
                               base=0, pattern=[[1, NE], [-1, NE]], channel_multiplier=0).then_inc(earlier_made, 1)

        @block.tensor
        def _(pe):
            norm.turn(pe, 0, c.xn, c.bank(4))
            pe.wait_ge(norm.outT, 1)
            pe.wait_ge(small_in, 32)
            for k in range(KT):
                mm = pe.matmul(c.bank(6)[:, 0:NE], c.xT[:, k, :], gw[:, k, :], start=(k == 0), stop=(k == KT - 1))
            mm.then_inc(logits_made, 1)

            def up(e, par, i):
                pe.wait_ge(up_in[par], 32 * i + 32)
                if not (isinstance(e, int) and e < 2):
                    pe.wait_ge(h_ready, ET * (e - 1))
                for t in range(ET):
                    for k in range(KT):
                        mm = pe.matmul(c.bank(2 * par + t // 4)[:, (t % 4) * S:(t % 4 + 1) * S], w1[par][:, k, t * P:(t + 1) * P], c.xT[:, k, :],
                                       start=(k == 0), stop=(k == KT - 1))
                    if t % 4 == 3:
                        mm.then_inc(up_made, 1)

            def down(e, par, i):
                pe.wait_ge(down_in[par], 16 * i + 16)
                if not (isinstance(e, int) and e < 2):
                    pe.wait_ge(added, e - 1)
                for t in range(ET):
                    pe.wait_ge(h_ready, ET * e + t + 1)
                    mm = pe.matmul(c.bank(4 + par)[:, 0:D], hT[par][:, t, :], w2[par][:, t, :], start=(t == 0), stop=(t == ET - 1))
                mm.then_inc(down_made, 1)

            up(0, 0, 0)
            pe.wait_ge(combine_ready, 1)
            pe.transpose(c.bank(7)[0:NE, 0:S], combine[:, :], c.ident[:, :]).then_inc(comb_turned, 1)
            pe.wait_ge(combT_ready, 1)
            pe.matmul(c.bank(6)[:, D:2 * D], combT[:, :], b2[:, :], start=True, stop=True).then_inc(bias_made, 1)

            def body(i):
                for par in range(2):
                    e = 2 * i + par
                    if not (isinstance(e, int) and e == NE - 1):
                        up(e + 1, 1 - par, i + par)
                    down(e, par, i)
            body(0)
            with pe.Fori(1, NE // 2 - 1) as i:
                body(i)
            body(NE // 2 - 1)

        @block.scalar
        def _(act):
            norm.scalar(act, 0)
            act.wait_ge(max_ready, 1)
            act.activation(ex[:, :], logit[:, :], ACT.Exp, bias=neg_max[:, 0:1]).then_inc(ex_ready, 1)

            def body(i):
                for par in range(2):
                    e = 2 * i + par
                    act.wait_ge(up_in[par], 32 * i + 32)
                    if not (isinstance(e, int) and e < 2):
                        act.wait_ge(down_made, e - 1)
                    for t in range(ET):
                        act.wait_ge(up_made, 2 * e + t // 4 + 1)
                        act.activation(hT[par][:, t, :], c.bank(2 * par + t // 4)[:, (t % 4) * S:(t % 4 + 1) * S], ACT.Gelu,
                                       bias=b1[par][:, t:t + 1]).then_inc(h_ready, 1)
            body(0)
            with act.Fori(1, NE // 2) as i:
                body(i)

        @block.vector
        def _(dve):
            chain = Chain(dve, steps)
            norm.vector(dve, 0, c.x[:, :], c.xn[:, :])
            norm.keep(dve, 0, c.bank(4), c.xT[:, :, :])
            dve.wait_ge(logits_made, 1)
            chain(dve.tensor_copy(logit[:, :], c.bank(6)[:, 0:NE]))
            dve.tensor_reduce(neg_max[:, :], logit[:, :], AX_X, ALU.max, negate=True).then_inc(max_ready, 1)
            other = logit[:, :].unsqueeze(1).broadcast_to((S, NE, NE))
            own = logit[:, :].unsqueeze(2).broadcast_to((S, NE, NE))
            chain(dve.tensor_tensor(beats[:, :, :], other, own, ALU.is_gt))
            chain(dve.tensor_tensor(ties[:, :, :], other, own, ALU.is_equal))
            dve.wait_ge(earlier_made, 1)
            chain(dve.tensor_tensor(ties[:, :, :], ties[:, :, :], earlier[:, :, :], ALU.mult))
            chain(dve.tensor_tensor(beats[:, :, :], beats[:, :, :], ties[:, :, :], ALU.add))
            chain(dve.reduce_sum(rank[:, :], beats[:, :, :], AX_X))
            chain(dve.tensor_scalar(rank[:, :], rank[:, :], float(TOP), None, ALU.is_lt))
            dve.wait_ge(ex_ready, 1)
            chain(dve.tensor_tensor(combine[:, :], ex[:, :], rank[:, :], ALU.mult))
            chain(dve.reduce_sum(total[:, :], combine[:, :], AX_X))
            chain(dve.reciprocal(total[:, :], total[:, :]))
            dve.tensor_scalar(combine[:, :], combine[:, :], total[:, 0:1], None, ALU.mult).then_inc(combine_ready, 1)
            dve.wait_ge(comb_turned, 1)
            dve.tensor_copy(combT[:, :], c.bank(7)[0:NE, 0:S]).then_inc(combT_ready, 1)
            dve.wait_ge(bias_made, 1)
            chain(dve.tensor_tensor(c.x[:, :], c.x[:, :], c.bank(6)[:, D:2 * D], ALU.add))

            def body(i):
                for par in range(2):
                    e = 2 * i + par
                    if not (isinstance(e, int) and e == 0):
                        dve.wait_ge(added, e)
                    dve.tensor_copy(share[par][:, :], combine[:, bass.ds(e, 1)]).then_inc(shared, 1)
                    dve.wait_ge(shared, e + 1)
                    dve.wait_ge(down_made, e + 1)
                    dve.scalar_tensor_tensor(out=c.x[:, :], in0=c.bank(4 + par)[:, 0:D], scalar=share[par][:, 0:1], in1=c.x[:, :],
                                             op0=ALU.mult, op1=ALU.add).then_inc(added, 1)
            body(0)
            with dve.Fori(1, NE // 2) as i:
                body(i)
            dve.wait_ge(added, NE)



def lay_out_experts(t):
    return {"gate_w": t["gate_w"], "W1": t["W1"], "b1": t["b1"].reshape(NE, ET, P).transpose(0, 2, 1), "W2": t["W2"], "b2": t["b2"]}


CF = 1024
CT = CF // P


def biased_feed_forward(nc, c):
    with ExitStack() as ctx:
        def sb(nm, shape):
            return ctx.enter_context(nc.sbuf_tensor(f"cff_{nm}", shape, F32))

        def sem(nm):
            return c.sem(f"cff_{nm}")

        w1, w2 = sb("w1", [P, KT, CF]), sb("w2", [P, CT, D])
        cols, rows = sb("cols", [P, 2 * KT + CT]), sb("rows", [S, 3, D])
        hT = sb("hT", [P, CT, S])
        norm = Norm(c, "cff_norm")
        w_in, up_made, h_ready, down_made, steps = sem("w_in"), sem("up_made"), sem("h_ready"), sem("down_made"), sem("steps")
        block = ctx.enter_context(nc.Block())

        @block.sync
        def _(sp):
            sp.dma_start(cols[:, :], c.cff["cols"]).then_inc(w_in, 16)
            sp.dma_start(rows[:, :, :].rearrange("s l n -> s (l n)"),
                         c.cff["rows"].rearrange("(o l) n -> o (l n)", o=1).broadcast_to((S, 3 * D))).then_inc(w_in, 16)
            sp.dma_start(w1[:, :, :], c.cff["W1"]).then_inc(w_in, 16)
            sp.dma_start(w2[:, :, :], c.cff["W2"]).then_inc(w_in, 16)

        @block.tensor
        def _(pe):
            norm.turn(pe, 0, c.xn, c.bank(4))
            pe.wait_ge(norm.outT, 1)
            pe.wait_ge(w_in, 64)
            for t in range(CT):
                for k in range(KT):
                    mm = pe.matmul(c.bank(t // 4)[:, (t % 4) * S:(t % 4 + 1) * S], w1[:, k, t * P:(t + 1) * P], c.xT[:, k, :],
                                   start=(k == 0), stop=(k == KT - 1))
                if t % 4 == 3:
                    mm.then_inc(up_made, 1)
            for t in range(CT):
                pe.wait_ge(h_ready, t + 1)
                mm = pe.matmul(c.bank(5)[:, 0:D], hT[:, t, :], w2[:, t, :], start=(t == 0), stop=(t == CT - 1))
            mm.then_inc(down_made, 1)

        @block.scalar
        def _(act):
            norm.scalar(act, 0)
            act.wait_ge(w_in, 64)
            for t in range(CT):
                act.wait_ge(up_made, t // 4 + 1)
                act.activation(hT[:, t, :], c.bank(t // 4)[:, (t % 4) * S:(t % 4 + 1) * S], ACT.Gelu,
                               bias=cols[:, 2 * KT + t:2 * KT + t + 1]).then_inc(h_ready, 1)
            norm.scalar(act, 1)

        @block.vector
        def _(dve):
            chain = Chain(dve, steps)
            norm.vector(dve, 0, c.z[:, :], c.xn[:, :])
            dve.wait_ge(w_in, 64)
            dve.wait_ge(norm.turned, 1)
            for k in range(KT):
                ins = dve.tensor_scalar(c.xT[:, k, :], c.bank(4)[:, k * S:(k + 1) * S], cols[:, k:k + 1], cols[:, KT + k:KT + k + 1], ALU.mult, ALU.add)
            ins.then_inc(norm.outT, 1)
            chain(dve.tensor_tensor(c.z[:, :], c.z[:, :], rows[:, 0, :], ALU.add))
            dve.wait_ge(down_made, 1)
            chain(dve.tensor_tensor(c.z[:, :], c.z[:, :], c.bank(5)[:, 0:D], ALU.add))
            norm.vector(dve, 1, c.z[:, :], c.xn[:, :])
            dve.wait_ge(norm.out, 2)
            chain(dve.tensor_tensor(c.xn[:, :], c.xn[:, :], rows[:, 1, :], ALU.mult))
            chain(dve.tensor_tensor(c.xn[:, :], c.xn[:, :], rows[:, 2, :], ALU.add))
            chain(dve.tensor_tensor(c.x[:, :], c.x[:, :], c.xn[:, :], ALU.add))


def program(nc, a, out):
    with ExitStack() as ctx:
        c = Core(nc, ctx)
        c.x_dram, c.ctxT = a["x"], a["ctxT"]
        c.T = c.ctxT.shape[1]
        c.z = c.sb("z_rows", [S, D])
        c.wkA, c.wkD, c.wvA, c.wvD = (tiled(a[k]) for k in ("wkA", "wkD", "wvA", "wvD"))
        c.k2_dram = nc.dram_tensor("keys2_scratch", (KT, P, c.T), F32).ap()
        c.v1_dram = nc.dram_tensor("vals1_scratch", (NKV, P, c.T // P, HD), F32).ap()
        c.v2_dram = nc.dram_tensor("vals2_scratch", (NH, P, c.T // P, HD), F32).ap()

        def part(prefix, matrices):
            return {k[len(prefix):]: (tiled(v) if k[len(prefix):] in matrices else v) for k, v in a.items() if k.startswith(prefix)}

        c.rel = part("rel_", ("W_q", "W_k", "W_v", "W_o"))
        c.loc = part("loc_", ())
        c.cff = part("cff_", ("W1", "W2"))
        c.rec = part("rec_", ("Wq", "Wk", "Wv", "Wo"))
        c.moe = part("moe_", ("gate_w",))

        def cross(name, rows, wq, groups, v_dram, heads_per_v, bias, keys_dram, wo, base, dst):
            with ExitStack() as mem:
                c.qm = mem.enter_context(nc.sbuf_tensor(f"{name}_queries", [P, NH, S], F32))
                c.attn = mem.enter_context(nc.sbuf_tensor(f"{name}_attn", [S, D], F32))
                c.scores = [mem.enter_context(nc.sbuf_tensor(f"{name}_scores{i}", [P, c.T], F32)) for i in range(2)]
                c.run(queries, name, wq, rows, groups)
                c.run(attention, name, rows, v_dram, heads_per_v, bias, keys_dram)
                c.run(project_out, name, wo, base, dst)

        c.run(consts)
        with nc.sbuf_tensor("gqa_keys", [P, c.T], F32) as c.keys:
            c.run(context_products)
            cross("gqa", KVA, tiled(a["wqA"]), True, c.v1_dram, GRP, None, None, tiled(a["woA"]), c.x, c.x)
        c.run(relative_attention)
        c.run(local_transformer)
        with nc.sbuf_tensor("biased_keys", [P, c.T], F32) as c.keys:
            cross("biased", P, tiled(a["wqD"]), False, c.v2_dram, 1, a["bias"], c.k2_dram, tiled(a["woD"]), c.xn, c.z)
        c.run(biased_feed_forward)
        c.run(gated_recurrence)
        c.run(experts)
        c.run(store_x, out)


def lay_out(i):
    import numpy as _np
    t = {k: _np.asarray(v) for k, v in i.items()}

    def part(prefix):
        return {k[len(prefix):]: v for k, v in t.items() if k.startswith(prefix)}

    gqa, rel, bia = part("L0_xattn_"), part("L0_attn_"), part("L1_xattn_")
    out = {
        "x": t["x"][0], "ctxT": t["ctx_1024"][0].T, "bias": t["fside_Bx16xSxS2_0"][0],
        "wqA": gqa["Wq"].reshape(NKV, GRP, HD, D).transpose(3, 1, 0, 2).reshape(D, D),
        "wkA": gqa["Wk"].T, "wvA": gqa["Wv"].T, "woA": gqa["Wo"].T,
        "wqD": bia["Wq"].T, "wkD": bia["Wk"].T, "wvD": bia["Wv"].T, "woD": bia["Wo"].T,
    }
    for n in "qk":
        rel[f"b_{n}"] = rel[f"b_{n}"].reshape(KT, P).T
    rel["rel_kT"] = rel.pop("rel_k_table").T
    cff = {"W1": bia["W1"].T, "W2": bia["W2"].T, "rows": _np.stack([bia["b2"], bia["g2"], bia["be2"]]),
           "cols": _np.concatenate([bia["g1"].reshape(KT, P).T, bia["be1"].reshape(KT, P).T, bia["b1"].reshape(CT, P).T], 1)}
    parts = {"rel_": rel, "loc_": lay_out_local(part("L0_ffn_")), "cff_": cff,
             "rec_": lay_out_recurrence(part("L1_attn_")), "moe_": lay_out_experts(part("L1_ffn_"))}
    for prefix, p in parts.items():
        out.update({prefix + k: v for k, v in p.items()})
    return out


def kernel(**inputs):
    import numpy as _np
    import concourse.bacc as _bacc
    from concourse import mybir as _mybir
    from concourse.bass_utils import run_bass_kernel_spmd as _run

    nc = _bacc.Bacc("TRN2", target_bir_lowering=False, num_devices=1)
    arrays, aps = {}, {}
    for name, a in lay_out(inputs).items():
        a = _np.ascontiguousarray(a)
        arrays[f"in_{name}"] = a
        aps[name] = nc.dram_tensor(f"in_{name}", a.shape, _mybir.dt.from_np(a.dtype), kind="ExternalInput").ap()
    out = nc.dram_tensor("out_x", (1, S, D), F32, kind="ExternalOutput").ap()
    program(nc, aps, out)
    r = _run(nc, [arrays], core_ids=[0])
    return r.results[0]["out_x"]
```

```python
from contextlib import ExitStack

import concourse.bass as bass
from concourse import mybir

F32 = mybir.dt.float32
F32R = mybir.dt.float32r
ALU = mybir.AluOpType
ACT = mybir.ActivationFunctionType
AX_X = mybir.AxisListType.X

P = 128
S = 128
D = 256
KT = D // P
NH = 16
HD = D // NH
NKV = 4
GRP = NH // NKV
KVA = NKV * HD
BLK = 7
CH = BLK * P
HC = CH // 2
PA = 4
LOWEST = -3.0e38
HPT = P // HD
KG = 4
KR = KG * HD
SPLIT = 2
LN_EPS = 1e-5


class Core:

    def __init__(self, nc, ctx):
        self.nc, self.ctx, self.sems = nc, ctx, []
        self.ps = self.psum("banks", [P, 8, 512])
        self.sc = [self.ps[:, 2 * i:2 * i + 2, :] for i in range(2)]
        self.single = [self.ps[:, 4 + i, :] for i in range(4)]

    def sb(self, name, shape, dt=F32):
        return self.ctx.enter_context(self.nc.sbuf_tensor(name, shape, dt))

    def psum(self, name, shape, dt=F32):
        return self.ctx.enter_context(self.nc.psum_tensor(name, shape, dt))

    def sem(self, name):
        self.sems.append(self.nc.alloc_semaphore(name))
        return self.sems[-1]

    def run(self, stage, *args):
        stage(self.nc, self, *args)
        self.nc.clear_and_free_semaphores(self.sems)
        self.nc.all_engine_barrier()
        self.sems = []

    def bank(self, i):
        return self.ps[:, i, :]


class Chain:

    def __init__(self, eng, sem, base=0):
        self.eng, self.sem, self.base, self.n = eng, sem, base, 0

    def __call__(self, ins):
        ins.then_inc(self.sem, 1)
        self.n += 1
        self.eng.wait_ge(self.sem, self.base + self.n)


def consts(nc, c):
    c.ident = c.sb("ident", [P, P])
    c.headmask = c.sb("headmask", [P, HPT])
    c.keymask = c.sb("keymask", [P, KG])
    c.fold = c.sb("fold", [SPLIT * HD, HD])
    c.eps = c.sb("eps", [P, 1])
    c.x = c.sb("x_rows", [S, D])
    c.xn = c.sb("x_normed", [S, D])
    c.xT = c.sb("x_normedT", [P, KT, S])
    c.gate, c.gates = c.sb("gate", [S, 16]), 0
    c.stats = c.sb("ln_stats", [S, 6])
    c.mv = c.sb("ln_mean_var", [S, 2])
    c.std = c.sb("ln_std", [S, 1])
    c.rstd = c.sb("ln_rstd", [S, 1])
    filled, selected, loaded = c.sem("const_filled"), c.sem("const_selected"), c.sem("x_loaded")
    folded = c.sem("fold_made")
    with nc.Block() as block:
        @block.sync
        def _(sp):
            sp.dma_start(c.x[:, :], c.x_dram).then_inc(loaded, 16)
            sp.wait_ge(loaded, 16)

        @block.gpsimd
        def _(pool):
            pool.memset(c.ident[:, :], 0.0).then_inc(filled, 1)
            pool.memset(c.headmask[:, :], 1.0).then_inc(filled, 1)
            pool.memset(c.eps[:, :], LN_EPS).then_inc(filled, 1)
            pool.memset(c.fold[:, :], 0.0).then_inc(filled, 1)
            pool.wait_ge(filled, 4)
            for part in range(SPLIT):
                pool.affine_select(out=c.fold[:, :], in_=c.fold[:, :], compare_op=ALU.not_equal, fill=1.0,
                                   base=-HD * part, pattern=[[-1, HD]], channel_multiplier=1).then_inc(folded, 1)
                pool.wait_ge(folded, part + 1)
            pool.affine_select(out=c.ident[:, :], in_=c.ident[:, :], compare_op=ALU.not_equal, fill=1.0,
                               base=0, pattern=[[-1, P]], channel_multiplier=1).then_inc(selected, 1)
            pool.affine_select(out=c.headmask[:, :], in_=c.headmask[:, :], compare_op=ALU.is_ge, fill=0.0,
                               base=0, pattern=[[-HD, HPT]], channel_multiplier=1).then_inc(selected, 1)
            pool.wait_ge(selected, 2)
            pool.affine_select(out=c.headmask[:, :], in_=c.headmask[:, :], compare_op=ALU.is_ge, fill=0.0,
                               base=HD - 1, pattern=[[HD, HPT]], channel_multiplier=-1).then_inc(selected, 1)
            pool.wait_ge(selected, 3)
            pool.tensor_tensor(c.keymask[:, :], c.headmask[:, 0:KG], c.headmask[:, KG:HPT], ALU.add).then_inc(selected, 1)
            pool.wait_ge(selected, 4)


class Norm:

    def __init__(self, c, name):
        self.c = c
        self.gate = c.gate[:, c.gates:c.gates + 1]
        c.gates += 1
        self.gated = c.sem(f"{name}_gated")
        self.stats = c.sem(f"{name}_stats")
        self.var = c.sem(f"{name}_var")
        self.std = c.sem(f"{name}_std")
        self.rstd = c.sem(f"{name}_rstd")
        self.out = c.sem(f"{name}_out")
        self.turned = c.sem(f"{name}_turned")
        self.outT = c.sem(f"{name}_outT")

    def vector(self, dve, n, x, out):
        c = self.c
        dve.bn_stats(c.stats[:, :], x).then_inc(self.stats, 1)
        dve.wait_ge(self.stats, n + 1)
        if not (isinstance(n, int) and n == 0):
            dve.wait_ge(self.gated, n)
        dve.memset(self.gate, 0.0).then_inc(self.gated, 1)
        dve.bn_aggr(c.mv[:, :], c.stats[:, :]).then_inc(self.var, 1)
        dve.wait_ge(self.std, n + 1)
        dve.reciprocal(c.rstd[:, :], c.std[:, :]).then_inc(self.rstd, 1)
        dve.wait_ge(self.rstd, n + 1)
        dve.tensor_scalar(out, x, c.mv[:, 0:1], c.rstd[:, 0:1], ALU.subtract, ALU.mult).then_inc(self.out, 1)

    def scalar(self, act, n):
        c = self.c
        act.wait_ge(self.var, n + 1)
        act.activation(c.std[:, :], c.mv[:, 1:2], ACT.Sqrt, bias=c.eps[:, 0:1]).then_inc(self.std, 1)

    def turn(self, pe, n, src, bank):
        pe.wait_ge(self.out, n + 1)
        for k in range(KT):
            mm = pe.transpose(bank[:, k * S:(k + 1) * S], src[:, k * P:(k + 1) * P], self.c.ident[:, :])
        mm.then_inc(self.turned, 1)

    def keep(self, dve, n, bank, dst):
        dve.wait_ge(self.turned, n + 1)
        dve.tensor_copy(dst, bank[:, 0:KT * S].rearrange("p (k s) -> p k s", k=KT)).then_inc(self.outT, 1)


def context_products(nc, c):
    T = c.T
    n_chunks = T // CH
    W = KVA + D
    VH = NKV + NH
    with ExitStack() as ctx:
        def sb(name, shape, dt=F32):
            return ctx.enter_context(nc.sbuf_tensor(name, shape, dt))

        ctx_tile = [sb(f"ctx_tile{i}", [P, KT, CH]) for i in range(2)]
        wk, wv = sb("wk_both", [P, KT, W]), sb("wv_both", [P, KT, W])
        keys = [sb(f"keys_out{i}", [P, SPLIT, 1 + KT, CH], F32R) for i in range(2)]
        vals = [sb(f"vals_out{i}", [P, VH, BLK, SPLIT, HD], F32R) for i in range(2)]
        w_in = c.sem("kv_weights_in")
        ctx_in = [c.sem(f"ctx_in{i}") for i in range(2)]
        stored = [c.sem(f"kv_stored{i}") for i in range(2)]
        k_made = c.sem("k_made")
        k_high, k_low = c.sem("k_high"), c.sem("k_low")
        v_made = c.sem("v_made")
        v_high, v_low = c.sem("v_high"), c.sem("v_low")
        k_units = [(KVA, 0, 0, n) for n in range(2)] + [(P, KVA + m * P, 1 + m, n) for m in range(KT) for n in range(2)]
        KU = len(k_units)
        STORES = 2 * SPLIT * KT + SPLIT + 1
        block = ctx.enter_context(nc.Block())

        def first(i):
            return isinstance(i, int) and i == 0

        @block.sync
        def _(sp):
            sp.dma_start(wk[:, :, 0:KVA], c.wkA).then_inc(w_in, 16)
            sp.dma_start(wk[:, :, KVA:W], c.wkD).then_inc(w_in, 16)
            sp.dma_start(wv[:, :, 0:KVA], c.wvA).then_inc(w_in, 16)
            sp.dma_start(wv[:, :, KVA:W], c.wvD).then_inc(w_in, 16)
            ctx_v = c.ctxT.rearrange("(k p) t -> p k t", p=P)
            for par in range(2):
                sp.dma_start(ctx_tile[par][:, :, :], ctx_v[:, :, par * CH:(par + 1) * CH]).then_inc(ctx_in[par], 16)

            def store(i, par):
                cols = bass.ds((2 * i + par) * CH, CH)
                sp.wait_ge(k_low, KU * (2 * i + par + 1))
                for part in range(SPLIT):
                    rows = slice(part * KR, (part + 1) * KR)
                    sp.dma_start(c.k1_dram[0, rows, cols], keys[par][0:KR, part, 0, :].bitcast(F32)).then_inc(stored[par], 16)
                    for m in range(KT):
                        for a in range(2):
                            sp.dma_start(c.k2_dram[2 * m + a, rows, cols], keys[par][a * KR:(a + 1) * KR, part, 1 + m, :].bitcast(F32)).then_inc(stored[par], 16)
                sp.wait_ge(v_low, BLK * (2 * i + par + 1))
                sp.dma_start(c.v_dram.rearrange("h p n d -> p h n d")[:, :, bass.ds((2 * i + par) * BLK, BLK), :],
                             vals[par][:, :, :, :, :].rearrange("p h b s d -> p h b (s d)").bitcast(F32)).then_inc(stored[par], 16)

            def load(i, par):
                sp.wait_ge(v_made, BLK * (2 * i + par - 1))
                sp.dma_start(ctx_tile[par][:, :, :], ctx_v[:, :, bass.ds((2 * i + par) * CH, CH)]).then_inc(ctx_in[par], 16)

            if n_chunks > 2:
                with sp.Fori(1, n_chunks // 2) as i:
                    for par in range(2):
                        load(i, par)
                        store(i - 1, par)
            for par in range(2):
                store(n_chunks // 2 - 1, par)
            for par in range(2):
                sp.wait_ge(stored[par], 16 * STORES * (n_chunks // 2))

        def each_chunk(eng, body):
            for par in range(2):
                body(0, par)
            if n_chunks > 2:
                with eng.Fori(1, n_chunks // 2) as i:
                    for par in range(2):
                        body(i, par)

        @block.tensor
        def _(pe):
            pe.wait_ge(w_in, 64)

            def body(i, par):
                ch = 2 * i + par
                pe.wait_ge(ctx_in[par], 16 * (i + 1))
                for u, (m, w0, _, n) in enumerate(k_units):
                    if not (first(i) and par == 0):
                        pe.wait_ge(k_low, KU * (ch - 1) + u + 1)
                    for k in range(KT):
                        mm = pe.matmul(c.bank(u)[0:m, 0:HC], wk[:, k, w0:w0 + m], ctx_tile[par][:, k, n * HC:(n + 1) * HC],
                                       start=(k == 0), stop=(k == KT - 1))
                    mm.then_inc(k_made, 1)
                for b in range(BLK):
                    u = BLK * par + b
                    if not (first(i) and u < 2):
                        pe.wait_ge(v_low, BLK * ch + b - 1)
                    for k in range(KT):
                        mm = pe.matmul(c.bank(6 + u % 2)[:, 0:W], ctx_tile[par][:, k, b * P:(b + 1) * P], wv[:, k, :],
                                       start=(k == 0), stop=(k == KT - 1))
                    mm.then_inc(v_made, 1)
            each_chunk(pe, body)

        def v_unit(par, b):
            return c.bank(6 + (BLK * par + b) % 2)[:, 0:W].rearrange("p (h d) -> p h d", d=HD)

        @block.scalar
        def _(act):
            def body(i, par):
                ch = 2 * i + par
                if not first(i):
                    act.wait_ge(stored[par], 16 * STORES * i)
                for u, (m, _, r, n) in enumerate(k_units):
                    act.wait_ge(k_made, KU * ch + u + 1)
                    act.copy(keys[par][0:m, 0, r, n * HC:(n + 1) * HC], c.bank(u)[0:m, 0:HC]).then_inc(k_high, 1)
                for b in range(BLK):
                    act.wait_ge(v_made, BLK * ch + b + 1)
                    act.copy(vals[par][:, :, b, 0, :], v_unit(par, b)).then_inc(v_high, 1)
            each_chunk(act, body)

        @block.vector
        def _(dve):
            def body(i, par):
                ch = 2 * i + par
                if not first(i):
                    dve.wait_ge(stored[par], 16 * STORES * i)
                for u, (m, _, r, n) in enumerate(k_units):
                    cols = slice(n * HC, (n + 1) * HC)
                    dve.wait_ge(k_high, KU * ch + u + 1)
                    dve.tensor_tensor(keys[par][0:m, 1, r, cols], c.bank(u)[0:m, 0:HC], keys[par][0:m, 0, r, cols].bitcast(F32),
                                      ALU.subtract).then_inc(k_low, 1)
                for b in range(BLK):
                    dve.wait_ge(v_high, BLK * ch + b + 1)
                    dve.tensor_tensor(vals[par][:, :, b, 1, :], v_unit(par, b), vals[par][:, :, b, 0, :].bitcast(F32),
                                      ALU.subtract).then_inc(v_low, 1)
            each_chunk(dve, body)


def queries(nc, c, name, w_dram, groups):
    tiles = NH // KG
    with ExitStack() as ctx:
        wq = ctx.enter_context(nc.sbuf_tensor(f"{name}_wq", [P, KT, tiles * P], F32))
        w_in = c.sem(f"{name}_wq_in")
        q = ctx.enter_context(nc.sbuf_tensor(f"{name}_q", [P, NH, S], F32))
        made = c.sem(f"{name}_q_made")
        kept = c.sem(f"{name}_q_kept")
        split = c.sem(f"{name}_q_split")
        norm = Norm(c, f"{name}_norm")
        block = ctx.enter_context(nc.Block())

        @block.sync
        def _(sp):
            sp.dma_start(wq[:, :, :], w_dram).then_inc(w_in, 16)
            sp.wait_ge(w_in, 16)

        @block.scalar
        def _(act):
            norm.scalar(act, 0)

        @block.tensor
        def _(pe):
            norm.turn(pe, 0, c.xn, c.bank(4))
            pe.wait_ge(norm.outT, 1)
            pe.wait_ge(w_in, 16)
            for t in range(tiles):
                for k in range(KT):
                    mm = pe.matmul(c.bank(t)[:, 0:S], wq[:, k, t * P:(t + 1) * P], c.xT[:, k, :],
                                   start=(k == 0), stop=(k == KT - 1))
                mm.then_inc(made, 1)

        @block.vector
        def _(dve):
            norm.vector(dve, 0, c.x[:, :], c.xn[:, :])
            norm.keep(dve, 0, c.bank(4), c.xT[:, :, :])
            for t in range(tiles):
                dve.wait_ge(made, t + 1)
                for g in range(KG):
                    h = GRP * g + t if groups else t * KG + g
                    dve.tensor_scalar(q[:, h, :], c.bank(t)[:, 0:S], c.keymask[:, g:g + 1],
                                      float(HD) ** -0.5, ALU.mult, ALU.mult).then_inc(kept, 1)
            dve.wait_ge(kept, NH)
            dve.tensor_copy(c.qm[:, :, 0, :], q[:, :, :]).then_inc(split, 1)
            dve.wait_ge(split, 1)
            dve.tensor_tensor(c.qm[:, :, 1, :], q[:, :, :], c.qm[:, :, 0, :].bitcast(F32), ALU.subtract).then_inc(split, 1)
            dve.wait_ge(split, 2)


def attention(nc, c, name, v_dram, heads_per_v, bias, keys_dram):
    T = c.T
    NC = T // CH
    NB = T // P
    HALF = NC // 2
    HB = HALF * CH
    LEAD = 2
    key_tiles = keys_dram.shape[0]
    with ExitStack() as ctx:
        def sb(nm, shape, dt=F32):
            return ctx.enter_context(nc.sbuf_tensor(f"{name}_{nm}", shape, dt))

        def sem(nm):
            return c.sem(f"{name}_{nm}")

        q_head = [sb(f"q_head{i}", [P, SPLIT, S], F32R) for i in range(2)]
        v_half = [sb(f"v_half{j}", [P, NB // 2, SPLIT * HD], F32R) for j in range(2)]
        keys = sb("keys", [P, T], F32R)
        s = c.scores
        probT = [sb(f"probT{i}", [P, SPLIT, BLK, S], F32R) for i in range(2)]
        chunk_max = [sb(f"chunk_max{i}", [S, NC]) for i in range(2)]
        neg_max = [sb(f"neg_max{i}", [S, 1]) for i in range(2)]
        chunk_sum = [sb(f"chunk_sum{i}", [S, NC]) for i in range(2)]
        total, inv_total = sb("total", [S, 1]), sb("inv_total", [S, 1])
        gate = sb("gate", [S, 1])
        outT = [sb(f"outT{i}", [SPLIT * HD, S]) for i in range(2)]
        q_staged = sem("q_staged")
        v_in = [sem(f"v_in{j}") for j in range(2)]
        bias_in = [[sem(f"bias_in{i}{j}") for j in range(2)] for i in range(2)]
        keys_in = [sem(f"keys_in{j}") for j in range(2)]
        made = sem("scores_made")
        kept = sem("scores_kept")
        max_ready = sem("max_ready")
        exp_ready = sem("exp_ready")
        turned = [sem("turned_a"), sem("turned_b")]
        high = [sem("prob_high_a"), sem("prob_high_b")]
        low = [sem("prob_low_a"), sem("prob_low_b")]
        pv_done = sem("pv_done")
        outT_kept = sem("outT_kept")
        out_ready = sem("out_ready")
        head_done = sem("head_done")
        step = sem("small_step")
        gated = sem("gated")
        block = ctx.enter_context(nc.Block())
        units = [(0, PA), (PA, BLK)]
        PAIRS = NH // 2
        PPT = PAIRS // key_tiles

        def ahead(ch):
            return [n for n in range(NC) if n * (NC - LEAD) // NC == ch]

        def known(h):
            return isinstance(h, int)

        def one(ap, h):
            return ap[h:h + 1] if known(h) else ap[bass.ds(h, 1)]

        def pairs(eng, body):
            peeled = sorted({0, PAIRS - 1} | {t * PPT - 1 for t in range(1, key_tiles)})
            for a, b in zip(peeled, peeled[1:]):
                body(a)
                if b - a == 2:
                    body(a + 1)
                elif b - a > 2:
                    with eng.Fori(a + 1, b) as it:
                        body(it)
            body(PAIRS - 1)

        @block.sync
        def _(sp):
            def load_v(h, j):
                sp.dma_start(v_half[j][:, :, :].bitcast(F32),
                             one(v_dram, h // heads_per_v)[:, :, j * (NB // 2):(j + 1) * (NB // 2), :].rearrange("o p n d -> (o p) n d")).then_inc(v_in[j], 16)

            def load_bias(h, par, j):
                sp.dma_start(s[par][:, j * HB:(j + 1) * HB], one(bias, h)[:, :, j * HB:(j + 1) * HB].rearrange("o q t -> (o q) t")).then_inc(bias_in[par][j], 16)

            def load_keys(t, j):
                sp.dma_start(keys[:, j * HB:(j + 1) * HB].bitcast(F32), keys_dram[t, :, j * HB:(j + 1) * HB]).then_inc(keys_in[j], 16)

            for j in range(2):
                load_keys(0, j)
                if bias is not None:
                    load_bias(0, 0, j)
            for j in range(2):
                load_v(0, j)
                if bias is not None:
                    load_bias(1, 1, j)

            def body(it):
                for par in range(2):
                    h = 2 * it + par
                    changes = known(h) and par == 0 and (it + 1) % PPT == 0 and it < PAIRS - 1
                    if known(h) and h == NH - 1:
                        continue
                    for j in range(2):
                        if changes:
                            sp.wait_ge(made, (h + 1) * NC + HALF * (j + 1))
                            load_keys((it + 1) // PPT, j)
                        if bias is not None and not (known(h) and h == NH - 2):
                            sp.wait_ge(turned[1], h * NC + HALF * (j + 1))
                            load_bias(h + 2, par, j)
                        sp.wait_ge(pv_done, h * NC + HALF * (j + 1))
                        load_v(h + 1, j)
            pairs(sp, body)

        @block.gpsimd
        def _(pool):
            def stage(h, par):
                src = c.qm[:, h, :, :] if known(h) else c.qm[:, bass.ds(h, 1), :, :].rearrange("p o a s -> p (o a) s")
                pool.tensor_copy(q_head[par][:, :, :], src).then_inc(q_staged, 1)

            for par in range(2):
                stage(par, par)

            def body(it):
                if known(it) and it == PAIRS - 1:
                    return
                for par in range(2):
                    h = 2 * it + par
                    pool.wait_ge(made, (h + 1) * NC)
                    stage(h + 2, par)
            pairs(pool, body)

        @block.tensor
        def _(pe):
            def scores(h, par, ch):
                n = h * NC + ch
                if ch == 0:
                    pe.wait_ge(q_staged, h + 1)
                if ch % HALF == 0 and known(h) and h % (2 * PPT) == 0:
                    pe.wait_ge(keys_in[ch // HALF], 16 * (h // (2 * PPT) + 1))
                if not (known(h) and n < 2):
                    pe.wait_ge(kept, n - 1)
                for part in range(SPLIT):
                    for k in range(2):
                        mm = pe.matmul(c.sc[ch % 2][:, k, 0:HC], q_head[par][:, part, :],
                                       keys[:, ch * CH + k * HC:ch * CH + (k + 1) * HC], start=(part == 0), stop=(part == SPLIT - 1))
                mm.then_inc(made, 1)

            def turn(h, par, ch):
                n = h * NC + ch
                pe.wait_ge(exp_ready, n + 1)
                for u, (b0, b1) in enumerate(units):
                    if not (known(h) and n == 0):
                        pe.wait_ge(low[u], n)
                    for b in range(b0, b1):
                        col = ch * CH + b * P
                        mm = pe.transpose(c.single[u][:, (b - b0) * S:(b - b0 + 1) * S], s[par][:, col:col + P], c.ident[:, :])
                    mm.then_inc(turned[u], 1)

            def weigh(h, par, ch):
                if ch == 0 and not (known(h) and h < 2):
                    pe.wait_ge(head_done, h - 1)
                if ch % HALF == 0:
                    pe.wait_ge(v_in[ch // HALF], 16 * (h + 1))
                for u, (b0, b1) in enumerate(units):
                    pe.wait_ge(low[u], h * NC + ch + 1)
                    for b in range(b0, b1):
                        for part in range(SPLIT):
                            mm = pe.matmul(c.single[2 + par][0:SPLIT * HD, 0:S], v_half[ch // HALF][:, (ch % HALF) * BLK + b, :],
                                           probT[ch % 2][:, part, b, :],
                                           start=(ch == 0 and b == 0 and part == 0), stop=(ch == NC - 1 and b == BLK - 1 and part == SPLIT - 1))
                mm.then_inc(pv_done, 1)

            def fold(h, par):
                pe.wait_ge(outT_kept, h + 1)
                pe.matmul(c.single[2 + par][:, 2 * P:2 * P + HD], outT[par][:, :], c.fold[:, :],
                          start=True, stop=True).then_inc(out_ready, 1)

            for ch in range(NC):
                scores(0, 0, ch)

            def body(it):
                for par in range(2):
                    h = 2 * it + par
                    for ch in range(NC):
                        if not (known(h) and h == NH - 1):
                            for n in ahead(ch):
                                scores(h + 1, 1 - par, n)
                        turn(h, par, ch)
                        if ch >= 1:
                            weigh(h, par, ch - 1)
                        elif not (known(h) and h == 0):
                            weigh(h - 1, 1 - par, NC - 1)
                        if ch == 1 and not (known(h) and h == 0):
                            fold(h - 1, 1 - par)
            pairs(pe, body)
            weigh(NH - 1, 1, NC - 1)
            fold(NH - 1, 1)

        @block.scalar
        def _(act):
            def exp(h, par, ch):
                if ch == 0:
                    act.wait_ge(max_ready, h + 1)
                    if not (known(h) and h < 2):
                        act.wait_ge(head_done, h - 1)
                part = s[par][:, ch * CH:(ch + 1) * CH]
                act.activation(part, part, ACT.Exp, bias=neg_max[par][:, 0:1],
                               accum_out=chunk_sum[par][:, ch:ch + 1]).then_inc(exp_ready, 1)

            def keep_out(h, par):
                act.wait_ge(pv_done, (h + 1) * NC)
                act.copy(outT[par][:, :], c.single[2 + par][0:SPLIT * HD, 0:S]).then_inc(outT_kept, 1)

            for ch in range(LEAD):
                exp(0, 0, ch)

            def body(it):
                for par in range(2):
                    h = 2 * it + par
                    for ch in range(NC):
                        n = h * NC + ch
                        for u, (b0, b1) in enumerate(units):
                            act.wait_ge(turned[u], n + 1)
                            if u == 0 and not (known(h) and n < 2):
                                act.wait_ge(pv_done, n - 1)
                            act.copy(probT[ch % 2][:, 0, b0:b1, :], c.single[u][:, 0:(b1 - b0) * S].rearrange("p (b s) -> p b s", s=S)).then_inc(high[u], 1)
                        if ch + LEAD < NC:
                            exp(h, par, ch + LEAD)
                        elif not (known(h) and h == NH - 1):
                            exp(h + 1, 1 - par, ch + LEAD - NC)
                        if ch == 0 and not (known(h) and h == 0):
                            keep_out(h - 1, 1 - par)
            pairs(act, body)
            keep_out(NH - 1, 1)

        @block.vector
        def _(dve):
            def keep(h, par, ch, it_in):
                n = h * NC + ch
                dve.wait_ge(made, n + 1)
                src = c.sc[ch % 2][:, :, 0:HC]
                dst = s[par][:, ch * CH:(ch + 1) * CH].rearrange("p (k n) -> p k n", k=2)
                if bias is None:
                    if not (known(h) and h < 2):
                        dve.wait_ge(turned[1], (h - 2) * NC + ch + 1)
                    dve.tensor_scalar(dst, src, 1.0, LOWEST, ALU.mult, ALU.max,
                                      accum_out=chunk_max[par][:, ch:ch + 1]).then_inc(kept, 1)
                else:
                    if ch % HALF == 0:
                        dve.wait_ge(bias_in[par][ch // HALF], 16 * (it_in + 1))
                    if not (known(h) and n == 0):
                        dve.wait_ge(gated, n)
                    dve.memset(gate[:, :], 0.0).then_inc(gated, 1)
                    dve.tensor_tensor_reduce(dst, src, dst, 1.0, LOWEST, ALU.add, ALU.max,
                                             chunk_max[par][:, ch:ch + 1]).then_inc(kept, 1)

            def head_max(h, par):
                dve.wait_ge(kept, (h + 1) * NC)
                if not (known(h) and h < 2):
                    dve.wait_ge(exp_ready, (h - 1) * NC)
                dve.tensor_reduce(neg_max[par][:, :], chunk_max[par][:, :], AX_X, ALU.max, negate=True).then_inc(max_ready, 1)

            def low_parts(h, ch):
                n = h * NC + ch
                for u, (b0, b1) in enumerate(units):
                    dve.wait_ge(high[u], n + 1)
                    dve.tensor_tensor(probT[ch % 2][:, 1, b0:b1, :], c.single[u][:, 0:(b1 - b0) * S].rearrange("p (b s) -> p b s", s=S),
                                      probT[ch % 2][:, 0, b0:b1, :].bitcast(F32), ALU.subtract).then_inc(low[u], 1)

            def divide(h, par):
                dve.wait_ge(exp_ready, (h + 1) * NC)
                dve.reduce_sum(total[:, :], chunk_sum[par][:, :], AX_X).then_inc(step, 1)
                dve.wait_ge(step, 2 * h + 1)
                dve.reciprocal(inv_total[:, :], total[:, :]).then_inc(step, 1)
                dve.wait_ge(step, 2 * h + 2)
                dve.wait_ge(out_ready, h + 1)
                dve.tensor_scalar(c.attn[:, bass.ds(h * HD, HD)], c.single[2 + par][:, 2 * P:2 * P + HD],
                                  inv_total[:, 0:1], None, ALU.mult).then_inc(head_done, 1)

            for ch in range(NC):
                keep(0, 0, ch, 0)
            head_max(0, 0)

            def body(it):
                for par in range(2):
                    h = 2 * it + par
                    for ch in range(NC):
                        for n in ahead(ch):
                            if not (known(h) and h == NH - 1):
                                keep(h + 1, 1 - par, n, it + par)
                                if n == NC - 1:
                                    head_max(h + 1, 1 - par)
                        low_parts(h, ch)
                        if ch == 2 and not (known(h) and h == 0):
                            divide(h - 1, 1 - par)
            pairs(dve, body)
            divide(NH - 1, 1)


def project_out(nc, c, name, w_dram, base, dst):
    with ExitStack() as ctx:
        w = ctx.enter_context(nc.sbuf_tensor(f"{name}_wo", [P, KT, D], F32))
        w_in = c.sem(f"{name}_wo_in")
        turned = c.sem(f"{name}_attn_turned")
        attnT = c.sem(f"{name}_attnT_kept")
        made = c.sem(f"{name}_out_made")
        added = c.sem(f"{name}_x_added")
        block = ctx.enter_context(nc.Block())

        @block.sync
        def _(sp):
            sp.dma_start(w[:, :, :], w_dram).then_inc(w_in, 16)

        @block.tensor
        def _(pe):
            for k in range(KT):
                mm = pe.transpose(c.bank(4)[:, k * S:(k + 1) * S], c.attn[:, k * P:(k + 1) * P], c.ident[:, :])
            mm.then_inc(turned, 1)
            pe.wait_ge(attnT, 1)
            pe.wait_ge(w_in, 16)
            for k in range(KT):
                mm = pe.matmul(c.bank(5)[:, 0:D], c.xT[:, k, :], w[:, k, :], start=(k == 0), stop=(k == KT - 1))
            mm.then_inc(made, 1)

        @block.vector
        def _(dve):
            dve.wait_ge(turned, 1)
            dve.tensor_copy(c.xT[:, :, :], c.bank(4)[:, 0:KT * S].rearrange("p (k s) -> p k s", k=KT)).then_inc(attnT, 1)
            dve.wait_ge(made, 1)
            dve.tensor_tensor(dst[:, :], base[:, :], c.bank(5)[:, 0:D], ALU.add).then_inc(added, 1)
            dve.wait_ge(added, 1)


def relative_attention(nc, c):
    R = 5
    BAND = 3
    with ExitStack() as ctx:
        def sb(nm, shape):
            return ctx.enter_context(nc.sbuf_tensor(f"rel_{nm}", shape, F32))

        def sem(nm):
            return c.sem(f"rel_{nm}")

        w = {n: sb(f"w{n}", [P, KT, D]) for n in "qkvo"}
        bcol = {n: sb(f"bcol_{n}", [P, KT]) for n in "qk"}
        brow = {n: sb(f"brow_{n}", [S, D]) for n in "vo"}
        relk = sb("relk", [P, R])
        relk_heads = sb("relk_heads", [P, HPT, R])
        relv = sb("relv", [S, R, HD])
        band = sb("band", [S, BAND, S])
        qT, kT, v = sb("qT", [P, KT, S]), sb("kT", [P, KT, S]), sb("v", [S, D])
        qm = sb("qm", [P, NH, S])
        r = sb("r", [S, NH, R])
        sc, t = sb("scores", [S, NH, S]), sb("t", [S, NH, S])
        pT = sb("pT", [S, NH, S])
        mx, total, wgt = sb("mx", [S, NH]), sb("total", [S, NH]), sb("wgt", [S, BAND, NH])
        o, ot = sb("o", [S, NH, HD]), sb("ot", [S, NH, HD])
        norm = Norm(c, "rel_norm")
        w_in, band_step, band_made = sem("w_in"), sem("band_step"), sem("band_made")
        proj_made, q_ready, scores_made, r_made = sem("proj_made"), sem("q_ready"), sem("scores_made"), sem("r_made")
        rel_added, masked, max_ready, exp_ready = sem("rel_added"), sem("masked"), sem("max_ready"), sem("exp_ready")
        p_turned, pT_ready, pv_made, o_ready = sem("p_turned"), sem("pT_ready"), sem("pv_made"), sem("o_ready")
        o_turned, oT_ready, out_made, steps = sem("o_turned"), sem("oT_ready"), sem("out_made"), sem("steps")
        LOADS = 4 + 2 + 2 + HPT + 1
        block = ctx.enter_context(nc.Block())

        @block.sync
        def _(sp):
            for n in "qkvo":
                sp.dma_start(w[n][:, :, :], c.rel[f"W_{n}"]).then_inc(w_in, 16)
            for n in "qk":
                sp.dma_start(bcol[n][:, :], c.rel[f"b_{n}"]).then_inc(w_in, 16)
            for n in "vo":
                sp.dma_start(brow[n][:, :], c.rel[f"b_{n}"].rearrange("(o d) -> o d", o=1).broadcast_to((S, D))).then_inc(w_in, 16)
            for h in range(HPT):
                sp.dma_start(relk[h * HD:(h + 1) * HD, :], c.rel["rel_kT"]).then_inc(w_in, 16)
            sp.dma_start(relv[:, :, :].rearrange("p r d -> p (r d)"),
                         c.rel["rel_v_table"].rearrange("(o r) d -> o (r d)", o=1).broadcast_to((S, R * HD))).then_inc(w_in, 16)
            sp.wait_ge(w_in, 16 * LOADS)

        @block.gpsimd
        def _(pool):
            pool.memset(band[:, 0, :], 1.0).then_inc(band_step, 1)
            pool.memset(band[:, 1, :], 0.0).then_inc(band_step, 1)
            pool.tensor_copy(band[:, 2, :], c.ident[:, :]).then_inc(band_step, 1)
            pool.wait_ge(band_step, 3)
            pool.affine_select(out=band[:, 0, :], in_=band[:, 0, :], compare_op=ALU.is_ge, fill=0.0,
                               base=-2, pattern=[[-1, S]], channel_multiplier=1).then_inc(band_made, 1)
            pool.affine_select(out=band[:, 1, :], in_=band[:, 1, :], compare_op=ALU.not_equal, fill=1.0,
                               base=-1, pattern=[[-1, S]], channel_multiplier=1).then_inc(band_made, 1)
            pool.wait_ge(rel_added, 1)
            pool.affine_select(out=sc[:, :, :], in_=sc[:, :, :], compare_op=ALU.is_ge, fill=-1.0e9 * HD ** 0.5,
                               base=0, pattern=[[0, NH], [-1, S]], channel_multiplier=1).then_inc(masked, 1)

        @block.scalar
        def _(act):
            norm.scalar(act, 0)
            act.wait_ge(max_ready, 1)
            for h in range(NH):
                act.activation(sc[:, h, :], sc[:, h, :], ACT.Exp, bias=mx[:, h:h + 1], scale=HD ** -0.5,
                               accum_out=total[:, h:h + 1]).then_inc(exp_ready, 1)

        @block.tensor
        def _(pe):
            norm.turn(pe, 0, c.xn, c.bank(4))
            pe.wait_ge(norm.outT, 1)
            pe.wait_ge(w_in, 16 * LOADS)
            for i, n in enumerate("qk"):
                for m in range(KT):
                    for k in range(KT):
                        mm = pe.matmul(c.bank(i)[:, m * S:(m + 1) * S], w[n][:, k, m * P:(m + 1) * P], c.xT[:, k, :],
                                       start=(k == 0), stop=(k == KT - 1))
                mm.then_inc(proj_made, 1)
            for k in range(KT):
                mm = pe.matmul(c.bank(2)[:, 0:D], c.xT[:, k, :], w["v"][:, k, :], start=(k == 0), stop=(k == KT - 1))
            mm.then_inc(proj_made, 1)
            pe.wait_ge(q_ready, 1)
            for m in range(KT):
                mm = pe.matmul(c.bank(5)[:, m * HPT * R:(m + 1) * HPT * R], qT[:, m, :],
                               relk_heads[:, :, :].rearrange("p h r -> p (h r)"), start=True, stop=True)
            mm.then_inc(r_made, 1)
            pe.wait_ge(q_ready, 2)
            for h in range(NH):
                mm = pe.matmul(c.bank(h // 4)[:, (h % 4) * S:(h % 4 + 1) * S], qm[:, h, :], kT[:, h // HPT, :], start=True, stop=True)
            mm.then_inc(scores_made, 1)
            for h in range(NH):
                pe.wait_ge(exp_ready, h + 1)
                mm = pe.transpose(c.bank(h // 4)[:, (h % 4) * S:(h % 4 + 1) * S], sc[:, h, :], c.ident[:, :])
            mm.then_inc(p_turned, 1)
            pe.wait_ge(pT_ready, 1)
            for h in range(NH):
                mm = pe.matmul(c.bank(6)[:, h * HD:(h + 1) * HD], pT[:, h, :], v[:, h * HD:(h + 1) * HD], start=True, stop=True)
            mm.then_inc(pv_made, 1)
            pe.wait_ge(o_ready, 1)
            for k in range(KT):
                mm = pe.transpose(c.bank(4)[:, k * S:(k + 1) * S], o[:, k * HPT:(k + 1) * HPT, :].rearrange("p h d -> p (h d)"), c.ident[:, :])
            mm.then_inc(o_turned, 1)
            pe.wait_ge(oT_ready, 1)
            for k in range(KT):
                mm = pe.matmul(c.bank(7)[:, 0:D], c.xT[:, k, :], w["o"][:, k, :], start=(k == 0), stop=(k == KT - 1))
            mm.then_inc(out_made, 1)

        @block.vector
        def _(dve):
            chain = Chain(dve, steps)
            dve.wait_ge(w_in, 16 * LOADS)
            chain(dve.tensor_tensor(relk_heads[:, :, :], relk[:, :].unsqueeze(1).broadcast_to((P, HPT, R)),
                                    c.headmask[:, :].unsqueeze(2).broadcast_to((P, HPT, R)), ALU.mult))
            norm.vector(dve, 0, c.x[:, :], c.xn[:, :])
            norm.keep(dve, 0, c.bank(4), c.xT[:, :, :])
            dve.wait_ge(proj_made, 1)
            for m in range(KT):
                chain(dve.tensor_scalar(qT[:, m, :], c.bank(0)[:, m * S:(m + 1) * S], bcol["q"][:, m:m + 1], None, ALU.add))
            dve.sem_inc(q_ready, 1)
            dve.wait_ge(proj_made, 2)
            for m in range(KT):
                chain(dve.tensor_scalar(kT[:, m, :], c.bank(1)[:, m * S:(m + 1) * S], bcol["k"][:, m:m + 1], None, ALU.add))
            for h in range(NH):
                ins = dve.tensor_scalar(qm[:, h, :], qT[:, h // HPT, :], c.headmask[:, h % HPT:h % HPT + 1], None, ALU.mult)
            chain(ins)
            dve.wait_ge(proj_made, 3)
            chain(dve.tensor_tensor(v[:, :], c.bank(2)[:, 0:D], brow["v"][:, :], ALU.add))
            dve.sem_inc(q_ready, 1)
            dve.wait_ge(r_made, 1)
            chain(dve.tensor_copy(r[:, :, :].rearrange("p h r -> p (h r)"), c.bank(5)[:, 0:NH * R]))
            dve.wait_ge(band_made, 2)
            dve.wait_ge(scores_made, 1)
            for j in range(BAND):
                chain(dve.tensor_tensor(t[:, :, :], band[:, j, :].unsqueeze(1).broadcast_to((S, NH, S)),
                                        r[:, :, j:j + 1].broadcast_to((S, NH, S)), ALU.mult))
                acc = c.ps[:, 0:4, :].rearrange("p b (h s) -> p (b h) s", s=S) if j == 0 else sc[:, :, :]
                ins = dve.tensor_tensor(sc[:, :, :], acc, t[:, :, :], ALU.add)
                if j < BAND - 1:
                    chain(ins)
            ins.then_inc(rel_added, 1)
            dve.wait_ge(masked, 1)
            chain(dve.tensor_reduce(mx[:, :], sc[:, :, :], AX_X, ALU.max, negate=True))
            dve.tensor_scalar(mx[:, :], mx[:, :], HD ** -0.5, None, ALU.mult).then_inc(max_ready, 1)
            dve.wait_ge(p_turned, 1)
            dve.tensor_copy(pT[:, :, :], c.ps[:, 0:4, :].rearrange("p b (h s) -> p (b h) s", s=S)).then_inc(pT_ready, 1)
            dve.wait_ge(exp_ready, NH)
            for j in range(BAND):
                chain(dve.tensor_tensor(t[:, :, :], sc[:, :, :], band[:, j, :].unsqueeze(1).broadcast_to((S, NH, S)), ALU.mult))
                chain(dve.reduce_sum(wgt[:, j, :], t[:, :, :], AX_X))
            dve.wait_ge(pv_made, 1)
            for j in range(BAND):
                chain(dve.tensor_tensor(ot[:, :, :], wgt[:, j, :].unsqueeze(2).broadcast_to((S, NH, HD)),
                                        relv[:, j, :].unsqueeze(1).broadcast_to((S, NH, HD)), ALU.mult))
                acc = c.bank(6)[:, 0:D].rearrange("p (h d) -> p h d", d=HD) if j == 0 else o[:, :, :]
                chain(dve.tensor_tensor(o[:, :, :], acc, ot[:, :, :], ALU.add))
            chain(dve.reciprocal(total[:, :], total[:, :]))
            dve.tensor_tensor(o[:, :, :], o[:, :, :], total[:, :].unsqueeze(2).broadcast_to((S, NH, HD)), ALU.mult).then_inc(o_ready, 1)
            chain(dve.tensor_tensor(c.x[:, :], c.x[:, :], brow["o"][:, :], ALU.add))
            dve.wait_ge(o_turned, 1)
            dve.tensor_copy(c.xT[:, :, :], c.bank(4)[:, 0:KT * S].rearrange("p (k s) -> p k s", k=KT)).then_inc(oT_ready, 1)
            dve.wait_ge(out_made, 1)
            chain(dve.tensor_tensor(c.x[:, :], c.x[:, :], c.bank(7)[:, 0:D], ALU.add))


def tiled(w):
    return w.rearrange("(k p) n -> p k n", p=P)


def store_x(nc, c, out):
    stored = c.sem("x_stored")
    with nc.Block() as block:
        @block.sync
        def _(sp):
            sp.dma_start(out.rearrange("o s d -> (o s) d"), c.x[:, :]).then_inc(stored, 16)
            sp.wait_ge(stored, 16)


LH, LD = 16, 64
INNER = LH * LD
WINDOW = 64
QK_SCALE = 8.0
DEPTH = 6
FF = int(D * 4 * 2 / 3)
FT = -(-FF // P)
FLAST = FF - (FT - 1) * P
MASKED = -1.0e30


def rotary_tables():
    import numpy as np
    f = np.float32
    half = np.arange(0, LD, 2, dtype=f)
    inv_freq = (f(1.0) / f(10000.0) ** (half / f(LD))).astype(f)
    t = np.arange(S, dtype=f)
    freqs = np.concatenate([t[:, None] * inv_freq[None, :]] * 2, -1)
    base = (half + f(0.4 * LD)) / f(1.4 * LD)
    scale = base[None, :] ** ((t - S // 2) / f(WINDOW // 2))[:, None]
    scale = np.concatenate([scale, scale], -1)
    sign = np.where(np.arange(LD) < LD // 2, f(-1), f(1))
    cos, sin = np.cos(freqs), np.sin(freqs) * sign
    return np.stack([cos * scale, sin * scale, cos / scale, sin / scale], 1).astype(f)


def local_transformer(nc, c):
    with ExitStack() as ctx:
        def sb(nm, shape):
            return ctx.enter_context(nc.sbuf_tensor(f"loc_{nm}", shape, F32))

        def sem(nm):
            return c.sem(f"loc_{nm}")

        wqkv, wo = sb("wqkv", [P, KT, 3 * INNER]), sb("wo", [P, INNER // P, D])
        w1, w2 = sb("w1", [P, KT, 2 * FF]), sb("w2", [P, FT, D])
        cols_all, rows_all = sb("cols_all", [P, DEPTH, 2 * KT + 2 * FT]), sb("rows_all", [S, DEPTH, 2 * LD + D])
        cols, rows = sb("cols", [P, 2 * KT + 2 * FT]), sb("rows", [S, 2 * LD + D])
        rot_all, rot = sb("rot_all", [S, 4, LD]), sb("rot", [S, 4, LD])
        shift, mask = sb("shift", [S, S]), sb("mask", [S, S])
        y, shifted = sb("y", [S, D]), sb("shifted", [S, D])
        tT, hT = sb("tT", [P, KT, S]), sb("hT", [P, FT, S])
        v, sq = sb("v", [S, INNER]), sb("sq", [S, 2 * INNER])
        norms = sb("norms", [S, 2 * LH])
        qk = [sb(f"qk{i}", [S, LH, LD]) for i in range(2)]
        qa, qb = sb("qa", [S, LH, LD]), sb("qb", [S, LH, LD])
        qkT = [sb(f"qkT{i}", [P, LH // 2, S]) for i in range(2)]
        sc, pT = sb("sc", [S, LH, S]), sb("pT", [S, LH, S])
        mx, total, inv = sb("mx", [S, LH]), sb("total", [S, LH]), sb("inv", [S, LH // 2, 2])
        o, oT = sb("o", [S, LH, LD]), sb("oT", [P, INNER // P, S])
        gate = sb("gate", [P, FT, S])

        norm0, norm = Norm(c, "loc_in"), Norm(c, "loc_norm")
        small_in, made_mask, mask_step = sem("small_in"), sem("mask_made"), sem("mask_step")
        w_in = {n: sem(f"{n}_in") for n in ("wqkv", "wo", "w1", "w2")}
        y_ready, y_turned, tT_ready = sem("y_ready"), sem("y_turned"), sem("tT_ready")
        qkv_made, squared, normed = sem("qkv_made"), sem("squared"), sem("sums_ready")
        rooted, v_kept = sem("norms_rooted"), sem("v_kept")
        rotated, qk_turned, qkT_ready = sem("qk_rotated"), sem("qk_turned"), sem("qkT_ready")
        rot_ready, rot_step = sem("rot_ready"), sem("rot_step")
        scores_made, max_ready, exp_ready = sem("scores_made"), sem("max_ready"), sem("exp_ready")
        p_turned, pT_ready, pv_made, o_ready = sem("p_turned"), sem("pT_ready"), sem("pv_made"), sem("o_ready")
        o_turned, oT_ready, wo_made, mid_ready = sem("o_turned"), sem("oT_ready"), sem("wo_made"), sem("mid_ready")
        shift_made, h_made, gelu_ready, hT_ready, w2_made = sem("shift_made"), sem("h_made"), sem("gelu_ready"), sem("hT_ready"), sem("w2_made")
        steps, layer_done, cols_ready = sem("steps"), sem("layer_done"), sem("cols_ready")
        block = ctx.enter_context(nc.Block())
        QO, KO = 0, LD
        B2 = 2 * LD

        def h_tile(u, m):
            t = u % FT
            return c.bank(((3, 4), (5, 7))[u // FT][t // 4])[0:m, (t % 4) * S:(t % 4 + 1) * S]

        def h_signals(u):
            return 2 * (u // FT) + (u % FT) // 4 + 1

        def tile_rows(t):
            return P if t % FT < FT - 1 else FLAST

        @block.sync
        def _(sp):
            sp.dma_start(cols_all[:, :, :], c.loc["cols"]).then_inc(small_in, 16)
            sp.dma_start(rows_all[:, :, :].rearrange("s l n -> s (l n)"),
                         c.loc["rows"].rearrange("(o l) n -> o (l n)", o=1).broadcast_to((S, DEPTH * (2 * LD + D)))).then_inc(small_in, 16)
            sp.dma_start(rot_all[:, :, :], c.loc["rotary"]).then_inc(small_in, 16)

            def load_w(i, name, dst, src, free_sem, free_at):
                if not (isinstance(i, int) and i == 0):
                    sp.wait_ge(free_sem, free_at)
                sp.dma_start(dst, src).then_inc(w_in[name], 16)

            def body(i):
                def layer(w):
                    return w[bass.ds(i, 1)].rearrange("o r n -> (o r) n")
                load_w(i, "wqkv", wqkv[:, :, :], tiled(layer(c.loc["Wqkv"])), qkv_made, 6 * i)
                load_w(i, "wo", wo[:, :, :], tiled(layer(c.loc["Wo"])), wo_made, i)
                load_w(i, "w1", w1[:, :, :], tiled(layer(c.loc["W1"])), h_made, 4 * i)
                src = layer(c.loc["W2"])
                load_w(i, "w2", w2[:, 0:FT - 1, :], tiled(src[0:(FT - 1) * P, :]), w2_made, i)
                sp.dma_start(w2[0:FLAST, FT - 1, :], src[(FT - 1) * P:FF, :]).then_inc(w_in["w2"], 16)
            body(0)
            with sp.Fori(1, DEPTH) as i:
                body(i)
            sp.wait_ge(w_in["w2"], 32 * DEPTH)

        @block.gpsimd
        def _(pool):
            pool.memset(shift[:, :], 0.0).then_inc(mask_step, 1)
            pool.memset(mask[:, :], 0.0).then_inc(mask_step, 1)
            pool.wait_ge(mask_step, 2)
            pool.affine_select(out=shift[:, :], in_=shift[:, :], compare_op=ALU.not_equal, fill=1.0,
                               base=-1, pattern=[[1, S]], channel_multiplier=-1).then_inc(made_mask, 1)
            pool.affine_select(out=mask[:, :], in_=mask[:, :], compare_op=ALU.is_ge, fill=MASKED,
                               base=0, pattern=[[-1, S]], channel_multiplier=1).then_inc(made_mask, 1)
            pool.wait_ge(made_mask, 2)
            pool.affine_select(out=mask[:, :], in_=mask[:, :], compare_op=ALU.is_ge, fill=MASKED,
                               base=WINDOW, pattern=[[1, S]], channel_multiplier=-1).then_inc(made_mask, 1)
            pool.wait_ge(small_in, 48)

            def body(i):
                if not (isinstance(i, int) and i == 0):
                    pool.wait_ge(layer_done, i)
                pool.tensor_copy(cols[:, :], cols_all[:, bass.ds(i, 1), :].rearrange("p o n -> p (o n)")).then_inc(cols_ready, 1)
                pool.tensor_copy(rows[:, :], rows_all[:, bass.ds(i, 1), :].rearrange("p o n -> p (o n)")).then_inc(cols_ready, 1)
                pool.wait_ge(cols_ready, 2 * i + 2)
                H = LD // 2
                for j, off in enumerate((QO, KO)):
                    pool.tensor_tensor(rot[:, 2 * j, :], rot_all[:, 2 * j, :], rows[:, off:off + LD], ALU.mult).then_inc(rot_ready, 1)
                    pool.tensor_tensor(rot[:, 2 * j + 1, 0:H], rot_all[:, 2 * j + 1, 0:H], rows[:, off + H:off + LD], ALU.mult).then_inc(rot_ready, 1)
                    pool.tensor_tensor(rot[:, 2 * j + 1, H:LD], rot_all[:, 2 * j + 1, H:LD], rows[:, off:off + H], ALU.mult).then_inc(rot_ready, 1)
            body(0)
            with pool.Fori(1, DEPTH) as i:
                body(i)

        @block.tensor
        def _(pe):
            pe.wait_ge(made_mask, 3)

            def body(i):
                pe.wait_ge(y_ready, i + 1)
                for k in range(KT):
                    mm = pe.transpose(c.bank(4)[:, k * S:(k + 1) * S], y[:, k * P:(k + 1) * P], c.ident[:, :])
                mm.then_inc(y_turned, 1)
                pe.wait_ge(tT_ready, i + 1)
                pe.wait_ge(w_in["wqkv"], 16 * i + 16)
                for u, b in enumerate((0, 1, 2, 3, 6, 7)):
                    for k in range(KT):
                        mm = pe.matmul(c.bank(b), tT[:, k, :], wqkv[:, k, u * 512:(u + 1) * 512], start=(k == 0), stop=(k == KT - 1))
                    mm.then_inc(qkv_made, 1)
                for j in range(2):
                    pe.wait_ge(rotated, 2 * i + j + 1)
                    for t in range(LH // 2):
                        mm = pe.transpose(c.bank(2 * j + t // 4)[:, (t % 4) * S:(t % 4 + 1) * S],
                                          qk[j][:, 2 * t:2 * t + 2, :].rearrange("s h d -> s (h d)"), c.ident[:, :])
                    mm.then_inc(qk_turned, 1)
                pe.wait_ge(qkT_ready, 2 * i + 2)
                pe.wait_ge(v_kept, i + 1)
                for par in range(2):
                    for t in range(LH // 2):
                        lo = par * LD
                        mm = pe.matmul(c.bank(4 + 2 * par + t // 4)[:, (t % 4) * S:(t % 4 + 1) * S],
                                       qkT[0][lo:lo + LD, t, :], qkT[1][lo:lo + LD, t, :], start=True, stop=True)
                mm.then_inc(scores_made, 1)
                for hh in range(LH):
                    pe.wait_ge(exp_ready, LH * i + hh + 1)
                    mm = pe.transpose(c.bank(hh // 4)[:, (hh % 4) * S:(hh % 4 + 1) * S], sc[:, hh, :], c.ident[:, :])
                    if hh % 8 == 7:
                        mm.then_inc(p_turned, 1)
                for hh in range(LH):
                    if hh % 8 == 0:
                        pe.wait_ge(pT_ready, 2 * i + hh // 8 + 1)
                    h = 2 * (hh % 8) + hh // 8
                    mm = pe.matmul(c.bank(4 + h // 8)[:, (h % 8) * LD:(h % 8 + 1) * LD], pT[:, hh, :], v[:, h * LD:(h + 1) * LD], start=True, stop=True)
                mm.then_inc(pv_made, 1)
                pe.wait_ge(o_ready, i + 1)
                for t in range(INNER // P):
                    mm = pe.transpose(c.bank(6 + t // 4)[:, (t % 4) * S:(t % 4 + 1) * S],
                                      o[:, 2 * t:2 * t + 2, :].rearrange("s h d -> s (h d)"), c.ident[:, :])
                mm.then_inc(o_turned, 1)
                pe.wait_ge(oT_ready, i + 1)
                pe.wait_ge(w_in["wo"], 16 * i + 16)
                for t in range(INNER // P):
                    mm = pe.matmul(c.bank(0)[:, 0:D], oT[:, t, :], wo[:, t, :], start=(t == 0), stop=(t == INNER // P - 1))
                mm.then_inc(wo_made, 1)
                pe.wait_ge(mid_ready, i + 1)
                pe.matmul(c.bank(1)[:, 0:P], shift[:, :], y[:, P:D], start=True, stop=True).then_inc(shift_made, 1)
                norm.turn(pe, i, c.xn, c.bank(2))
                pe.wait_ge(norm.outT, i + 1)
                pe.wait_ge(w_in["w1"], 16 * i + 16)
                for u in range(2 * FT):
                    t = u % FT
                    w0 = t * P + (FF if u < FT else 0)
                    m = tile_rows(u)
                    for k in range(KT):
                        mm = pe.matmul(h_tile(u, m), w1[:, k, w0:w0 + m], c.xT[:, k, :],
                                       start=(k == 0), stop=(k == KT - 1))
                    if u % FT in (3, FT - 1):
                        mm.then_inc(h_made, 1)
                pe.wait_ge(hT_ready, i + 1)
                pe.wait_ge(w_in["w2"], 32 * i + 32)
                for t in range(FT):
                    m = tile_rows(t)
                    mm = pe.matmul(c.bank(6)[:, 0:D], hT[0:m, t, :], w2[0:m, t, :], start=(t == 0), stop=(t == FT - 1))
                mm.then_inc(w2_made, 1)
            body(0)
            with pe.Fori(1, DEPTH) as i:
                body(i)

        @block.scalar
        def _(act):
            norm0.scalar(act, 0)

            def body(i):
                for j in range(2):
                    act.wait_ge(qkv_made, 6 * i + 2 * j + 2)
                    act.activation(sq[:, j * INNER:(j + 1) * INNER].rearrange("s (b n) -> s b n", b=2), c.ps[:, 2 * j:2 * j + 2, :],
                                   ACT.Square).then_inc(squared, 1)
                act.wait_ge(normed, i + 1)
                act.activation(norms[:, :], norms[:, :], ACT.Sqrt).then_inc(rooted, 1)
                act.wait_ge(qkv_made, 6 * i + 6)
                act.copy(v[:, :].rearrange("s (b n) -> s b n", b=2), c.ps[:, 6:8, :]).then_inc(v_kept, 1)
                act.wait_ge(max_ready, i + 1)
                for hh in range(LH):
                    act.activation(sc[:, hh, :], sc[:, hh, :], ACT.Exp, bias=mx[:, hh:hh + 1], scale=QK_SCALE,
                                   accum_out=total[:, hh:hh + 1]).then_inc(exp_ready, 1)
                norm.scalar(act, i)
                for t in range(FT):
                    m = tile_rows(t)
                    act.wait_ge(h_made, 4 * i + h_signals(t))
                    act.activation(gate[0:m, t, :], h_tile(t, m), ACT.Gelu,
                                   bias=cols[0:m, 2 * KT + t:2 * KT + t + 1]).then_inc(gelu_ready, 1)
            body(0)
            with act.Fori(1, DEPTH) as i:
                body(i)

        @block.vector
        def _(dve):
            STEPS = 18
            first = Chain(dve, steps)
            first(dve.memset(tT[:, 1, 0:1], 0.0))
            dve.wait_ge(made_mask, 3)
            first(dve.memset(shifted[:, :], 0.0))
            norm0.vector(dve, 0, c.x[:, :], y[:, :])
            dve.wait_ge(norm0.out, 1)
            dve.sem_inc(y_ready, 1)

            def body(i):
                chain = Chain(dve, steps, STEPS * i + 2)
                dve.wait_ge(y_turned, i + 1)
                dve.tensor_copy(tT[:, 0, :], c.bank(4)[:, 0:S]).then_inc(steps, 1)
                chain.n += 1
                dve.tensor_copy(tT[:, 1, 1:S], c.bank(4)[:, S:2 * S - 1]).then_inc(tT_ready, 1)
                for j in range(2):
                    dve.wait_ge(squared, 2 * i + j + 1)
                    chain(dve.reduce_sum(norms[:, j * LH:(j + 1) * LH], sq[:, j * INNER:(j + 1) * INNER].rearrange("s (h d) -> s h d", d=LD), AX_X))
                dve.sem_inc(normed, 1)
                dve.wait_ge(rooted, i + 1)
                chain(dve.tensor_scalar(norms[:, :], norms[:, :], 1e-12, None, ALU.max))
                chain(dve.reciprocal(norms[:, :], norms[:, :]))
                dve.wait_ge(rot_ready, 6 * i + 6)
                H = LD // 2
                for j in range(2):
                    src = c.ps[:, 2 * j:2 * j + 2, :].rearrange("s b (h d) -> s (b h) d", d=LD)
                    chain(dve.tensor_tensor(qa[:, :, :], src, norms[:, j * LH:(j + 1) * LH].unsqueeze(2).broadcast_to((S, LH, LD)), ALU.mult))
                    dve.tensor_tensor(qb[:, :, 0:H], qa[:, :, H:LD], rot[:, 2 * j + 1, 0:H].unsqueeze(1).broadcast_to((S, LH, H)), ALU.mult)
                    chain(dve.tensor_tensor(qb[:, :, H:LD], qa[:, :, 0:H], rot[:, 2 * j + 1, H:LD].unsqueeze(1).broadcast_to((S, LH, H)), ALU.mult))
                    chain(dve.tensor_tensor(qa[:, :, :], qa[:, :, :], rot[:, 2 * j, :].unsqueeze(1).broadcast_to((S, LH, LD)), ALU.mult))
                    dve.tensor_tensor(qk[j][:, :, :], qa[:, :, :], qb[:, :, :], ALU.add).then_inc(rotated, 1)
                    dve.wait_ge(rotated, 2 * i + j + 1)
                for j in range(2):
                    dve.wait_ge(qk_turned, 2 * i + j + 1)
                    dve.tensor_copy(qkT[j][:, :, :], c.ps[:, 2 * j:2 * j + 2, :].rearrange("p b (t s) -> p (b t) s", s=S)).then_inc(qkT_ready, 1)
                dve.wait_ge(scores_made, i + 1)
                chain(dve.tensor_tensor(sc[:, :, :], c.ps[:, 4:8, :].rearrange("p b (t s) -> p (b t) s", s=S),
                                        mask[:, :].unsqueeze(1).broadcast_to((S, LH, S)), ALU.add))
                chain(dve.tensor_reduce(mx[:, :], sc[:, :, :], AX_X, ALU.max, negate=True))
                dve.tensor_scalar(mx[:, :], mx[:, :], QK_SCALE, None, ALU.mult).then_inc(max_ready, 1)
                for half in range(2):
                    dve.wait_ge(p_turned, 2 * i + half + 1)
                    dve.tensor_copy(pT[:, 8 * half:8 * half + 8, :], c.ps[:, 2 * half:2 * half + 2, :].rearrange("p b (t s) -> p (b t) s", s=S)).then_inc(pT_ready, 1)
                dve.wait_ge(exp_ready, LH * i + LH)
                chain(dve.reciprocal(inv[:, :, :], total[:, :].rearrange("s (a t) -> s t a", a=2)))
                dve.wait_ge(pv_made, i + 1)
                dve.tensor_tensor(o[:, :, :], c.ps[:, 4:6, :].rearrange("s b (h d) -> s (b h) d", d=LD),
                                  inv[:, :, :].rearrange("s t a -> s (t a)").unsqueeze(2).broadcast_to((S, LH, LD)), ALU.mult).then_inc(o_ready, 1)
                dve.wait_ge(o_turned, i + 1)
                dve.tensor_copy(oT[:, :, :], c.ps[:, 6:8, :].rearrange("p b (t s) -> p (b t) s", s=S)).then_inc(oT_ready, 1)
                dve.wait_ge(wo_made, i + 1)
                chain(dve.tensor_tensor(y[:, :], y[:, :], c.bank(0)[:, 0:D], ALU.add))
                dve.sem_inc(mid_ready, 1)
                dve.tensor_copy(shifted[:, 0:P], y[:, 0:P])
                dve.wait_ge(shift_made, i + 1)
                chain(dve.tensor_copy(shifted[:, P:D], c.bank(1)[:, 0:P]))
                norm.vector(dve, i, shifted[:, :], c.xn[:, :])
                dve.wait_ge(norm.turned, i + 1)
                for k in range(KT):
                    ins = dve.tensor_scalar(c.xT[:, k, :], c.bank(2)[:, k * S:(k + 1) * S], cols[:, k:k + 1], cols[:, KT + k:KT + k + 1], ALU.mult, ALU.add)
                    if k == KT - 1:
                        ins.then_inc(norm.outT, 1)
                for t in range(FT):
                    m = tile_rows(t)
                    u = FT + t
                    dve.wait_ge(h_made, 4 * i + h_signals(u))
                    dve.wait_ge(gelu_ready, FT * i + t + 1)
                    ins = dve.scalar_tensor_tensor(out=hT[0:m, t, :], in0=h_tile(u, m),
                                                   scalar=cols[0:m, 2 * KT + u:2 * KT + u + 1], in1=gate[0:m, t, :], op0=ALU.add, op1=ALU.mult)
                ins.then_inc(hT_ready, 1)
                chain(dve.tensor_tensor(y[:, :], y[:, :], rows[:, B2:B2 + D], ALU.add))
                dve.wait_ge(w2_made, i + 1)
                chain(dve.tensor_tensor(y[:, :], y[:, :], c.bank(6)[:, 0:D], ALU.add))
                dve.sem_inc(y_ready, 1)
                dve.sem_inc(layer_done, 1)
                assert chain.n == STEPS, chain.n
            body(0)
            with dve.Fori(1, DEPTH) as i:
                body(i)
            dve.tensor_tensor(c.x[:, :], c.x[:, :], y[:, :], ALU.add).then_inc(layer_done, 1)
            dve.wait_ge(layer_done, DEPTH + 1)



def lay_out_local(t):
    import numpy as _np
    b1 = _np.zeros((2, FT * P, DEPTH), t["b1"].dtype)
    b1[0, 0:FF] = t["b1"][:, FF:].T
    b1[1, 0:FF] = t["b1"][:, :FF].T
    cols = [t[n].reshape(DEPTH, KT, P).transpose(2, 0, 1) for n in ("ln_g", "ln_b")]
    cols.append(b1.reshape(2 * FT, P, DEPTH).transpose(1, 2, 0))
    return {"Wqkv": t["Wqkv"], "Wo": t["Wo"], "W1": t["W1"], "W2": t["W2"], "rotary": rotary_tables(),
            "cols": _np.concatenate(cols, 2), "rows": _np.concatenate([t["q_scale"], t["k_scale"], t["b2"]], 1)}


RH = 2
LEVELS = S.bit_length() - 1


def level_masks():
    import numpy as np
    i = np.arange(S)
    out = [((i[None, :] >> l) == (i[:, None] >> l) + 1) & (((i[None, :] >> l) & 1) == 1) for l in range(LEVELS)]
    out.append(np.eye(S, dtype=bool))
    return np.stack(out, 1).astype(np.float32)


def gated_recurrence(nc, c):
    with ExitStack() as ctx:
        def sb(nm, shape):
            return ctx.enter_context(nc.sbuf_tensor(f"rec_{nm}", shape, F32))

        def sem(nm):
            return c.sem(f"rec_{nm}")

        w = {n: sb(f"w{n}", [P, KT, D]) for n in "qkvo"}
        gates = sb("gates", [P, 4, RH])
        masks = sb("masks", [S, LEVELS + 1, S])
        qT, vT = sb("qT", [P, RH, S]), sb("vT", [P, RH, S])
        kn, kT = sb("kn", [S, D]), sb("kT", [P, RH, S])
        ksum, sq = sb("ksum", [S, RH]), sb("sq", [S, D])
        gamma, lam = sb("gamma", [P, RH, S]), sb("lam", [P, RH, S])
        decay = [sb(f"decay{l}", [P, RH * S]) for l in range(LEVELS)]
        wk = [sb(f"wk{l}", [P, RH * S]) for l in range(LEVELS)]
        am = sb("am", [S, RH, LEVELS + 1, S])
        wkN = [sb(f"wkN{l}", [S, RH, P]) for l in range(LEVELS)]
        yT, t = sb("yT", [P, RH, S]), sb("t", [P, RH, S])
        norm = Norm(c, "rec_norm")
        w_in, proj_made, qv_kept, squared = sem("w_in"), sem("proj_made"), sem("qv_kept"), sem("squared")
        rooted, kn_ready, k_turned, kT_ready = sem("rooted"), sem("kn_ready"), sem("k_turned"), sem("kT_ready")
        gated, steps, a_made = sem("gates_ready"), sem("steps"), sem("a_made")
        decay_ready, wk_step, wk_ready = sem("decay_ready"), sem("wk_step"), sem("wk_ready")
        wk_turned, wkN_ready, am_ready, level_made, level_used = sem("wk_turned"), sem("wkN_ready"), sem("am_ready"), sem("level_made"), sem("level_used")
        yT_ready, out_made = sem("yT_ready"), sem("out_made")
        block = ctx.enter_context(nc.Block())

        def pair(ap, l):
            return ap.rearrange("p (b a r) -> p b a r", a=2, r=1 << l)

        @block.sync
        def _(sp):
            for n in "kqvo":
                sp.dma_start(w[n][:, :, :], c.rec[f"W{n}"]).then_inc(w_in, 16)
            sp.dma_start(gates[:, :, :], c.rec["gates"]).then_inc(w_in, 16)
            sp.dma_start(masks[:, :, :], c.rec["masks"]).then_inc(w_in, 16)
            sp.wait_ge(w_in, 96)

        @block.tensor
        def _(pe):
            norm.turn(pe, 0, c.xn, c.bank(4))
            pe.wait_ge(norm.outT, 1)
            pe.wait_ge(w_in, 96)
            for k in range(KT):
                mm = pe.matmul(c.bank(0)[:, 0:D], c.xT[:, k, :], w["k"][:, k, :], start=(k == 0), stop=(k == KT - 1))
            mm.then_inc(proj_made, 1)
            for i, n in enumerate("qv"):
                for h in range(RH):
                    for k in range(KT):
                        mm = pe.matmul(c.bank(1 + i)[:, h * S:(h + 1) * S], w[n][:, k, h * P:(h + 1) * P], c.xT[:, k, :],
                                       start=(k == 0), stop=(k == KT - 1))
                mm.then_inc(proj_made, 1)
            pe.wait_ge(qv_kept, 2)
            for h in range(RH):
                mm = pe.matmul(c.bank(3)[:, h * S:(h + 1) * S], vT[:, h, :], qT[:, h, :], start=True, stop=True)
            mm.then_inc(a_made, 1)
            pe.wait_ge(kn_ready, RH)
            for h in range(RH):
                mm = pe.transpose(c.bank(4)[:, h * S:(h + 1) * S], kn[:, h * P:(h + 1) * P], c.ident[:, :])
            mm.then_inc(k_turned, 1)

            def turn(l):
                pe.wait_ge(wk_ready, l + 1)
                if l >= 2:
                    pe.wait_ge(wkN_ready, l - 1)
                for h in range(RH):
                    mm = pe.transpose(c.bank(l % 2)[:, h * P:(h + 1) * P], wk[l][:, h * S:(h + 1) * S], c.ident[:, :])
                mm.then_inc(wk_turned, 1)

            def level(n, l, j):
                if l == 0:
                    pe.wait_ge(am_ready, RH)
                pe.wait_ge(wkN_ready, l + 1)
                if n >= 2:
                    pe.wait_ge(level_used, n - 1)
                for h in range(RH):
                    mm = pe.matmul(c.bank(6 + n % 2)[:, h * S:(h + 1) * S], wkN[l][:, h, :], am[:, h, j, :], start=True, stop=True)
                mm.then_inc(level_made, 1)

            turn(0)
            turn(1)
            level(0, 0, LEVELS)
            for l in range(LEVELS):
                if l + 2 < LEVELS:
                    turn(l + 2)
                level(l + 1, l, l)
            pe.wait_ge(yT_ready, 1)
            for k in range(KT):
                mm = pe.matmul(c.bank(5)[:, 0:D], yT[:, k, :], w["o"][:, k, :], start=(k == 0), stop=(k == KT - 1))
            mm.then_inc(out_made, 1)

        @block.scalar
        def _(act):
            norm.scalar(act, 0)
            act.wait_ge(proj_made, 1)
            for h in range(RH):
                act.activation(sq[:, h * P:(h + 1) * P], c.bank(0)[:, h * P:(h + 1) * P], ACT.Square, accum_out=ksum[:, h:h + 1]).then_inc(squared, 1)
            act.wait_ge(squared, RH)
            act.activation(ksum[:, :], ksum[:, :], ACT.Sqrt).then_inc(rooted, 1)
            act.wait_ge(w_in, 96)
            act.wait_ge(kT_ready, 1)
            for h in range(RH):
                act.activation(gamma[:, h, :], kT[:, h, :], ACT.Sigmoid, bias=gates[:, 1, h:h + 1], scale=gates[:, 0, h:h + 1]).then_inc(gated, 1)
                act.activation(lam[:, h, :], kT[:, h, :], ACT.Sigmoid, bias=gates[:, 3, h:h + 1], scale=gates[:, 2, h:h + 1]).then_inc(gated, 1)
            for l in range(LEVELS):
                act.wait_ge(wk_turned, l + 1)
                act.copy(wkN[l][:, :, :].rearrange("s h k -> s (h k)"), c.bank(l % 2)[:, 0:RH * P]).then_inc(wkN_ready, 1)

        @block.gpsimd
        def _(pool):
            for l in range(1, LEVELS):
                pool.wait_ge(decay_ready, l)
                pool.wait_ge(wk_ready, l)
                old, new, d = pair(wk[l - 1][:, :], l - 1), pair(wk[l][:, :], l - 1), pair(decay[l - 1][:, :], l - 1)
                r = 1 << (l - 1)
                pool.tensor_copy(new[:, :, 1, :], old[:, :, 1, :]).then_inc(wk_step, 1)
                pool.wait_ge(wk_step, l)
                pool.tensor_tensor(new[:, :, 0, :], old[:, :, 0, :], d[:, :, 1, r - 1:r].broadcast_to((P, S // r, r)), ALU.mult).then_inc(wk_ready, 1)

        @block.vector
        def _(dve):
            chain = Chain(dve, steps)
            norm.vector(dve, 0, c.x[:, :], c.xn[:, :])
            norm.keep(dve, 0, c.bank(4), c.xT[:, :, :])
            dve.wait_ge(rooted, 1)
            chain(dve.tensor_scalar(ksum[:, :], ksum[:, :], 1e-12, None, ALU.max))
            chain(dve.reciprocal(ksum[:, :], ksum[:, :]))
            for h in range(RH):
                dve.tensor_scalar(kn[:, h * P:(h + 1) * P], c.bank(0)[:, h * P:(h + 1) * P], ksum[:, h:h + 1], None, ALU.mult).then_inc(kn_ready, 1)
            for i, dst in enumerate((qT, vT)):
                dve.wait_ge(proj_made, 2 + i)
                dve.tensor_copy(dst[:, :, :].rearrange("p h s -> p (h s)"), c.bank(1 + i)[:, 0:RH * S]).then_inc(qv_kept, 1)
            dve.wait_ge(k_turned, 1)
            dve.tensor_copy(kT[:, :, :].rearrange("p h s -> p (h s)"), c.bank(4)[:, 0:RH * S]).then_inc(kT_ready, 1)
            dve.wait_ge(a_made, 1)
            for h in range(RH):
                dve.tensor_tensor(am[:, h, :, :], c.bank(3)[:, h * S:(h + 1) * S].unsqueeze(1).broadcast_to((S, LEVELS + 1, S)), masks[:, :, :], ALU.mult).then_inc(am_ready, 1)
            dve.wait_ge(gated, 2 * RH)
            flat = [g[:, :, :].rearrange("p h s -> p (h s)") for g in (gamma, lam, kT)]
            chain(dve.tensor_scalar(flat[1], flat[1], -1.0, 1.0, ALU.mult, ALU.add))
            dve.tensor_tensor(decay[0][:, :], flat[1], flat[0], ALU.mult).then_inc(decay_ready, 1)
            dve.wait_ge(decay_ready, 1)
            chain(dve.tensor_scalar(flat[0], decay[0][:, :], -1.0, 1.0, ALU.mult, ALU.add))
            dve.tensor_tensor(wk[0][:, :], flat[0], flat[2], ALU.mult).then_inc(wk_ready, 1)
            for l in range(1, LEVELS):
                old, new = pair(decay[l - 1][:, :], l - 1), pair(decay[l][:, :], l - 1)
                r = 1 << (l - 1)
                dve.tensor_copy(new[:, :, 0, :], old[:, :, 0, :])
                dve.tensor_tensor(new[:, :, 1, :], old[:, :, 1, :], old[:, :, 0, r - 1:r].broadcast_to((P, S // r, r)), ALU.mult).then_inc(decay_ready, 1)
                dve.wait_ge(decay_ready, l + 1)
            dve.wait_ge(level_made, 1)
            y = yT[:, :, :].rearrange("p h s -> p (h s)")
            tf = t[:, :, :].rearrange("p h s -> p (h s)")
            dve.tensor_copy(y, c.bank(6)[:, 0:RH * S]).then_inc(level_used, 1)
            for l in range(LEVELS):
                dve.wait_ge(level_made, l + 2)
                dve.tensor_tensor(tf, c.bank(6 + (l + 1) % 2)[:, 0:RH * S], decay[l][:, :], ALU.mult).then_inc(level_used, 1)
                dve.wait_ge(level_used, l + 2)
                ins = dve.tensor_tensor(y, y, tf, ALU.add)
                if l < LEVELS - 1:
                    chain(ins)
            ins.then_inc(yT_ready, 1)
            dve.wait_ge(out_made, 1)
            chain(dve.tensor_tensor(c.x[:, :], c.x[:, :], c.bank(5)[:, 0:D], ALU.add))



def lay_out_recurrence(t):
    import numpy as _np
    return {**{f"W{n}": t[f"W{n}"].T for n in "qkvo"}, "masks": level_masks(),
            "gates": _np.stack([t[n].T for n in ("W_gamma", "b_gamma", "W_lambda", "b_lambda")], 1)}


NE = 8
EF = 1024
ET = EF // P
TOP = 2


def experts(nc, c):
    with ExitStack() as ctx:
        def sb(nm, shape):
            return ctx.enter_context(nc.sbuf_tensor(f"moe_{nm}", shape, F32))

        def sem(nm):
            return c.sem(f"moe_{nm}")

        gw, b2 = sb("gate_w", [P, KT, NE]), sb("b2", [NE, D])
        w1 = [sb(f"w1_{i}", [P, KT, EF]) for i in range(2)]
        w2 = [sb(f"w2_{i}", [P, ET, D]) for i in range(2)]
        b1 = [sb(f"b1_{i}", [P, ET]) for i in range(2)]
        hT = [sb(f"hT{i}", [P, ET, S]) for i in range(2)]
        earlier = sb("earlier", [S, NE, NE])
        logit, ex = sb("logit", [S, NE]), sb("ex", [S, NE])
        beats, ties = sb("beats", [S, NE, NE]), sb("ties", [S, NE, NE])
        rank, neg_max, total = sb("rank", [S, NE]), sb("neg_max", [S, 1]), sb("total", [S, 1])
        combine, combT = sb("combine", [S, NE]), sb("combT", [NE, S])
        share = [sb(f"share{i}", [S, 1]) for i in range(2)]
        norm = Norm(c, "moe_norm")
        small_in, filled, earlier_made = sem("small_in"), sem("filled"), sem("earlier_made")
        up_in, down_in = [sem(f"up_in{i}") for i in range(2)], [sem(f"down_in{i}") for i in range(2)]
        logits_made, max_ready, ex_ready, steps = sem("logits_made"), sem("max_ready"), sem("ex_ready"), sem("steps")
        combine_ready, comb_turned, combT_ready, bias_made = sem("combine_ready"), sem("comb_turned"), sem("combT_ready"), sem("bias_made")
        up_made, h_ready, down_made, added, shared = sem("up_made"), sem("h_ready"), sem("down_made"), sem("added"), sem("shared")
        block = ctx.enter_context(nc.Block())

        @block.sync
        def _(sp):
            sp.dma_start(gw[:, :, :], c.moe["gate_w"]).then_inc(small_in, 16)
            sp.dma_start(b2[:, :], c.moe["b2"]).then_inc(small_in, 16)

            def load(e, par):
                def one(w):
                    return w[bass.ds(e, 1)].rearrange("o r n -> (o r) n")
                first = isinstance(e, int) and e < 2
                if not first:
                    sp.wait_ge(h_ready, ET * (e - 1))
                sp.dma_start(w1[par][:, :, :], tiled(one(c.moe["W1"]))).then_inc(up_in[par], 16)
                sp.dma_start(b1[par][:, :], one(c.moe["b1"])).then_inc(up_in[par], 16)
                if not first:
                    sp.wait_ge(down_made, e - 1)
                sp.dma_start(w2[par][:, :, :], tiled(one(c.moe["W2"]))).then_inc(down_in[par], 16)
            for par in range(2):
                load(par, par)
            with sp.Fori(1, NE // 2) as i:
                for par in range(2):
                    load(2 * i + par, par)

        @block.gpsimd
        def _(pool):
            pool.memset(earlier[:, :, :], 1.0).then_inc(filled, 1)
            pool.wait_ge(filled, 1)
            pool.affine_select(out=earlier[:, :, :], in_=earlier[:, :, :], compare_op=ALU.is_gt, fill=0.0,
                               base=0, pattern=[[1, NE], [-1, NE]], channel_multiplier=0).then_inc(earlier_made, 1)

        @block.tensor
        def _(pe):
            norm.turn(pe, 0, c.xn, c.bank(4))
            pe.wait_ge(norm.outT, 1)
            pe.wait_ge(small_in, 32)
            for k in range(KT):
                mm = pe.matmul(c.bank(6)[:, 0:NE], c.xT[:, k, :], gw[:, k, :], start=(k == 0), stop=(k == KT - 1))
            mm.then_inc(logits_made, 1)

            def up(e, par, i):
                pe.wait_ge(up_in[par], 32 * i + 32)
                if not (isinstance(e, int) and e < 2):
                    pe.wait_ge(h_ready, ET * (e - 1))
                for t in range(ET):
                    for k in range(KT):
                        mm = pe.matmul(c.bank(2 * par + t // 4)[:, (t % 4) * S:(t % 4 + 1) * S], w1[par][:, k, t * P:(t + 1) * P], c.xT[:, k, :],
                                       start=(k == 0), stop=(k == KT - 1))
                    if t % 4 == 3:
                        mm.then_inc(up_made, 1)

            def down(e, par, i):
                pe.wait_ge(down_in[par], 16 * i + 16)
                if not (isinstance(e, int) and e < 2):
                    pe.wait_ge(added, e - 1)
                for t in range(ET):
                    pe.wait_ge(h_ready, ET * e + t + 1)
                    mm = pe.matmul(c.bank(4 + par)[:, 0:D], hT[par][:, t, :], w2[par][:, t, :], start=(t == 0), stop=(t == ET - 1))
                mm.then_inc(down_made, 1)

            up(0, 0, 0)
            pe.wait_ge(combine_ready, 1)
            pe.transpose(c.bank(7)[0:NE, 0:S], combine[:, :], c.ident[:, :]).then_inc(comb_turned, 1)
            pe.wait_ge(combT_ready, 1)
            pe.matmul(c.bank(6)[:, D:2 * D], combT[:, :], b2[:, :], start=True, stop=True).then_inc(bias_made, 1)

            def body(i):
                for par in range(2):
                    e = 2 * i + par
                    if not (isinstance(e, int) and e == NE - 1):
                        up(e + 1, 1 - par, i + par)
                    down(e, par, i)
            body(0)
            with pe.Fori(1, NE // 2 - 1) as i:
                body(i)
            body(NE // 2 - 1)

        @block.scalar
        def _(act):
            norm.scalar(act, 0)
            act.wait_ge(max_ready, 1)
            act.activation(ex[:, :], logit[:, :], ACT.Exp, bias=neg_max[:, 0:1]).then_inc(ex_ready, 1)

            def body(i):
                for par in range(2):
                    e = 2 * i + par
                    act.wait_ge(up_in[par], 32 * i + 32)
                    if not (isinstance(e, int) and e < 2):
                        act.wait_ge(down_made, e - 1)
                    for t in range(ET):
                        act.wait_ge(up_made, 2 * e + t // 4 + 1)
                        act.activation(hT[par][:, t, :], c.bank(2 * par + t // 4)[:, (t % 4) * S:(t % 4 + 1) * S], ACT.Gelu,
                                       bias=b1[par][:, t:t + 1]).then_inc(h_ready, 1)
            body(0)
            with act.Fori(1, NE // 2) as i:
                body(i)

        @block.vector
        def _(dve):
            chain = Chain(dve, steps)
            norm.vector(dve, 0, c.x[:, :], c.xn[:, :])
            norm.keep(dve, 0, c.bank(4), c.xT[:, :, :])
            dve.wait_ge(logits_made, 1)
            chain(dve.tensor_copy(logit[:, :], c.bank(6)[:, 0:NE]))
            dve.tensor_reduce(neg_max[:, :], logit[:, :], AX_X, ALU.max, negate=True).then_inc(max_ready, 1)
            other = logit[:, :].unsqueeze(1).broadcast_to((S, NE, NE))
            own = logit[:, :].unsqueeze(2).broadcast_to((S, NE, NE))
            chain(dve.tensor_tensor(beats[:, :, :], other, own, ALU.is_gt))
            chain(dve.tensor_tensor(ties[:, :, :], other, own, ALU.is_equal))
            dve.wait_ge(earlier_made, 1)
            chain(dve.tensor_tensor(ties[:, :, :], ties[:, :, :], earlier[:, :, :], ALU.mult))
            chain(dve.tensor_tensor(beats[:, :, :], beats[:, :, :], ties[:, :, :], ALU.add))
            chain(dve.reduce_sum(rank[:, :], beats[:, :, :], AX_X))
            chain(dve.tensor_scalar(rank[:, :], rank[:, :], float(TOP), None, ALU.is_lt))
            dve.wait_ge(ex_ready, 1)
            chain(dve.tensor_tensor(combine[:, :], ex[:, :], rank[:, :], ALU.mult))
            chain(dve.reduce_sum(total[:, :], combine[:, :], AX_X))
            chain(dve.reciprocal(total[:, :], total[:, :]))
            dve.tensor_scalar(combine[:, :], combine[:, :], total[:, 0:1], None, ALU.mult).then_inc(combine_ready, 1)
            dve.wait_ge(comb_turned, 1)
            dve.tensor_copy(combT[:, :], c.bank(7)[0:NE, 0:S]).then_inc(combT_ready, 1)
            dve.wait_ge(bias_made, 1)
            chain(dve.tensor_tensor(c.x[:, :], c.x[:, :], c.bank(6)[:, D:2 * D], ALU.add))

            def body(i):
                for par in range(2):
                    e = 2 * i + par
                    if not (isinstance(e, int) and e == 0):
                        dve.wait_ge(added, e)
                    dve.tensor_copy(share[par][:, :], combine[:, bass.ds(e, 1)]).then_inc(shared, 1)
                    dve.wait_ge(shared, e + 1)
                    dve.wait_ge(down_made, e + 1)
                    dve.scalar_tensor_tensor(out=c.x[:, :], in0=c.bank(4 + par)[:, 0:D], scalar=share[par][:, 0:1], in1=c.x[:, :],
                                             op0=ALU.mult, op1=ALU.add).then_inc(added, 1)
            body(0)
            with dve.Fori(1, NE // 2) as i:
                body(i)
            dve.wait_ge(added, NE)



def lay_out_experts(t):
    return {"gate_w": t["gate_w"], "W1": t["W1"], "b1": t["b1"].reshape(NE, ET, P).transpose(0, 2, 1), "W2": t["W2"], "b2": t["b2"]}


CF = 1024
CT = CF // P


def biased_feed_forward(nc, c):
    with ExitStack() as ctx:
        def sb(nm, shape):
            return ctx.enter_context(nc.sbuf_tensor(f"cff_{nm}", shape, F32))

        def sem(nm):
            return c.sem(f"cff_{nm}")

        w1, w2 = sb("w1", [P, KT, CF]), sb("w2", [P, CT, D])
        cols, rows = sb("cols", [P, 2 * KT + CT]), sb("rows", [S, 3, D])
        hT = sb("hT", [P, CT, S])
        norm = Norm(c, "cff_norm")
        w_in, up_made, h_ready, down_made, steps = sem("w_in"), sem("up_made"), sem("h_ready"), sem("down_made"), sem("steps")
        block = ctx.enter_context(nc.Block())

        @block.sync
        def _(sp):
            sp.dma_start(cols[:, :], c.cff["cols"]).then_inc(w_in, 16)
            sp.dma_start(rows[:, :, :].rearrange("s l n -> s (l n)"),
                         c.cff["rows"].rearrange("(o l) n -> o (l n)", o=1).broadcast_to((S, 3 * D))).then_inc(w_in, 16)
            sp.dma_start(w1[:, :, :], c.cff["W1"]).then_inc(w_in, 16)
            sp.dma_start(w2[:, :, :], c.cff["W2"]).then_inc(w_in, 16)

        @block.tensor
        def _(pe):
            norm.turn(pe, 0, c.xn, c.bank(4))
            pe.wait_ge(norm.outT, 1)
            pe.wait_ge(w_in, 64)
            for t in range(CT):
                for k in range(KT):
                    mm = pe.matmul(c.bank(t // 4)[:, (t % 4) * S:(t % 4 + 1) * S], w1[:, k, t * P:(t + 1) * P], c.xT[:, k, :],
                                   start=(k == 0), stop=(k == KT - 1))
                if t % 4 == 3:
                    mm.then_inc(up_made, 1)
            for t in range(CT):
                pe.wait_ge(h_ready, t + 1)
                mm = pe.matmul(c.bank(5)[:, 0:D], hT[:, t, :], w2[:, t, :], start=(t == 0), stop=(t == CT - 1))
            mm.then_inc(down_made, 1)

        @block.scalar
        def _(act):
            norm.scalar(act, 0)
            act.wait_ge(w_in, 64)
            for t in range(CT):
                act.wait_ge(up_made, t // 4 + 1)
                act.activation(hT[:, t, :], c.bank(t // 4)[:, (t % 4) * S:(t % 4 + 1) * S], ACT.Gelu,
                               bias=cols[:, 2 * KT + t:2 * KT + t + 1]).then_inc(h_ready, 1)
            norm.scalar(act, 1)

        @block.vector
        def _(dve):
            chain = Chain(dve, steps)
            norm.vector(dve, 0, c.z[:, :], c.xn[:, :])
            dve.wait_ge(w_in, 64)
            dve.wait_ge(norm.turned, 1)
            for k in range(KT):
                ins = dve.tensor_scalar(c.xT[:, k, :], c.bank(4)[:, k * S:(k + 1) * S], cols[:, k:k + 1], cols[:, KT + k:KT + k + 1], ALU.mult, ALU.add)
            ins.then_inc(norm.outT, 1)
            chain(dve.tensor_tensor(c.z[:, :], c.z[:, :], rows[:, 0, :], ALU.add))
            dve.wait_ge(down_made, 1)
            chain(dve.tensor_tensor(c.z[:, :], c.z[:, :], c.bank(5)[:, 0:D], ALU.add))
            norm.vector(dve, 1, c.z[:, :], c.xn[:, :])
            dve.wait_ge(norm.out, 2)
            chain(dve.tensor_tensor(c.xn[:, :], c.xn[:, :], rows[:, 1, :], ALU.mult))
            chain(dve.tensor_tensor(c.xn[:, :], c.xn[:, :], rows[:, 2, :], ALU.add))
            chain(dve.tensor_tensor(c.x[:, :], c.x[:, :], c.xn[:, :], ALU.add))


def program(nc, a, out):
    with ExitStack() as ctx:
        c = Core(nc, ctx)
        c.x_dram, c.ctxT = a["x"], a["ctxT"]
        c.T = c.ctxT.shape[1]
        c.z = c.sb("z_rows", [S, D])
        c.wkA, c.wkD, c.wvA, c.wvD = (tiled(a[k]) for k in ("wkA", "wkD", "wvA", "wvD"))
        c.k1_dram = nc.dram_tensor("keys1_scratch", (1, P, c.T), F32).ap()
        c.k2_dram = nc.dram_tensor("keys2_scratch", (NH // KG, P, c.T), F32).ap()
        c.v_dram = nc.dram_tensor("values_scratch", (NKV + NH, P, c.T // P, SPLIT * HD), F32).ap()

        def part(prefix, matrices):
            return {k[len(prefix):]: (tiled(v) if k[len(prefix):] in matrices else v) for k, v in a.items() if k.startswith(prefix)}

        c.rel = part("rel_", ("W_q", "W_k", "W_v", "W_o"))
        c.loc = part("loc_", ())
        c.cff = part("cff_", ("W1", "W2"))
        c.rec = part("rec_", ("Wq", "Wk", "Wv", "Wo"))
        c.moe = part("moe_", ("gate_w",))

        def cross(name, wq, groups, v_dram, heads_per_v, bias, keys_dram, wo, base, dst):
            with ExitStack() as mem:
                c.qm = mem.enter_context(nc.sbuf_tensor(f"{name}_queries", [P, NH, SPLIT, S], F32R))
                c.attn = mem.enter_context(nc.sbuf_tensor(f"{name}_attn", [S, D], F32))
                c.scores = [mem.enter_context(nc.sbuf_tensor(f"{name}_scores{i}", [P, c.T], F32)) for i in range(2)]
                c.run(queries, name, wq, groups)
                c.run(attention, name, v_dram, heads_per_v, bias, keys_dram)
                c.run(project_out, name, wo, base, dst)

        c.run(consts)
        c.run(context_products)
        cross("gqa", tiled(a["wqA"]), True, c.v_dram[0:NKV], GRP, None, c.k1_dram, tiled(a["woA"]), c.x, c.x)
        c.run(relative_attention)
        c.run(local_transformer)
        cross("biased", tiled(a["wqD"]), False, c.v_dram[NKV:], 1, a["bias"], c.k2_dram, tiled(a["woD"]), c.xn, c.z)
        c.run(biased_feed_forward)
        c.run(gated_recurrence)
        c.run(experts)
        c.run(store_x, out)


def lay_out(i):
    import numpy as _np
    t = {k: _np.asarray(v) for k, v in i.items()}

    def twice(w):
        return _np.repeat(w.reshape(D, NH // KG, 1, KR), 2, axis=2).reshape(D, 2 * D)

    def part(prefix):
        return {k[len(prefix):]: v for k, v in t.items() if k.startswith(prefix)}

    gqa, rel, bia = part("L0_xattn_"), part("L0_attn_"), part("L1_xattn_")
    out = {
        "x": t["x"][0], "ctxT": t["ctx_1024"][0].T, "bias": t["fside_Bx16xSxS2_0"][0],
        "wqA": twice(gqa["Wq"].reshape(NKV, GRP, HD, D).transpose(3, 1, 0, 2).reshape(D, D)),
        "wkA": gqa["Wk"].T, "wvA": gqa["Wv"].T, "woA": gqa["Wo"].T,
        "wqD": twice(bia["Wq"].T), "wkD": bia["Wk"].T, "wvD": bia["Wv"].T, "woD": bia["Wo"].T,
    }
    for n in "qk":
        rel[f"b_{n}"] = rel[f"b_{n}"].reshape(KT, P).T
    rel["rel_kT"] = rel.pop("rel_k_table").T
    cff = {"W1": bia["W1"].T, "W2": bia["W2"].T, "rows": _np.stack([bia["b2"], bia["g2"], bia["be2"]]),
           "cols": _np.concatenate([bia["g1"].reshape(KT, P).T, bia["be1"].reshape(KT, P).T, bia["b1"].reshape(CT, P).T], 1)}
    parts = {"rel_": rel, "loc_": lay_out_local(part("L0_ffn_")), "cff_": cff,
             "rec_": lay_out_recurrence(part("L1_attn_")), "moe_": lay_out_experts(part("L1_ffn_"))}
    for prefix, p in parts.items():
        out.update({prefix + k: v for k, v in p.items()})
    return out


def kernel(**inputs):
    import numpy as _np
    import concourse.bacc as _bacc
    from concourse import mybir as _mybir
    from concourse.bass_utils import run_bass_kernel_spmd as _run

    nc = _bacc.Bacc("TRN2", target_bir_lowering=False, num_devices=1)
    arrays, aps = {}, {}
    for name, a in lay_out(inputs).items():
        a = _np.ascontiguousarray(a)
        arrays[f"in_{name}"] = a
        aps[name] = nc.dram_tensor(f"in_{name}", a.shape, _mybir.dt.from_np(a.dtype), kind="ExternalInput").ap()
    out = nc.dram_tensor("out_x", (1, S, D), F32, kind="ExternalOutput").ap()
    program(nc, aps, out)
    r = _run(nc, [arrays], core_ids=[0])
    return r.results[0]["out_x"]
```

```python
from contextlib import ExitStack

import concourse.bass as bass
from concourse import mybir

F32 = mybir.dt.float32
F32R = mybir.dt.float32r
ALU = mybir.AluOpType
ACT = mybir.ActivationFunctionType
AX_X = mybir.AxisListType.X

P = 128
S = 128
D = 256
KT = D // P
NH = 16
HD = D // NH
NKV = 4
GRP = NH // NKV
KVA = NKV * HD
BLK = 7
CH = BLK * P
HC = CH // 2
PA = 4
LOWEST = -3.0e38
HPT = P // HD
KG = 2
KR = KG * HD
KREP = 3
KP = KREP * KR
SPLIT = 2
LN_EPS = 1e-5


class Core:

    def __init__(self, nc, ctx):
        self.nc, self.ctx, self.sems = nc, ctx, []
        self.ps = self.psum("banks", [P, 8, 512])
        self.sc = [self.ps[:, 2 * i:2 * i + 2, :] for i in range(2)]
        self.single = [self.ps[:, 4 + i, :] for i in range(4)]

    def sb(self, name, shape, dt=F32):
        return self.ctx.enter_context(self.nc.sbuf_tensor(name, shape, dt))

    def psum(self, name, shape, dt=F32):
        return self.ctx.enter_context(self.nc.psum_tensor(name, shape, dt))

    def sem(self, name):
        self.sems.append(self.nc.alloc_semaphore(name))
        return self.sems[-1]

    def run(self, stage, *args):
        stage(self.nc, self, *args)
        self.nc.clear_and_free_semaphores(self.sems)
        self.nc.all_engine_barrier()
        self.sems = []

    def bank(self, i):
        return self.ps[:, i, :]


class Chain:

    def __init__(self, eng, sem, base=0):
        self.eng, self.sem, self.base, self.n = eng, sem, base, 0

    def __call__(self, ins):
        ins.then_inc(self.sem, 1)
        self.n += 1
        self.eng.wait_ge(self.sem, self.base + self.n)


def consts(nc, c):
    c.ident = c.sb("ident", [P, P])
    c.headmask = c.sb("headmask", [P, HPT])
    c.keymask = c.sb("keymask", [P, SPLIT, KG])
    c.fold = c.sb("fold", [SPLIT * HD, HD])
    c.eps = c.sb("eps", [P, 1])
    c.ones = c.sb("ones", [P, HD])
    c.x = c.sb("x_rows", [S, D])
    c.xn = c.sb("x_normed", [S, D])
    c.xT = c.sb("x_normedT", [P, KT, S])
    c.gate, c.gates = c.sb("gate", [S, 16]), 0
    c.stats = c.sb("ln_stats", [S, 6])
    c.mv = c.sb("ln_mean_var", [S, 2])
    c.std = c.sb("ln_std", [S, 1])
    c.rstd = c.sb("ln_rstd", [S, 1])
    filled, selected, loaded = c.sem("const_filled"), c.sem("const_selected"), c.sem("x_loaded")
    folded = c.sem("fold_made")
    with nc.Block() as block:
        @block.sync
        def _(sp):
            sp.dma_start(c.x[:, :], c.x_dram).then_inc(loaded, 16)
            sp.wait_ge(loaded, 16)

        @block.gpsimd
        def _(pool):
            pool.memset(c.ident[:, :], 0.0).then_inc(filled, 1)
            pool.memset(c.headmask[:, :], 1.0).then_inc(filled, 1)
            pool.memset(c.eps[:, :], LN_EPS).then_inc(filled, 1)
            pool.memset(c.fold[:, :], 0.0).then_inc(filled, 1)
            pool.memset(c.ones[:, :], 1.0).then_inc(filled, 1)
            pool.wait_ge(filled, 5)
            for part in range(SPLIT):
                pool.affine_select(out=c.fold[:, :], in_=c.fold[:, :], compare_op=ALU.not_equal, fill=1.0,
                                   base=-HD * part, pattern=[[-1, HD]], channel_multiplier=1).then_inc(folded, 1)
                pool.wait_ge(folded, part + 1)
            pool.affine_select(out=c.ident[:, :], in_=c.ident[:, :], compare_op=ALU.not_equal, fill=1.0,
                               base=0, pattern=[[-1, P]], channel_multiplier=1).then_inc(selected, 1)
            pool.affine_select(out=c.headmask[:, :], in_=c.headmask[:, :], compare_op=ALU.is_ge, fill=0.0,
                               base=0, pattern=[[-HD, HPT]], channel_multiplier=1).then_inc(selected, 1)
            pool.wait_ge(selected, 2)
            pool.affine_select(out=c.headmask[:, :], in_=c.headmask[:, :], compare_op=ALU.is_ge, fill=0.0,
                               base=HD - 1, pattern=[[HD, HPT]], channel_multiplier=-1).then_inc(selected, 1)
            pool.wait_ge(selected, 3)
            pool.tensor_tensor(c.keymask[:, 0, :], c.headmask[:, 0:KG], c.headmask[:, KG:2 * KG], ALU.add).then_inc(selected, 1)
            pool.tensor_copy(c.keymask[:, 1, :], c.headmask[:, 2 * KG:3 * KG]).then_inc(selected, 1)
            pool.wait_ge(selected, 5)


class Norm:

    def __init__(self, c, name):
        self.c = c
        self.gate = c.gate[:, c.gates:c.gates + 1]
        c.gates += 1
        self.gated = c.sem(f"{name}_gated")
        self.stats = c.sem(f"{name}_stats")
        self.var = c.sem(f"{name}_var")
        self.std = c.sem(f"{name}_std")
        self.rstd = c.sem(f"{name}_rstd")
        self.out = c.sem(f"{name}_out")
        self.turned = c.sem(f"{name}_turned")
        self.outT = c.sem(f"{name}_outT")

    def vector(self, dve, n, x, out):
        c = self.c
        dve.bn_stats(c.stats[:, :], x).then_inc(self.stats, 1)
        dve.wait_ge(self.stats, n + 1)
        if not (isinstance(n, int) and n == 0):
            dve.wait_ge(self.gated, n)
        dve.memset(self.gate, 0.0).then_inc(self.gated, 1)
        dve.bn_aggr(c.mv[:, :], c.stats[:, :]).then_inc(self.var, 1)
        dve.wait_ge(self.std, n + 1)
        dve.reciprocal(c.rstd[:, :], c.std[:, :]).then_inc(self.rstd, 1)
        dve.wait_ge(self.rstd, n + 1)
        dve.tensor_scalar(out, x, c.mv[:, 0:1], c.rstd[:, 0:1], ALU.subtract, ALU.mult).then_inc(self.out, 1)

    def scalar(self, act, n):
        c = self.c
        act.wait_ge(self.var, n + 1)
        act.activation(c.std[:, :], c.mv[:, 1:2], ACT.Sqrt, bias=c.eps[:, 0:1]).then_inc(self.std, 1)

    def turn(self, pe, n, src, bank):
        pe.wait_ge(self.out, n + 1)
        for k in range(KT):
            mm = pe.transpose(bank[:, k * S:(k + 1) * S], src[:, k * P:(k + 1) * P], self.c.ident[:, :])
        mm.then_inc(self.turned, 1)

    def keep(self, dve, n, bank, dst):
        dve.wait_ge(self.turned, n + 1)
        dve.tensor_copy(dst, bank[:, 0:KT * S].rearrange("p (k s) -> p k s", k=KT)).then_inc(self.outT, 1)


def context_products(nc, c):
    T = c.T
    n_chunks = T // CH
    W = KVA + D
    VH = NKV + NH
    with ExitStack() as ctx:
        def sb(name, shape, dt=F32):
            return ctx.enter_context(nc.sbuf_tensor(name, shape, dt))

        ctx_tile = [sb(f"ctx_tile{i}", [P, KT, CH]) for i in range(2)]
        wk, wv = sb("wk_both", [P, KT, W]), sb("wv_both", [P, KT, W])
        ctx_part = [sb(f"ctx_part{i}", [P, SPLIT, KT, CH], F32R) for i in range(2)]
        wk_part, wv_part = sb("wk_part", [P, SPLIT, KT, W], F32R), sb("wv_part", [P, SPLIT, KT, W], F32R)
        products = ((0, 0), (0, 1), (1, 0))
        keys = [sb(f"keys_out{i}", [P, SPLIT, 1 + KT, CH], F32R) for i in range(2)]
        vals = sb("vals_out", [P, VH, 2 * BLK, HD])
        w_in = c.sem("kv_weights_in")
        ctx_in = [c.sem(f"ctx_in{i}") for i in range(2)]
        w_high, w_low = c.sem("kv_weights_high"), c.sem("kv_weights_low")
        ctx_high, ctx_low = c.sem("ctx_high"), c.sem("ctx_low")
        stored = [c.sem(f"kv_stored{i}") for i in range(2)]
        k_made = c.sem("k_made")
        k_high, k_low = c.sem("k_high"), c.sem("k_low")
        v_made = c.sem("v_made")
        v_kept = c.sem("v_kept")
        v_stored = c.sem("v_stored")
        k_units = [(KVA, 0, 0, n) for n in range(2)] + [(P, KVA + m * P, 1 + m, n) for m in range(KT) for n in range(2)]
        KU = len(k_units)
        STORES = SPLIT * (KT + 1)
        block = ctx.enter_context(nc.Block())

        def first(i):
            return isinstance(i, int) and i == 0

        @block.sync
        def _(sp):
            sp.dma_start(wk[:, :, 0:KVA], c.wkA).then_inc(w_in, 16)
            sp.dma_start(wk[:, :, KVA:W], c.wkD).then_inc(w_in, 16)
            sp.dma_start(wv[:, :, 0:KVA], c.wvA).then_inc(w_in, 16)
            sp.dma_start(wv[:, :, KVA:W], c.wvD).then_inc(w_in, 16)
            ctx_v = c.ctxT.rearrange("(k p) t -> p k t", p=P)
            for par in range(2):
                sp.dma_start(ctx_tile[par][:, :, :], ctx_v[:, :, par * CH:(par + 1) * CH]).then_inc(ctx_in[par], 16)

            def store(i, par):
                cols = bass.ds((2 * i + par) * CH, CH)
                sp.wait_ge(k_low, KU * (2 * i + par + 1))
                for part in range(SPLIT):
                    sp.dma_start(c.k1_dram[part, :, cols], keys[par][0:KVA, part, 0, :].bitcast(F32)).then_inc(stored[par], 16)
                    for m in range(KT):
                        sp.dma_start(c.k2_dram[part, m * P:(m + 1) * P, cols], keys[par][:, part, 1 + m, :].bitcast(F32)).then_inc(stored[par], 16)
                if par == 1:
                    sp.wait_ge(v_kept, BLK * (2 * i + 2))
                    sp.dma_start(c.v_dram.rearrange("h p n d -> p h n d")[:, :, bass.ds(2 * i * BLK, 2 * BLK), :],
                                 vals[:, :, :, :]).then_inc(v_stored, 16)

            def load(i, par):
                sp.wait_ge(ctx_low, 2 * i + par - 1)
                sp.dma_start(ctx_tile[par][:, :, :], ctx_v[:, :, bass.ds((2 * i + par) * CH, CH)]).then_inc(ctx_in[par], 16)

            if n_chunks > 2:
                with sp.Fori(1, n_chunks // 2) as i:
                    for par in range(2):
                        load(i, par)
                        store(i - 1, par)
            for par in range(2):
                store(n_chunks // 2 - 1, par)
            for par in range(2):
                sp.wait_ge(stored[par], 16 * STORES * (n_chunks // 2))
            sp.wait_ge(v_stored, 16 * (n_chunks // 2))

        def each_chunk(eng, body):
            pairs = n_chunks // 2
            for i in sorted({0, pairs - 1}):
                if i > 1:
                    with eng.Fori(1, pairs - 1) as r:
                        for par in range(2):
                            body(r, par)
                for par in range(2):
                    body(i, par)

        def following(i, par):
            last = isinstance(i, int) and i == n_chunks // 2 - 1 and par == 1
            return None if last else (i + par, 1 - par, 2 * i + par + 1)

        def v_bank(b):
            return c.bank((KU + b) % 8)

        @block.tensor
        def _(pe):
            pe.wait_ge(w_low, 2)

            def body(i, par):
                ch = 2 * i + par
                pe.wait_ge(ctx_low, ch + 1)
                for u, (m, w0, _, n) in enumerate(k_units):
                    if not (first(i) and par == 0):
                        if u + 2 < BLK:
                            pe.wait_ge(v_kept, BLK * (ch - 1) + u + 3)
                        else:
                            pe.wait_ge(k_low, KU * (ch - 1) + u + 1)
                    terms = [(k, a, b) for k in range(KT) for a, b in products]
                    for t, (k, a, b) in enumerate(terms):
                        mm = pe.matmul(c.bank(u)[0:m, 0:HC], wk_part[:, a, k, w0:w0 + m], ctx_part[par][:, b, k, n * HC:(n + 1) * HC],
                                       start=(t == 0), stop=(t == len(terms) - 1))
                    mm.then_inc(k_made, 1)
                for b in range(BLK):
                    if b >= 2:
                        pe.wait_ge(k_low, KU * ch + b - 1)
                    elif not (first(i) and par == 0):
                        pe.wait_ge(v_kept, BLK * (ch - 1) + b + 1)
                    terms = [(k, x, w) for k in range(KT) for x, w in products]
                    for t, (k, x, w) in enumerate(terms):
                        mm = pe.matmul(v_bank(b)[:, 0:W], ctx_part[par][:, x, k, b * P:(b + 1) * P], wv_part[:, w, k, :],
                                       start=(t == 0), stop=(t == len(terms) - 1))
                    mm.then_inc(v_made, 1)
            each_chunk(pe, body)

        @block.scalar
        def _(act):
            act.wait_ge(w_in, 64)
            act.copy(wk_part[:, 0, :, :], wk[:, :, :]).then_inc(w_high, 1)
            act.copy(wv_part[:, 0, :, :], wv[:, :, :]).then_inc(w_high, 1)

            def split(pair, par, ch):
                act.wait_ge(ctx_in[par], 16 * (pair + 1))
                if not (isinstance(ch, int) and ch < 2):
                    act.wait_ge(v_made, BLK * (ch - 1))
                act.copy(ctx_part[par][:, 0, :, :], ctx_tile[par][:, :, :]).then_inc(ctx_high, 1)
            split(0, 0, 0)

            def body(i, par):
                ch = 2 * i + par
                if following(i, par):
                    split(*following(i, par))
                if not first(i):
                    act.wait_ge(stored[par], 16 * STORES * i)
                for u, (m, _, r, n) in enumerate(k_units):
                    act.wait_ge(k_made, KU * ch + u + 1)
                    act.copy(keys[par][0:m, 0, r, n * HC:(n + 1) * HC], c.bank(u)[0:m, 0:HC]).then_inc(k_high, 1)
                for b in range(BLK):
                    act.wait_ge(v_made, BLK * ch + b + 1)
                    if b == 0 and par == 0 and not first(i):
                        act.wait_ge(v_stored, 16 * i)
                    act.copy(vals[:, :, par * BLK + b, :], v_bank(b)[:, 0:W].rearrange("p (h d) -> p h d", d=HD)).then_inc(v_kept, 1)
            each_chunk(act, body)

        @block.vector
        def _(dve):
            for n, (part, whole) in enumerate(((wk_part, wk), (wv_part, wv))):
                dve.wait_ge(w_high, n + 1)
                dve.tensor_tensor(part[:, 1, :, :], whole[:, :, :], part[:, 0, :, :].bitcast(F32), ALU.subtract).then_inc(w_low, 1)

            def split(pair, par, ch):
                dve.wait_ge(ctx_high, ch + 1)
                dve.tensor_tensor(ctx_part[par][:, 1, :, :], ctx_tile[par][:, :, :], ctx_part[par][:, 0, :, :].bitcast(F32),
                                  ALU.subtract).then_inc(ctx_low, 1)
            split(0, 0, 0)

            def body(i, par):
                ch = 2 * i + par
                if following(i, par):
                    split(*following(i, par))
                if not first(i):
                    dve.wait_ge(stored[par], 16 * STORES * i)
                for u, (m, _, r, n) in enumerate(k_units):
                    cols = slice(n * HC, (n + 1) * HC)
                    dve.wait_ge(k_high, KU * ch + u + 1)
                    dve.tensor_tensor(keys[par][0:m, 1, r, cols], c.bank(u)[0:m, 0:HC], keys[par][0:m, 0, r, cols].bitcast(F32),
                                      ALU.subtract).then_inc(k_low, 1)
            each_chunk(dve, body)


def load_key_tile(c, sp, t, cols, keys_dram, signal):
    rows = slice(t * KR, (t + 1) * KR) if isinstance(t, int) else bass.ds(t * KR, KR)
    for rep in range(KREP):
        sp.dma_start(c.keys[rep * KR:(rep + 1) * KR, cols].bitcast(F32), keys_dram[rep % SPLIT, rows, cols]).then_inc(signal, 16)


def queries(nc, c, name, w_dram, groups, keys_dram):
    tiles = NH // KG
    with ExitStack() as ctx:
        wq = ctx.enter_context(nc.sbuf_tensor(f"{name}_wq", [P, KT, tiles * KP], F32))
        w_in = c.sem(f"{name}_wq_in")
        keys_in = c.sem(f"{name}_first_keys_in")
        q = ctx.enter_context(nc.sbuf_tensor(f"{name}_q", [P, tiles, S], F32))
        high = ctx.enter_context(nc.sbuf_tensor(f"{name}_q_high", [P, tiles, S], F32R))
        low = ctx.enter_context(nc.sbuf_tensor(f"{name}_q_low", [P, tiles, S], F32R))
        part_now = ctx.enter_context(nc.sbuf_tensor(f"{name}_q_low_masked", [P, NH, S], F32))
        masked, merged = c.sem(f"{name}_q_masked"), c.sem(f"{name}_q_merged")
        made = c.sem(f"{name}_q_made")
        kept = c.sem(f"{name}_q_kept")
        split = c.sem(f"{name}_q_split")
        norm = Norm(c, f"{name}_norm")
        block = ctx.enter_context(nc.Block())

        @block.sync
        def _(sp):
            sp.dma_start(wq[:, :, :], w_dram).then_inc(w_in, 16)
            load_key_tile(c, sp, 0, slice(0, c.T), keys_dram, keys_in)
            sp.wait_ge(w_in, 16)
            sp.wait_ge(keys_in, 16 * KREP)

        @block.scalar
        def _(act):
            norm.scalar(act, 0)
            act.wait_ge(split, 2)
            for t in range(tiles):
                for g in range(KG):
                    h = (KG * (t // GRP) + g) * GRP + t % GRP if groups else t * KG + g
                    act.activation(part_now[0:KP, h, :], low[0:KP, t, :].bitcast(F32), ACT.Copy, scale=c.keymask[0:KP, 1, g:g + 1]).then_inc(masked, 1)

        @block.tensor
        def _(pe):
            norm.turn(pe, 0, c.xn, c.bank(tiles - 1))
            pe.wait_ge(norm.outT, 1)
            pe.wait_ge(w_in, 16)
            for t in range(tiles):
                for k in range(KT):
                    mm = pe.matmul(c.bank(t)[0:KP, 0:S], wq[:, k, t * KP:(t + 1) * KP], c.xT[:, k, :],
                                   start=(k == 0), stop=(k == KT - 1))
                mm.then_inc(made, 1)

        @block.vector
        def _(dve):
            norm.vector(dve, 0, c.x[:, :], c.xn[:, :])
            norm.keep(dve, 0, c.bank(tiles - 1), c.xT[:, :, :])
            for t in range(tiles):
                dve.wait_ge(made, t + 1)
                dve.tensor_scalar(q[0:KP, t, :], c.bank(t)[0:KP, 0:S], float(HD) ** -0.5, None, ALU.mult).then_inc(kept, 1)
            dve.wait_ge(kept, tiles)
            dve.tensor_copy(high[0:KP, :, :], q[0:KP, :, :]).then_inc(split, 1)
            dve.wait_ge(split, 1)
            dve.tensor_tensor(low[0:KP, :, :], q[0:KP, :, :], high[0:KP, :, :].bitcast(F32), ALU.subtract).then_inc(split, 1)
            dve.wait_ge(split, 2)
            done = 0
            for t in range(tiles):
                for g in range(KG):
                    h = (KG * (t // GRP) + g) * GRP + t % GRP if groups else t * KG + g
                    done += 1
                    dve.wait_ge(masked, done)
                    dve.scalar_tensor_tensor(c.qm[0:KP, h, :], high[0:KP, t, :].bitcast(F32), c.keymask[0:KP, 0, g:g + 1],
                                             part_now[0:KP, h, :], ALU.mult, ALU.add).then_inc(merged, 1)
            dve.wait_ge(merged, NH)


def attention(nc, c, name, v_dram, heads_per_v, bias, keys_dram):
    T = c.T
    NC = T // CH
    NB = T // P
    HALF = NC // 2
    HB = HALF * CH
    LEAD = 2
    OUT = SPLIT * S
    key_tiles = keys_dram.shape[1] // KR
    with ExitStack() as ctx:
        def sb(nm, shape, dt=F32):
            return ctx.enter_context(nc.sbuf_tensor(f"{name}_{nm}", shape, dt))

        def sem(nm):
            return c.sem(f"{name}_{nm}")

        q_head = [sb(f"q_head{i}", [P, S], F32R) for i in range(2)]
        v_raw = [sb(f"v_raw{j}", [P, NB // 2, HD]) for j in range(2)]
        v_half = [sb(f"v_half{j}", [P, NB // 2, SPLIT * HD], F32R) for j in range(2)]
        keys = c.keys
        s = c.scores
        probT = [sb(f"probT{i}", [P, BLK, SPLIT, S], F32R) for i in range(2)]
        chunk_max = [sb(f"chunk_max{i}", [S, NC]) for i in range(2)]
        neg_max = [sb(f"neg_max{i}", [S, 1]) for i in range(2)]
        chunk_sum = [sb(f"chunk_sum{i}", [S, NC]) for i in range(2)]
        total, inv_total = sb("total", [S, 1]), sb("inv_total", [S, 1])
        gate = sb("gate", [S, 1])
        outT = [sb(f"outT{i}", [SPLIT * HD, SPLIT, S]) for i in range(2)]
        q_staged = sem("q_staged")
        v_high = [sem(f"v_high{j}") for j in range(2)]
        v_low = [sem(f"v_low{j}") for j in range(2)]
        v_in = [sem(f"v_in{j}") for j in range(2)]
        bias_in = [[sem(f"bias_in{i}{j}") for j in range(2)] for i in range(2)]
        keys_in = [sem(f"keys_in{j}") for j in range(2)]
        made = sem("scores_made")
        kept = sem("scores_kept")
        max_ready = sem("max_ready")
        exp_ready = sem("exp_ready")
        turned = [sem("turned_a"), sem("turned_b")]
        high = [sem("prob_high_a"), sem("prob_high_b")]
        low = [sem("prob_low_a"), sem("prob_low_b")]
        pv_done = sem("pv_done")
        outT_kept = sem("outT_kept")
        out_ready = sem("out_ready")
        head_done = sem("head_done")
        step = sem("small_step")
        gated = sem("gated")
        block = ctx.enter_context(nc.Block())
        units = [(0, PA), (PA, BLK)]
        PAIRS = NH // 2
        PPT = PAIRS // key_tiles

        def ahead(it, par, ch):
            heads_on, chunk = 1 + (ch + LEAD) // NC, (ch + LEAD) % NC
            if known(it) and 2 * it + par + heads_on >= NH:
                return None
            return it + (par + heads_on) // 2, (par + heads_on) % 2, 2 * it + par + heads_on, chunk

        def known(h):
            return isinstance(h, int)

        def one(ap, h):
            return ap[h:h + 1] if known(h) else ap[bass.ds(h, 1)]

        def pairs(eng, body):
            peeled = sorted({0, PAIRS - 1} | ({t * PPT - 1 for t in range(1, key_tiles)} if PPT > 1 else set()))
            for a, b in zip(peeled, peeled[1:]):
                body(a)
                if b - a == 2:
                    body(a + 1)
                elif b - a > 2:
                    with eng.Fori(a + 1, b) as it:
                        body(it)
            body(PAIRS - 1)

        @block.sync
        def _(sp):
            def load_v(h, j):
                sp.dma_start(v_raw[j][:, :, :],
                             one(v_dram, h // heads_per_v)[:, :, j * (NB // 2):(j + 1) * (NB // 2), :].rearrange("o p n d -> (o p) n d")).then_inc(v_in[j], 16)

            def load_bias(h, par, j):
                sp.dma_start(s[par][:, j * HB:(j + 1) * HB], one(bias, h)[:, :, j * HB:(j + 1) * HB].rearrange("o q t -> (o q) t")).then_inc(bias_in[par][j], 16)

            def load_keys(t, j):
                load_key_tile(c, sp, t, slice(j * HB, (j + 1) * HB), keys_dram, keys_in[j])

            if bias is not None:
                for j in range(2):
                    load_bias(0, 0, j)
            for j in range(2):
                load_v(0, j)
                if bias is not None:
                    load_bias(1, 1, j)

            def body(it):
                for par in range(2):
                    h = 2 * it + par
                    changes = par == 0 and (PPT == 1 or (known(h) and (it + 1) % PPT == 0)) and not (known(h) and it == PAIRS - 1)
                    if known(h) and h == NH - 1:
                        continue
                    for j in range(2):
                        if changes:
                            sp.wait_ge(made, (h + 1) * NC + HALF * (j + 1))
                            load_keys((it + 1) // PPT if known(h) else it + 1, j)
                        if bias is not None and not (known(h) and h == NH - 2):
                            sp.wait_ge(turned[1], h * NC + HALF * (j + 1))
                            load_bias(h + 2, par, j)
                        sp.wait_ge(v_low[j], h + 1)
                        load_v(h + 1, j)
            pairs(sp, body)

        @block.gpsimd
        def _(pool):
            def stage(h, par):
                src = c.qm[0:KP, h, :] if known(h) else c.qm[0:KP, bass.ds(h, 1), :].rearrange("p o s -> p (o s)")
                pool.tensor_copy(q_head[par][0:KP, :], src).then_inc(q_staged, 1)

            def split_v(h, j, free_at):
                pool.wait_ge(v_in[j], 16 * (h + 1))
                if free_at is not None:
                    pool.wait_ge(pv_done, free_at)
                pool.tensor_tensor(v_half[j][:, :, 0:HD], v_raw[j][:, :, :], c.ones[:, :].unsqueeze(1).broadcast_to((P, NB // 2, HD)), ALU.mult).then_inc(v_high[j], 1)
                pool.wait_ge(v_high[j], h + 1)
                pool.tensor_tensor(v_half[j][:, :, HD:2 * HD], v_raw[j][:, :, :], v_half[j][:, :, 0:HD].bitcast(F32),
                                   ALU.subtract).then_inc(v_low[j], 1)

            for par in range(2):
                stage(par, par)
            for j in range(2):
                split_v(0, j, None)

            def body(it):
                for par in range(2):
                    h = 2 * it + par
                    if not (known(it) and it == PAIRS - 1):
                        pool.wait_ge(made, (h + 1) * NC)
                        stage(h + 2, par)
                    if not (known(h) and h == NH - 1):
                        for j in range(2):
                            split_v(h + 1, j, h * NC + HALF * (j + 1))
            pairs(pool, body)

        @block.tensor
        def _(pe):
            def scores(h, par, ch, tile=None):
                n = h * NC + ch
                if ch == 0:
                    pe.wait_ge(q_staged, h + 1)
                if ch % HALF == 0 and tile is not None:
                    pe.wait_ge(keys_in[ch // HALF], 16 * KREP * tile)
                if not (known(h) and n < 2):
                    pe.wait_ge(kept, n - 1)
                for k in range(2):
                    mm = pe.matmul(c.sc[ch % 2][:, k, 0:HC], q_head[par][0:KP, :],
                                   keys[0:KP, ch * CH + k * HC:ch * CH + (k + 1) * HC], start=True, stop=True)
                mm.then_inc(made, 1)

            def turn(h, par, ch):
                n = h * NC + ch
                pe.wait_ge(exp_ready, n + 1)
                for u, (b0, b1) in enumerate(units):
                    if not (known(h) and n == 0):
                        pe.wait_ge(low[u], n)
                    for b in range(b0, b1):
                        col = ch * CH + b * P
                        mm = pe.transpose(c.single[u][:, (b - b0) * S:(b - b0 + 1) * S], s[par][:, col:col + P], c.ident[:, :])
                    mm.then_inc(turned[u], 1)

            def weigh(h, par, ch):
                if ch == 0 and not (known(h) and h < 2):
                    pe.wait_ge(head_done, h - 1)
                if ch % HALF == 0:
                    pe.wait_ge(v_low[ch // HALF], h + 1)
                for u, (b0, b1) in enumerate(units):
                    pe.wait_ge(low[u], h * NC + ch + 1)
                    for b in range(b0, b1):
                        mm = pe.matmul(c.single[2 + par][0:SPLIT * HD, 0:SPLIT * S], v_half[ch // HALF][:, (ch % HALF) * BLK + b, :],
                                       probT[ch % 2][:, b, :, :].rearrange("p a s -> p (a s)"),
                                       start=(ch == 0 and b == 0), stop=(ch == NC - 1 and b == BLK - 1))
                mm.then_inc(pv_done, 1)

            def fold(h, par):
                pe.wait_ge(outT_kept, h + 1)
                for part in range(SPLIT):
                    mm = pe.matmul(c.single[2 + par][:, OUT:OUT + HD], outT[par][:, part, :], c.fold[:, :],
                                   start=(part == 0), stop=(part == SPLIT - 1))
                mm.then_inc(out_ready, 1)

            for ch in range(NC):
                scores(0, 0, ch)
            for ch in range(LEAD):
                scores(1, 1, ch)

            def new_tile(it, par):
                if par == 1:
                    return None
                if PPT == 1:
                    return it
                return it // PPT if known(it) and it % PPT == 0 else None

            def body(it):
                for par in range(2):
                    h = 2 * it + par
                    for ch in range(NC):
                        on = ahead(it, par, ch)
                        if on:
                            scores(on[2], on[1], on[3], new_tile(on[0], on[1]))
                        turn(h, par, ch)
                        if ch >= 1:
                            weigh(h, par, ch - 1)
                        elif not (known(h) and h == 0):
                            weigh(h - 1, 1 - par, NC - 1)
                        if ch == 1 and not (known(h) and h == 0):
                            fold(h - 1, 1 - par)
            pairs(pe, body)
            weigh(NH - 1, 1, NC - 1)
            fold(NH - 1, 1)

        @block.scalar
        def _(act):
            def exp(h, par, ch):
                if ch == 0:
                    act.wait_ge(max_ready, h + 1)
                    if not (known(h) and h < 2):
                        act.wait_ge(head_done, h - 1)
                part = s[par][:, ch * CH:(ch + 1) * CH]
                act.activation(part, part, ACT.Exp, bias=neg_max[par][:, 0:1],
                               accum_out=chunk_sum[par][:, ch:ch + 1]).then_inc(exp_ready, 1)

            def keep_out(h, par):
                act.wait_ge(pv_done, (h + 1) * NC)
                act.copy(outT[par][:, :, :], c.single[2 + par][0:SPLIT * HD, 0:SPLIT * S].rearrange("p (a s) -> p a s", s=S)).then_inc(outT_kept, 1)

            for ch in range(LEAD):
                exp(0, 0, ch)

            def body(it):
                for par in range(2):
                    h = 2 * it + par
                    for ch in range(NC):
                        n = h * NC + ch
                        for u, (b0, b1) in enumerate(units):
                            act.wait_ge(turned[u], n + 1)
                            if u == 0 and not (known(h) and n < 2):
                                act.wait_ge(pv_done, n - 1)
                            act.copy(probT[ch % 2][:, b0:b1, 0, :], c.single[u][:, 0:(b1 - b0) * S].rearrange("p (b s) -> p b s", s=S)).then_inc(high[u], 1)
                        if ch + LEAD < NC:
                            exp(h, par, ch + LEAD)
                        elif not (known(h) and h == NH - 1):
                            exp(h + 1, 1 - par, ch + LEAD - NC)
                        if ch == 0 and not (known(h) and h == 0):
                            keep_out(h - 1, 1 - par)
            pairs(act, body)
            keep_out(NH - 1, 1)

        @block.vector
        def _(dve):
            def keep(it, par, h, ch):
                n = h * NC + ch
                dve.wait_ge(made, n + 1)
                src = c.sc[ch % 2][:, :, 0:HC]
                dst = s[par][:, ch * CH:(ch + 1) * CH].rearrange("p (k n) -> p k n", k=2)
                if bias is None:
                    if not (known(h) and h < 2):
                        dve.wait_ge(turned[1], (h - 2) * NC + ch + 1)
                    dve.tensor_scalar(dst, src, 1.0, LOWEST, ALU.mult, ALU.max,
                                      accum_out=chunk_max[par][:, ch:ch + 1]).then_inc(kept, 1)
                else:
                    if ch % HALF == 0:
                        dve.wait_ge(bias_in[par][ch // HALF], 16 * (it + 1))
                    if not (known(h) and n == 0):
                        dve.wait_ge(gated, n)
                    dve.memset(gate[:, :], 0.0).then_inc(gated, 1)
                    dve.tensor_tensor_reduce(dst, src, dst, 1.0, LOWEST, ALU.add, ALU.max,
                                             chunk_max[par][:, ch:ch + 1]).then_inc(kept, 1)

            def head_max(h, par):
                dve.wait_ge(kept, (h + 1) * NC)
                if not (known(h) and h < 2):
                    dve.wait_ge(exp_ready, (h - 1) * NC)
                dve.tensor_reduce(neg_max[par][:, :], chunk_max[par][:, :], AX_X, ALU.max, negate=True).then_inc(max_ready, 1)

            def low_parts(h, ch):
                n = h * NC + ch
                for u, (b0, b1) in enumerate(units):
                    dve.wait_ge(high[u], n + 1)
                    dve.tensor_tensor(probT[ch % 2][:, b0:b1, 1, :], c.single[u][:, 0:(b1 - b0) * S].rearrange("p (b s) -> p b s", s=S),
                                      probT[ch % 2][:, b0:b1, 0, :].bitcast(F32), ALU.subtract).then_inc(low[u], 1)

            def divide(h, par):
                dve.wait_ge(exp_ready, (h + 1) * NC)
                dve.reduce_sum(total[:, :], chunk_sum[par][:, :], AX_X).then_inc(step, 1)
                dve.wait_ge(step, 2 * h + 1)
                dve.reciprocal(inv_total[:, :], total[:, :]).then_inc(step, 1)
                dve.wait_ge(step, 2 * h + 2)
                dve.wait_ge(out_ready, h + 1)
                dve.tensor_scalar(c.attn[:, bass.ds(h * HD, HD)], c.single[2 + par][:, OUT:OUT + HD],
                                  inv_total[:, 0:1], None, ALU.mult).then_inc(head_done, 1)

            for ch in range(NC):
                keep(0, 0, 0, ch)
            head_max(0, 0)
            for ch in range(LEAD):
                keep(0, 1, 1, ch)

            def body(it):
                for par in range(2):
                    h = 2 * it + par
                    for ch in range(NC):
                        on = ahead(it, par, ch)
                        if on:
                            keep(*on)
                            if on[3] == NC - 1:
                                head_max(on[2], on[1])
                        low_parts(h, ch)
                        if ch == 2 and not (known(h) and h == 0):
                            divide(h - 1, 1 - par)
            pairs(dve, body)
            divide(NH - 1, 1)


def project_out(nc, c, name, w_dram, base, dst):
    with ExitStack() as ctx:
        w = ctx.enter_context(nc.sbuf_tensor(f"{name}_wo", [P, KT, D], F32))
        w_in = c.sem(f"{name}_wo_in")
        turned = c.sem(f"{name}_attn_turned")
        attnT = c.sem(f"{name}_attnT_kept")
        made = c.sem(f"{name}_out_made")
        added = c.sem(f"{name}_x_added")
        block = ctx.enter_context(nc.Block())

        @block.sync
        def _(sp):
            sp.dma_start(w[:, :, :], w_dram).then_inc(w_in, 16)

        @block.tensor
        def _(pe):
            for k in range(KT):
                mm = pe.transpose(c.bank(4)[:, k * S:(k + 1) * S], c.attn[:, k * P:(k + 1) * P], c.ident[:, :])
            mm.then_inc(turned, 1)
            pe.wait_ge(attnT, 1)
            pe.wait_ge(w_in, 16)
            for k in range(KT):
                mm = pe.matmul(c.bank(5)[:, 0:D], c.xT[:, k, :], w[:, k, :], start=(k == 0), stop=(k == KT - 1))
            mm.then_inc(made, 1)

        @block.vector
        def _(dve):
            dve.wait_ge(turned, 1)
            dve.tensor_copy(c.xT[:, :, :], c.bank(4)[:, 0:KT * S].rearrange("p (k s) -> p k s", k=KT)).then_inc(attnT, 1)
            dve.wait_ge(made, 1)
            dve.tensor_tensor(dst[:, :], base[:, :], c.bank(5)[:, 0:D], ALU.add).then_inc(added, 1)
            dve.wait_ge(added, 1)


def relative_attention(nc, c):
    R = 5
    BAND = 3
    with ExitStack() as ctx:
        def sb(nm, shape):
            return ctx.enter_context(nc.sbuf_tensor(f"rel_{nm}", shape, F32))

        def sem(nm):
            return c.sem(f"rel_{nm}")

        w = {n: sb(f"w{n}", [P, KT, D]) for n in "qkvo"}
        bcol = {n: sb(f"bcol_{n}", [P, KT]) for n in "qk"}
        brow = {n: sb(f"brow_{n}", [S, D]) for n in "vo"}
        relk = sb("relk", [P, R])
        relk_heads = sb("relk_heads", [P, HPT, R])
        relv = sb("relv", [S, R, HD])
        band = sb("band", [S, BAND, S])
        qT, kT, v = sb("qT", [P, KT, S]), sb("kT", [P, KT, S]), sb("v", [S, D])
        qm = sb("qm", [P, NH, S])
        r = sb("r", [S, NH, R])
        sc, t, t2 = sb("scores", [S, NH, S]), sb("t", [S, NH, S]), sb("t2", [S, NH, S])
        r_kept, last_band = sem("r_kept"), sem("last_band")
        pT = sb("pT", [S, NH, S])
        mx, total, wgt = sb("mx", [S, NH]), sb("total", [S, NH]), sb("wgt", [S, BAND, NH])
        o, ot = sb("o", [S, NH, HD]), sb("ot", [S, NH, HD])
        norm = Norm(c, "rel_norm")
        w_in, band_step, band_made = sem("w_in"), sem("band_step"), sem("band_made")
        proj_made, q_ready, scores_made, r_made = sem("proj_made"), sem("q_ready"), sem("scores_made"), sem("r_made")
        rel_added, masked, max_ready, exp_ready = sem("rel_added"), sem("masked"), sem("max_ready"), sem("exp_ready")
        p_turned, pT_ready, pv_made, o_ready = sem("p_turned"), sem("pT_ready"), sem("pv_made"), sem("o_ready")
        o_turned, oT_ready, out_made, steps = sem("o_turned"), sem("oT_ready"), sem("out_made"), sem("steps")
        LOADS = 4 + 2 + 2 + HPT + 1
        block = ctx.enter_context(nc.Block())

        @block.sync
        def _(sp):
            for n in "qkvo":
                sp.dma_start(w[n][:, :, :], c.rel[f"W_{n}"]).then_inc(w_in, 16)
            for n in "qk":
                sp.dma_start(bcol[n][:, :], c.rel[f"b_{n}"]).then_inc(w_in, 16)
            for n in "vo":
                sp.dma_start(brow[n][:, :], c.rel[f"b_{n}"].rearrange("(o d) -> o d", o=1).broadcast_to((S, D))).then_inc(w_in, 16)
            for h in range(HPT):
                sp.dma_start(relk[h * HD:(h + 1) * HD, :], c.rel["rel_kT"]).then_inc(w_in, 16)
            sp.dma_start(relv[:, :, :].rearrange("p r d -> p (r d)"),
                         c.rel["rel_v_table"].rearrange("(o r) d -> o (r d)", o=1).broadcast_to((S, R * HD))).then_inc(w_in, 16)
            sp.wait_ge(w_in, 16 * LOADS)

        @block.gpsimd
        def _(pool):
            pool.memset(band[:, 0, :], 1.0).then_inc(band_step, 1)
            pool.memset(band[:, 1, :], 0.0).then_inc(band_step, 1)
            pool.tensor_copy(band[:, 2, :], c.ident[:, :]).then_inc(band_step, 1)
            pool.wait_ge(band_step, 3)
            pool.affine_select(out=band[:, 0, :], in_=band[:, 0, :], compare_op=ALU.is_ge, fill=0.0,
                               base=-2, pattern=[[-1, S]], channel_multiplier=1).then_inc(band_made, 1)
            pool.affine_select(out=band[:, 1, :], in_=band[:, 1, :], compare_op=ALU.not_equal, fill=1.0,
                               base=-1, pattern=[[-1, S]], channel_multiplier=1).then_inc(band_made, 1)
            pool.wait_ge(r_kept, 1)
            pool.wait_ge(band_made, 2)
            pool.tensor_tensor(t2[:, :, :], band[:, 2, :].unsqueeze(1).broadcast_to((S, NH, S)),
                               r[:, :, 2:3].broadcast_to((S, NH, S)), ALU.mult).then_inc(last_band, 1)
            pool.wait_ge(rel_added, 1)
            pool.affine_select(out=sc[:, :, :], in_=sc[:, :, :], compare_op=ALU.is_ge, fill=-1.0e9 * HD ** 0.5,
                               base=0, pattern=[[0, NH], [-1, S]], channel_multiplier=1).then_inc(masked, 1)
            pool.wait_ge(exp_ready, NH)
            pool.tensor_tensor(t2[:, :, :], sc[:, :, :], band[:, 2, :].unsqueeze(1).broadcast_to((S, NH, S)), ALU.mult).then_inc(last_band, 1)

        @block.scalar
        def _(act):
            norm.scalar(act, 0)
            act.wait_ge(max_ready, 1)
            for h in range(NH):
                act.activation(sc[:, h, :], sc[:, h, :], ACT.Exp, bias=mx[:, h:h + 1], scale=HD ** -0.5,
                               accum_out=total[:, h:h + 1]).then_inc(exp_ready, 1)
            act.wait_ge(p_turned, 1)
            act.copy(pT[:, :, :], c.ps[:, 0:4, :].rearrange("p b (h s) -> p (b h) s", s=S)).then_inc(pT_ready, 1)

        @block.tensor
        def _(pe):
            norm.turn(pe, 0, c.xn, c.bank(4))
            pe.wait_ge(norm.outT, 1)
            pe.wait_ge(w_in, 16 * LOADS)
            for i, n in enumerate("qk"):
                for m in range(KT):
                    for k in range(KT):
                        mm = pe.matmul(c.bank(i)[:, m * S:(m + 1) * S], w[n][:, k, m * P:(m + 1) * P], c.xT[:, k, :],
                                       start=(k == 0), stop=(k == KT - 1))
                mm.then_inc(proj_made, 1)
            for k in range(KT):
                mm = pe.matmul(c.bank(2)[:, 0:D], c.xT[:, k, :], w["v"][:, k, :], start=(k == 0), stop=(k == KT - 1))
            mm.then_inc(proj_made, 1)
            pe.wait_ge(q_ready, 1)
            for m in range(KT):
                mm = pe.matmul(c.bank(5)[:, m * HPT * R:(m + 1) * HPT * R], qT[:, m, :],
                               relk_heads[:, :, :].rearrange("p h r -> p (h r)"), start=True, stop=True)
            mm.then_inc(r_made, 1)
            pe.wait_ge(q_ready, 2)
            for h in range(NH):
                mm = pe.matmul(c.bank(h // 4)[:, (h % 4) * S:(h % 4 + 1) * S], qm[:, h, :], kT[:, h // HPT, :], start=True, stop=True)
            mm.then_inc(scores_made, 1)
            for h in range(NH):
                pe.wait_ge(exp_ready, h + 1)
                mm = pe.transpose(c.bank(h // 4)[:, (h % 4) * S:(h % 4 + 1) * S], sc[:, h, :], c.ident[:, :])
            mm.then_inc(p_turned, 1)
            pe.wait_ge(pT_ready, 1)
            for h in range(NH):
                mm = pe.matmul(c.bank(6)[:, h * HD:(h + 1) * HD], pT[:, h, :], v[:, h * HD:(h + 1) * HD], start=True, stop=True)
            mm.then_inc(pv_made, 1)
            pe.wait_ge(o_ready, 1)
            for k in range(KT):
                mm = pe.transpose(c.bank(4)[:, k * S:(k + 1) * S], o[:, k * HPT:(k + 1) * HPT, :].rearrange("p h d -> p (h d)"), c.ident[:, :])
            mm.then_inc(o_turned, 1)
            pe.wait_ge(oT_ready, 1)
            for k in range(KT):
                mm = pe.matmul(c.bank(7)[:, 0:D], c.xT[:, k, :], w["o"][:, k, :], start=(k == 0), stop=(k == KT - 1))
            mm.then_inc(out_made, 1)

        @block.vector
        def _(dve):
            chain = Chain(dve, steps)
            dve.wait_ge(w_in, 16 * LOADS)
            chain(dve.tensor_tensor(relk_heads[:, :, :], relk[:, :].unsqueeze(1).broadcast_to((P, HPT, R)),
                                    c.headmask[:, :].unsqueeze(2).broadcast_to((P, HPT, R)), ALU.mult))
            norm.vector(dve, 0, c.x[:, :], c.xn[:, :])
            norm.keep(dve, 0, c.bank(4), c.xT[:, :, :])
            dve.wait_ge(proj_made, 1)
            for m in range(KT):
                chain(dve.tensor_scalar(qT[:, m, :], c.bank(0)[:, m * S:(m + 1) * S], bcol["q"][:, m:m + 1], None, ALU.add))
            dve.sem_inc(q_ready, 1)
            dve.wait_ge(proj_made, 2)
            for m in range(KT):
                chain(dve.tensor_scalar(kT[:, m, :], c.bank(1)[:, m * S:(m + 1) * S], bcol["k"][:, m:m + 1], None, ALU.add))
            for h in range(NH):
                ins = dve.tensor_scalar(qm[:, h, :], qT[:, h // HPT, :], c.headmask[:, h % HPT:h % HPT + 1], None, ALU.mult)
            chain(ins)
            dve.wait_ge(proj_made, 3)
            chain(dve.tensor_tensor(v[:, :], c.bank(2)[:, 0:D], brow["v"][:, :], ALU.add))
            dve.sem_inc(q_ready, 1)
            dve.wait_ge(r_made, 1)
            dve.tensor_copy(r[:, :, :].rearrange("p h r -> p (h r)"), c.bank(5)[:, 0:NH * R]).then_inc(r_kept, 1)
            dve.wait_ge(r_kept, 1)
            dve.wait_ge(band_made, 2)
            def band_term(j, out):
                return dve.tensor_tensor(out[:, :, :], band[:, j, :].unsqueeze(1).broadcast_to((S, NH, S)),
                                         r[:, :, j:j + 1].broadcast_to((S, NH, S)), ALU.mult)
            chain(band_term(0, sc))
            chain(band_term(1, t))
            chain(dve.tensor_tensor(sc[:, :, :], sc[:, :, :], t[:, :, :], ALU.add))
            dve.wait_ge(last_band, 1)
            chain(dve.tensor_tensor(sc[:, :, :], sc[:, :, :], t2[:, :, :], ALU.add))
            dve.wait_ge(scores_made, 1)
            dve.tensor_tensor(sc[:, :, :], c.ps[:, 0:4, :].rearrange("p b (h s) -> p (b h) s", s=S), sc[:, :, :], ALU.add).then_inc(rel_added, 1)
            dve.wait_ge(masked, 1)
            chain(dve.tensor_reduce(mx[:, :], sc[:, :, :], AX_X, ALU.max, negate=True))
            dve.tensor_scalar(mx[:, :], mx[:, :], HD ** -0.5, None, ALU.mult).then_inc(max_ready, 1)
            dve.wait_ge(exp_ready, NH)
            chain(dve.tensor_tensor(t[:, :, :], sc[:, :, :], band[:, 1, :].unsqueeze(1).broadcast_to((S, NH, S)), ALU.mult))
            chain(dve.reduce_sum(wgt[:, 1, :], t[:, :, :], AX_X))
            dve.wait_ge(last_band, 2)
            chain(dve.reduce_sum(wgt[:, 2, :], t2[:, :, :], AX_X))
            chain(dve.tensor_tensor(wgt[:, 0, :], total[:, :], wgt[:, 1, :], ALU.subtract))
            chain(dve.tensor_tensor(wgt[:, 0, :], wgt[:, 0, :], wgt[:, 2, :], ALU.subtract))
            dve.wait_ge(pv_made, 1)
            for j in range(BAND):
                chain(dve.tensor_tensor(ot[:, :, :], wgt[:, j, :].unsqueeze(2).broadcast_to((S, NH, HD)),
                                        relv[:, j, :].unsqueeze(1).broadcast_to((S, NH, HD)), ALU.mult))
                acc = c.bank(6)[:, 0:D].rearrange("p (h d) -> p h d", d=HD) if j == 0 else o[:, :, :]
                chain(dve.tensor_tensor(o[:, :, :], acc, ot[:, :, :], ALU.add))
            chain(dve.reciprocal(total[:, :], total[:, :]))
            dve.tensor_tensor(o[:, :, :], o[:, :, :], total[:, :].unsqueeze(2).broadcast_to((S, NH, HD)), ALU.mult).then_inc(o_ready, 1)
            chain(dve.tensor_tensor(c.x[:, :], c.x[:, :], brow["o"][:, :], ALU.add))
            dve.wait_ge(o_turned, 1)
            dve.tensor_copy(c.xT[:, :, :], c.bank(4)[:, 0:KT * S].rearrange("p (k s) -> p k s", k=KT)).then_inc(oT_ready, 1)
            dve.wait_ge(out_made, 1)
            chain(dve.tensor_tensor(c.x[:, :], c.x[:, :], c.bank(7)[:, 0:D], ALU.add))


def tiled(w):
    return w.rearrange("(k p) n -> p k n", p=P)


def store_x(nc, c, out):
    stored = c.sem("x_stored")
    with nc.Block() as block:
        @block.sync
        def _(sp):
            sp.dma_start(out.rearrange("o s d -> (o s) d"), c.x[:, :]).then_inc(stored, 16)
            sp.wait_ge(stored, 16)


LH, LD = 16, 64
INNER = LH * LD
WINDOW = 64
QK_SCALE = 8.0
DEPTH = 6
FF = int(D * 4 * 2 / 3)
FT = -(-FF // P)
FLAST = FF - (FT - 1) * P
MASKED = -1.0e30


def rotary_tables():
    import numpy as np
    f = np.float32
    half = np.arange(0, LD, 2, dtype=f)
    inv_freq = (f(1.0) / f(10000.0) ** (half / f(LD))).astype(f)
    t = np.arange(S, dtype=f)
    freqs = np.concatenate([t[:, None] * inv_freq[None, :]] * 2, -1)
    base = (half + f(0.4 * LD)) / f(1.4 * LD)
    scale = base[None, :] ** ((t - S // 2) / f(WINDOW // 2))[:, None]
    scale = np.concatenate([scale, scale], -1)
    sign = np.where(np.arange(LD) < LD // 2, f(-1), f(1))
    cos, sin = np.cos(freqs), np.sin(freqs) * sign
    return np.stack([cos * scale, sin * scale, cos / scale, sin / scale], 1).astype(f)


def local_transformer(nc, c):
    with ExitStack() as ctx:
        def sb(nm, shape):
            return ctx.enter_context(nc.sbuf_tensor(f"loc_{nm}", shape, F32))

        def sem(nm):
            return c.sem(f"loc_{nm}")

        wqkv, wo = sb("wqkv", [P, KT, 3 * INNER]), sb("wo", [P, INNER // P, D])
        w1, w2 = sb("w1", [P, KT, 2 * FF]), sb("w2", [P, FT, D])
        cols_all, rows_all = sb("cols_all", [P, DEPTH, 2 * KT + 2 * FT]), sb("rows_all", [S, DEPTH, 2 * LD + D])
        cols, rows = sb("cols", [P, 2 * KT + 2 * FT]), sb("rows", [S, 2 * LD + D])
        rot_all, rot = sb("rot_all", [S, 4, LD]), sb("rot", [S, 4, LD])
        shift, mask = sb("shift", [S, S]), sb("mask", [S, S])
        y, shifted = sb("y", [S, D]), sb("shifted", [S, D])
        tT, hT = sb("tT", [P, KT, S]), sb("hT", [P, FT, S])
        v, sq = sb("v", [S, INNER]), sb("sq", [S, 2 * INNER])
        norms = sb("norms", [S, 2 * LH])
        qk = [sb(f"qk{i}", [S, LH, LD]) for i in range(2)]
        qa, qb = sb("qa", [S, LH, LD]), sb("qb", [S, LH, LD])
        qkT = [sb(f"qkT{i}", [P, LH // 2, S]) for i in range(2)]
        sc, pT = sb("sc", [S, LH, S]), sb("pT", [S, LH, S])
        mx, total, inv, q_scale = (sb(n, [S, LH]) for n in ("mx", "total", "inv", "q_scale"))
        oT = sb("oT", [P, INNER // P, S])
        spare = sb("spare", [P, 1])
        gate = sb("gate", [P, FT, S])

        norm0, norm = Norm(c, "loc_in"), Norm(c, "loc_norm")
        small_in, made_mask, mask_step = sem("small_in"), sem("mask_made"), sem("mask_step")
        w_in = {n: sem(f"{n}_in") for n in ("wqkv", "wo", "w1", "w2")}
        y_ready, y_turned, tT_ready = sem("y_ready"), sem("y_turned"), sem("tT_ready")
        qkv_made, squared, normed = sem("qkv_made"), sem("squared"), sem("sums_ready")
        rooted, v_kept = sem("norms_rooted"), sem("v_kept")
        rotated, qk_turned, qkT_ready = sem("qk_rotated"), sem("qk_turned"), sem("qkT_ready")
        rot_ready, rot_step = sem("rot_ready"), sem("rot_step")
        scores_made, max_ready, exp_ready = sem("scores_made"), sem("max_ready"), sem("exp_ready")
        inverted, scaled, table_in = sem("inverted"), sem("scaled"), sem("table_in")
        p_turned, pT_ready, pv_made = sem("p_turned"), sem("pT_ready"), sem("pv_made")
        oT_ready, wo_made, mid_ready = sem("oT_ready"), sem("wo_made"), sem("mid_ready")
        shift_made, h_made, gelu_ready, hT_ready, w2_made = sem("shift_made"), sem("h_made"), sem("gelu_ready"), sem("hT_ready"), sem("w2_made")
        steps, layer_done, cols_ready = sem("steps"), sem("layer_done"), sem("cols_ready")
        block = ctx.enter_context(nc.Block())
        QO, KO = 0, LD
        B2 = 2 * LD

        def h_tile(u, m):
            t = u % FT
            return c.bank(((3, 4), (5, 7))[u // FT][t // 4])[0:m, (t % 4) * S:(t % 4 + 1) * S]

        def h_signals(u):
            return 2 * (u // FT) + (u % FT) // 4 + 1

        def tile_rows(t):
            return P if t % FT < FT - 1 else FLAST

        @block.sync
        def _(sp):
            sp.dma_start(cols_all[:, :, :], c.loc["cols"]).then_inc(small_in, 16)
            sp.dma_start(rows_all[:, :, :].rearrange("s l n -> s (l n)"),
                         c.loc["rows"].rearrange("(o l) n -> o (l n)", o=1).broadcast_to((S, DEPTH * (2 * LD + D)))).then_inc(small_in, 16)
            sp.dma_start(rot_all[:, :, :], c.loc["rotary"]).then_inc(small_in, 16)

            def load_w(i, name, dst, src, free_sem, free_at):
                if not (isinstance(i, int) and i == 0):
                    sp.wait_ge(free_sem, free_at)
                sp.dma_start(dst, src).then_inc(w_in[name], 16)

            def body(i):
                def layer(w):
                    return w[bass.ds(i, 1)].rearrange("o r n -> (o r) n")
                load_w(i, "wqkv", wqkv[:, :, :], tiled(layer(c.loc["Wqkv"])), qkv_made, 6 * i)
                load_w(i, "wo", wo[:, :, :], tiled(layer(c.loc["Wo"])), wo_made, i)
                load_w(i, "w1", w1[:, :, :], tiled(layer(c.loc["W1"])), h_made, 4 * i)
                src = layer(c.loc["W2"])
                load_w(i, "w2", w2[:, 0:FT - 1, :], tiled(src[0:(FT - 1) * P, :]), w2_made, i)
                sp.dma_start(w2[0:FLAST, FT - 1, :], src[(FT - 1) * P:FF, :]).then_inc(w_in["w2"], 16)
            body(0)
            with sp.Fori(1, DEPTH) as i:
                body(i)
            sp.wait_ge(w_in["w2"], 32 * DEPTH)

        @block.gpsimd
        def _(pool):
            pool.memset(shift[:, :], 0.0).then_inc(mask_step, 1)
            pool.memset(mask[:, :], 0.0).then_inc(mask_step, 1)
            pool.wait_ge(mask_step, 2)
            pool.affine_select(out=shift[:, :], in_=shift[:, :], compare_op=ALU.not_equal, fill=1.0,
                               base=-1, pattern=[[1, S]], channel_multiplier=-1).then_inc(made_mask, 1)
            pool.affine_select(out=mask[:, :], in_=mask[:, :], compare_op=ALU.is_ge, fill=MASKED,
                               base=0, pattern=[[-1, S]], channel_multiplier=1).then_inc(made_mask, 1)
            pool.wait_ge(made_mask, 2)
            pool.affine_select(out=mask[:, :], in_=mask[:, :], compare_op=ALU.is_ge, fill=MASKED,
                               base=WINDOW, pattern=[[1, S]], channel_multiplier=-1).then_inc(made_mask, 1)
            pool.wait_ge(small_in, 48)

            def body(i):
                if not (isinstance(i, int) and i == 0):
                    pool.wait_ge(layer_done, i)
                pool.tensor_copy(cols[:, :], cols_all[:, bass.ds(i, 1), :].rearrange("p o n -> p (o n)")).then_inc(cols_ready, 1)
                pool.tensor_copy(rows[:, :], rows_all[:, bass.ds(i, 1), :].rearrange("p o n -> p (o n)")).then_inc(cols_ready, 1)
                pool.wait_ge(cols_ready, 2 * i + 2)
                H = LD // 2
                for j, off in enumerate((QO, KO)):
                    pool.tensor_tensor(rot[:, 2 * j, :], rot_all[:, 2 * j, :], rows[:, off:off + LD], ALU.mult).then_inc(rot_ready, 1)
                    pool.tensor_tensor(rot[:, 2 * j + 1, 0:H], rot_all[:, 2 * j + 1, 0:H], rows[:, off + H:off + LD], ALU.mult).then_inc(rot_ready, 1)
                    pool.tensor_tensor(rot[:, 2 * j + 1, H:LD], rot_all[:, 2 * j + 1, H:LD], rows[:, off:off + H], ALU.mult).then_inc(rot_ready, 1)
            body(0)
            with pool.Fori(1, DEPTH) as i:
                body(i)

        def stay_awake(pe, bank, n):
            for _ in range(n):
                pe.transpose(c.bank(bank)[:, 0:P], c.ident[:, :], c.ident[:, :])

        @block.tensor
        def _(pe):
            pe.wait_ge(made_mask, 3)

            def body(i):
                pe.wait_ge(y_ready, i + 1)
                for k in range(KT):
                    mm = pe.transpose(c.bank(4)[:, k * S:(k + 1) * S], y[:, k * P:(k + 1) * P], c.ident[:, :])
                mm.then_inc(y_turned, 1)
                pe.wait_ge(tT_ready, i + 1)
                pe.wait_ge(w_in["wqkv"], 16 * i + 16)
                for u, b in enumerate((0, 1, 2, 3, 6, 7)):
                    for k in range(KT):
                        mm = pe.matmul(c.bank(b), tT[:, k, :], wqkv[:, k, u * 512:(u + 1) * 512], start=(k == 0), stop=(k == KT - 1))
                    mm.then_inc(qkv_made, 1)
                for j in range(2):
                    if j == 1:
                        stay_awake(pe, 4, 28)
                    pe.wait_ge(rotated, 2 * i + j + 1)
                    for t in range(LH // 2):
                        mm = pe.transpose(c.bank(2 * j + t // 4)[:, (t % 4) * S:(t % 4 + 1) * S],
                                          qk[j][:, 2 * t:2 * t + 2, :].rearrange("s h d -> s (h d)"), c.ident[:, :])
                    mm.then_inc(qk_turned, 1)
                pe.wait_ge(qkT_ready, 2 * i + 2)
                pe.wait_ge(v_kept, i + 1)
                for par in range(2):
                    for t in range(LH // 2):
                        lo = par * LD
                        mm = pe.matmul(c.bank(4 + 2 * par + t // 4)[:, (t % 4) * S:(t % 4 + 1) * S],
                                       qkT[0][lo:lo + LD, t, :], qkT[1][lo:lo + LD, t, :], start=True, stop=True)
                    mm.then_inc(scores_made, 1)
                stay_awake(pe, 0, 28)
                for hh in range(LH):
                    pe.wait_ge(scaled, LH * i + hh + 1)
                    mm = pe.transpose(c.bank(hh // 4)[:, (hh % 4) * S:(hh % 4 + 1) * S], sc[:, hh, :], c.ident[:, :])
                    if hh % 8 == 7:
                        mm.then_inc(p_turned, 1)
                for hh in range(LH):
                    if hh % 8 == 0:
                        pe.wait_ge(pT_ready, 2 * i + hh // 8 + 1)
                    par, t = hh // 8, hh % 8
                    h = 2 * t + par
                    mm = pe.matmul(c.bank(4 + t // 4)[par * LD:(par + 1) * LD, (t % 4) * S:(t % 4 + 1) * S],
                                   v[:, h * LD:(h + 1) * LD], pT[:, hh, :], start=True, stop=True)
                    if hh in (11, 15):
                        mm.then_inc(pv_made, 1)
                pe.wait_ge(w_in["wo"], 16 * i + 16)
                for t in range(INNER // P):
                    if t % 4 == 0:
                        pe.wait_ge(oT_ready, 2 * i + t // 4 + 1)
                    mm = pe.matmul(c.bank(0)[:, 0:D], oT[:, t, :], wo[:, t, :], start=(t == 0), stop=(t == INNER // P - 1))
                mm.then_inc(wo_made, 1)
                pe.wait_ge(mid_ready, i + 1)
                pe.matmul(c.bank(1)[:, 0:P], shift[:, :], y[:, P:D], start=True, stop=True).then_inc(shift_made, 1)
                stay_awake(pe, 7, 10)
                norm.turn(pe, i, c.xn, c.bank(2))
                pe.wait_ge(norm.outT, i + 1)
                pe.wait_ge(w_in["w1"], 16 * i + 16)
                for u in range(2 * FT):
                    t = u % FT
                    w0 = t * P + (FF if u < FT else 0)
                    m = tile_rows(u)
                    for k in range(KT):
                        mm = pe.matmul(h_tile(u, m), w1[:, k, w0:w0 + m], c.xT[:, k, :],
                                       start=(k == 0), stop=(k == KT - 1))
                    if u % FT in (3, FT - 1):
                        mm.then_inc(h_made, 1)
                pe.wait_ge(hT_ready, i + 1)
                pe.wait_ge(w_in["w2"], 32 * i + 32)
                for t in range(FT):
                    m = tile_rows(t)
                    mm = pe.matmul(c.bank(6)[:, 0:D], hT[0:m, t, :], w2[0:m, t, :], start=(t == 0), stop=(t == FT - 1))
                mm.then_inc(w2_made, 1)
                stay_awake(pe, 0, 4)
            body(0)
            with pe.Fori(1, DEPTH) as i:
                body(i)

        @block.scalar
        def _(act):
            norm0.scalar(act, 0)

            def body(i):
                for j in range(2):
                    act.wait_ge(qkv_made, 6 * i + 2 * j + 2)
                    act.activation(sq[:, j * INNER:(j + 1) * INNER].rearrange("s (b n) -> s b n", b=2), c.ps[:, 2 * j:2 * j + 2, :],
                                   ACT.Square).then_inc(squared, 1)
                def root(j):
                    half = norms[:, j * LH:(j + 1) * LH]
                    act.wait_ge(normed, 2 * i + 2 - j)
                    act.activation(half, half, ACT.Sqrt).then_inc(rooted, 1)
                root(1)
                act.wait_ge(qkv_made, 6 * i + 6)
                act.copy(v[:, :].rearrange("s (b n) -> s b n", b=2), c.ps[:, 6:8, :]).then_inc(v_kept, 1)
                root(0)
                for hh in range(LH):
                    if hh % 8 == 0:
                        act.wait_ge(max_ready, 2 * i + hh // 8 + 1)
                    act.activation(sc[:, hh, :], sc[:, hh, :], ACT.Exp, bias=mx[:, hh:hh + 1], scale=q_scale[:, hh:hh + 1],
                                   accum_out=total[:, hh:hh + 1]).then_inc(exp_ready, 1)
                norm.scalar(act, i)
                for t in range(FT):
                    m = tile_rows(t)
                    act.wait_ge(h_made, 4 * i + h_signals(t))
                    act.activation(gate[0:m, t, :], h_tile(t, m), ACT.Gelu,
                                   bias=cols[0:m, 2 * KT + t:2 * KT + t + 1]).then_inc(gelu_ready, 1)
                act.activation(spare[:, :], c.eps[:, :], ACT.Sqrt).then_inc(table_in, 1)
                act.wait_ge(table_in, i + 1)
            body(0)
            with act.Fori(1, DEPTH) as i:
                body(i)

        @block.vector
        def _(dve):
            STEPS = 19
            first = Chain(dve, steps)
            first(dve.memset(tT[:, 1, 0:1], 0.0))
            dve.wait_ge(made_mask, 3)
            first(dve.memset(shifted[:, :], 0.0))
            norm0.vector(dve, 0, c.x[:, :], y[:, :])
            dve.wait_ge(norm0.out, 1)
            dve.sem_inc(y_ready, 1)

            def body(i):
                chain = Chain(dve, steps, STEPS * i + 2)
                dve.wait_ge(y_turned, i + 1)
                dve.tensor_copy(tT[:, 0, :], c.bank(4)[:, 0:S]).then_inc(steps, 1)
                chain.n += 1
                dve.tensor_copy(tT[:, 1, 1:S], c.bank(4)[:, S:2 * S - 1]).then_inc(tT_ready, 1)
                def norm_sum(j):
                    dve.wait_ge(squared, 2 * i + j + 1)
                    dve.reduce_sum(norms[:, j * LH:(j + 1) * LH], sq[:, j * INNER:(j + 1) * INNER].rearrange("s (h d) -> s h d", d=LD), AX_X).then_inc(normed, 1)

                def inverse_norm(j):
                    half = norms[:, j * LH:(j + 1) * LH]
                    dve.wait_ge(rooted, 2 * i + 2 - j)
                    chain(dve.tensor_scalar(half, half, 1e-12, None, ALU.max))
                    chain(dve.reciprocal(half, half))

                def turned_halves(j, src):
                    dve.tensor_tensor(qb[:, :, 0:H], src[:, :, H:LD], rot[:, 2 * j + 1, 0:H].unsqueeze(1).broadcast_to((S, LH, H)), ALU.mult)
                    chain(dve.tensor_tensor(qb[:, :, H:LD], src[:, :, 0:H], rot[:, 2 * j + 1, H:LD].unsqueeze(1).broadcast_to((S, LH, H)), ALU.mult))

                def straight(j, src):
                    chain(dve.tensor_tensor(qa[:, :, :], src[:, :, :], rot[:, 2 * j, :].unsqueeze(1).broadcast_to((S, LH, LD)), ALU.mult))

                H = LD // 2
                q_src, k_src = (c.ps[:, 2 * j:2 * j + 2, :].rearrange("s b (h d) -> s (b h) d", d=LD) for j in range(2))
                dve.wait_ge(rot_ready, 6 * i + 6)
                dve.wait_ge(squared, 2 * i + 1)
                turned_halves(0, q_src)
                straight(0, q_src)
                dve.tensor_tensor(qk[0][:, :, :], qa[:, :, :], qb[:, :, :], ALU.add).then_inc(rotated, 1)
                dve.wait_ge(rotated, 2 * i + 1)
                norm_sum(1)
                turned_halves(1, k_src)
                straight(1, k_src)
                chain(dve.tensor_tensor(qa[:, :, :], qa[:, :, :], qb[:, :, :], ALU.add))
                inverse_norm(1)
                dve.tensor_tensor(qk[1][:, :, :], qa[:, :, :], norms[:, LH:2 * LH].unsqueeze(2).broadcast_to((S, LH, LD)), ALU.mult).then_inc(rotated, 1)
                for j in range(2):
                    dve.wait_ge(qk_turned, 2 * i + j + 1)
                    dve.tensor_copy(qkT[j][:, :, :], c.ps[:, 2 * j:2 * j + 2, :].rearrange("p b (t s) -> p (b t) s", s=S)).then_inc(qkT_ready, 1)
                norm_sum(0)
                inverse_norm(0)
                chain(dve.tensor_scalar(q_scale[:, :].rearrange("s (a t) -> s a t", a=2), norms[:, 0:LH].rearrange("s (t a) -> s a t", a=2),
                                        QK_SCALE, None, ALU.mult))
                for half in range(2):
                    hs = slice(8 * half, 8 * half + 8)
                    dve.wait_ge(scores_made, 2 * i + half + 1)
                    chain(dve.tensor_tensor(sc[:, hs, :], c.ps[:, 4 + 2 * half:6 + 2 * half, :].rearrange("p b (t s) -> p (b t) s", s=S),
                                            mask[:, :].unsqueeze(1).broadcast_to((S, 8, S)), ALU.add))
                    chain(dve.tensor_reduce(mx[:, hs], sc[:, hs, :], AX_X, ALU.max, negate=True))
                    dve.tensor_tensor(mx[:, hs], mx[:, hs], q_scale[:, hs], ALU.mult).then_inc(max_ready, 1)
                for hh in range(LH + 1):
                    if hh < LH:
                        dve.wait_ge(exp_ready, LH * i + hh + 1)
                        dve.reciprocal(inv[:, hh:hh + 1], total[:, hh:hh + 1]).then_inc(inverted, 1)
                    if hh > 0:
                        dve.wait_ge(inverted, LH * i + hh)
                        dve.tensor_scalar(sc[:, hh - 1, :], sc[:, hh - 1, :], inv[:, hh - 1:hh], None, ALU.mult).then_inc(scaled, 1)
                    if hh == 12:
                        dve.wait_ge(p_turned, 2 * i + 1)
                        dve.tensor_copy(pT[:, 0:8, :], c.ps[:, 0:2, :].rearrange("p b (t s) -> p (b t) s", s=S)).then_inc(pT_ready, 1)
                dve.wait_ge(p_turned, 2 * i + 2)
                dve.tensor_copy(pT[:, 8:16, :], c.ps[:, 2:4, :].rearrange("p b (t s) -> p (b t) s", s=S)).then_inc(pT_ready, 1)
                for half in range(2):
                    dve.wait_ge(pv_made, 2 * i + half + 1)
                    dve.tensor_copy(oT[:, 4 * half:4 * half + 4, :], c.bank(4 + half).rearrange("p (t s) -> p t s", s=S)).then_inc(oT_ready, 1)
                dve.wait_ge(wo_made, i + 1)
                chain(dve.tensor_tensor(y[:, :], y[:, :], c.bank(0)[:, 0:D], ALU.add))
                dve.sem_inc(mid_ready, 1)
                dve.tensor_copy(shifted[:, 0:P], y[:, 0:P])
                dve.wait_ge(shift_made, i + 1)
                chain(dve.tensor_copy(shifted[:, P:D], c.bank(1)[:, 0:P]))
                norm.vector(dve, i, shifted[:, :], c.xn[:, :])
                dve.wait_ge(norm.turned, i + 1)
                for k in range(KT):
                    ins = dve.tensor_scalar(c.xT[:, k, :], c.bank(2)[:, k * S:(k + 1) * S], cols[:, k:k + 1], cols[:, KT + k:KT + k + 1], ALU.mult, ALU.add)
                    if k == KT - 1:
                        ins.then_inc(norm.outT, 1)
                for t in range(FT):
                    m = tile_rows(t)
                    u = FT + t
                    dve.wait_ge(h_made, 4 * i + h_signals(u))
                    dve.wait_ge(gelu_ready, FT * i + t + 1)
                    ins = dve.scalar_tensor_tensor(out=hT[0:m, t, :], in0=h_tile(u, m),
                                                   scalar=cols[0:m, 2 * KT + u:2 * KT + u + 1], in1=gate[0:m, t, :], op0=ALU.add, op1=ALU.mult)
                ins.then_inc(hT_ready, 1)
                chain(dve.tensor_tensor(y[:, :], y[:, :], rows[:, B2:B2 + D], ALU.add))
                dve.wait_ge(w2_made, i + 1)
                chain(dve.tensor_tensor(y[:, :], y[:, :], c.bank(6)[:, 0:D], ALU.add))
                dve.sem_inc(y_ready, 1)
                dve.sem_inc(layer_done, 1)
                assert chain.n == STEPS, chain.n
            body(0)
            with dve.Fori(1, DEPTH) as i:
                body(i)
            dve.tensor_tensor(c.x[:, :], c.x[:, :], y[:, :], ALU.add).then_inc(layer_done, 1)
            dve.wait_ge(layer_done, DEPTH + 1)



def lay_out_local(t):
    import numpy as _np
    b1 = _np.zeros((2, FT * P, DEPTH), t["b1"].dtype)
    b1[0, 0:FF] = t["b1"][:, FF:].T
    b1[1, 0:FF] = t["b1"][:, :FF].T
    cols = [t[n].reshape(DEPTH, KT, P).transpose(2, 0, 1) for n in ("ln_g", "ln_b")]
    cols.append(b1.reshape(2 * FT, P, DEPTH).transpose(1, 2, 0))
    return {"Wqkv": t["Wqkv"], "Wo": t["Wo"], "W1": t["W1"], "W2": t["W2"], "rotary": rotary_tables(),
            "cols": _np.concatenate(cols, 2), "rows": _np.concatenate([t["q_scale"], t["k_scale"], t["b2"]], 1)}


RH = 2
LEVELS = S.bit_length() - 1


def level_masks():
    import numpy as np
    i = np.arange(S)
    out = [((i[None, :] >> l) == (i[:, None] >> l) + 1) & (((i[None, :] >> l) & 1) == 1) for l in range(LEVELS)]
    out.append(np.eye(S, dtype=bool))
    return np.stack(out, 1).astype(np.float32)


def gated_recurrence(nc, c):
    with ExitStack() as ctx:
        def sb(nm, shape):
            return ctx.enter_context(nc.sbuf_tensor(f"rec_{nm}", shape, F32))

        def sem(nm):
            return c.sem(f"rec_{nm}")

        w = {n: sb(f"w{n}", [P, KT, D]) for n in "qkvo"}
        gates = sb("gates", [P, 4, RH])
        masks = sb("masks", [S, LEVELS + 1, S])
        qT, vT = sb("qT", [P, RH, S]), sb("vT", [P, RH, S])
        kn, kT = sb("kn", [S, D]), sb("kT", [P, RH, S])
        ksum, sq = sb("ksum", [S, RH]), sb("sq", [S, D])
        gamma, lam = sb("gamma", [P, RH, S]), sb("lam", [P, RH, S])
        decay = [sb(f"decay{l}", [P, RH * S]) for l in range(LEVELS)]
        wk = [sb(f"wk{l}", [P, RH * S]) for l in range(LEVELS)]
        am = sb("am", [S, RH, LEVELS + 1, S])
        wkN = [sb(f"wkN{l}", [S, RH, P]) for l in range(LEVELS)]
        yT, t = sb("yT", [P, RH, S]), sb("t", [P, RH, S])
        norm = Norm(c, "rec_norm")
        w_in, proj_made, qv_kept, squared = sem("w_in"), sem("proj_made"), sem("qv_kept"), sem("squared")
        rooted, kn_ready, k_turned, kT_ready = sem("rooted"), sem("kn_ready"), sem("k_turned"), sem("kT_ready")
        gated, steps, a_made = sem("gates_ready"), sem("steps"), sem("a_made")
        decay_ready, wk_step, wk_ready = sem("decay_ready"), sem("wk_step"), sem("wk_ready")
        wk_turned, wkN_ready, am_ready, level_made, level_used = sem("wk_turned"), sem("wkN_ready"), sem("am_ready"), sem("level_made"), sem("level_used")
        yT_ready, out_made = sem("yT_ready"), sem("out_made")
        block = ctx.enter_context(nc.Block())

        def pair(ap, l):
            return ap.rearrange("p (b a r) -> p b a r", a=2, r=1 << l)

        @block.sync
        def _(sp):
            for n in "kqvo":
                sp.dma_start(w[n][:, :, :], c.rec[f"W{n}"]).then_inc(w_in, 16)
            sp.dma_start(gates[:, :, :], c.rec["gates"]).then_inc(w_in, 16)
            sp.dma_start(masks[:, :, :], c.rec["masks"]).then_inc(w_in, 16)
            sp.wait_ge(w_in, 96)

        @block.tensor
        def _(pe):
            norm.turn(pe, 0, c.xn, c.bank(4))
            pe.wait_ge(norm.outT, 1)
            pe.wait_ge(w_in, 96)
            for k in range(KT):
                mm = pe.matmul(c.bank(0)[:, 0:D], c.xT[:, k, :], w["k"][:, k, :], start=(k == 0), stop=(k == KT - 1))
            mm.then_inc(proj_made, 1)
            for i, n in enumerate("qv"):
                for h in range(RH):
                    for k in range(KT):
                        mm = pe.matmul(c.bank(1 + i)[:, h * S:(h + 1) * S], w[n][:, k, h * P:(h + 1) * P], c.xT[:, k, :],
                                       start=(k == 0), stop=(k == KT - 1))
                mm.then_inc(proj_made, 1)
            pe.wait_ge(qv_kept, 2)
            for h in range(RH):
                mm = pe.matmul(c.bank(3)[:, h * S:(h + 1) * S], vT[:, h, :], qT[:, h, :], start=True, stop=True)
            mm.then_inc(a_made, 1)
            pe.wait_ge(kn_ready, RH)
            for h in range(RH):
                mm = pe.transpose(c.bank(4)[:, h * S:(h + 1) * S], kn[:, h * P:(h + 1) * P], c.ident[:, :])
            mm.then_inc(k_turned, 1)

            def turn(l):
                pe.wait_ge(wk_ready, l + 1)
                if l >= 2:
                    pe.wait_ge(wkN_ready, l - 1)
                for h in range(RH):
                    mm = pe.transpose(c.bank(l % 2)[:, h * P:(h + 1) * P], wk[l][:, h * S:(h + 1) * S], c.ident[:, :])
                mm.then_inc(wk_turned, 1)

            def level(n, l, j):
                if l == 0:
                    pe.wait_ge(am_ready, RH)
                pe.wait_ge(wkN_ready, l + 1)
                if n >= 2:
                    pe.wait_ge(level_used, n - 1)
                for h in range(RH):
                    mm = pe.matmul(c.bank(6 + n % 2)[:, h * S:(h + 1) * S], wkN[l][:, h, :], am[:, h, j, :], start=True, stop=True)
                mm.then_inc(level_made, 1)

            turn(0)
            turn(1)
            level(0, 0, LEVELS)
            for l in range(LEVELS):
                if l + 2 < LEVELS:
                    turn(l + 2)
                level(l + 1, l, l)
            pe.wait_ge(yT_ready, 1)
            for k in range(KT):
                mm = pe.matmul(c.bank(5)[:, 0:D], yT[:, k, :], w["o"][:, k, :], start=(k == 0), stop=(k == KT - 1))
            mm.then_inc(out_made, 1)

        @block.scalar
        def _(act):
            norm.scalar(act, 0)
            act.wait_ge(proj_made, 1)
            for h in range(RH):
                act.activation(sq[:, h * P:(h + 1) * P], c.bank(0)[:, h * P:(h + 1) * P], ACT.Square, accum_out=ksum[:, h:h + 1]).then_inc(squared, 1)
            act.wait_ge(squared, RH)
            act.activation(ksum[:, :], ksum[:, :], ACT.Sqrt).then_inc(rooted, 1)
            act.wait_ge(w_in, 96)
            act.wait_ge(kT_ready, 1)
            for h in range(RH):
                act.activation(gamma[:, h, :], kT[:, h, :], ACT.Sigmoid, bias=gates[:, 1, h:h + 1], scale=gates[:, 0, h:h + 1]).then_inc(gated, 1)
                act.activation(lam[:, h, :], kT[:, h, :], ACT.Sigmoid, bias=gates[:, 3, h:h + 1], scale=gates[:, 2, h:h + 1]).then_inc(gated, 1)
            for l in range(LEVELS):
                act.wait_ge(wk_turned, l + 1)
                act.copy(wkN[l][:, :, :].rearrange("s h k -> s (h k)"), c.bank(l % 2)[:, 0:RH * P]).then_inc(wkN_ready, 1)

        @block.gpsimd
        def _(pool):
            for l in range(1, LEVELS):
                pool.wait_ge(decay_ready, l)
                pool.wait_ge(wk_ready, l)
                old, new, d = pair(wk[l - 1][:, :], l - 1), pair(wk[l][:, :], l - 1), pair(decay[l - 1][:, :], l - 1)
                r = 1 << (l - 1)
                pool.tensor_copy(new[:, :, 1, :], old[:, :, 1, :]).then_inc(wk_step, 1)
                pool.wait_ge(wk_step, l)
                pool.tensor_tensor(new[:, :, 0, :], old[:, :, 0, :], d[:, :, 1, r - 1:r].broadcast_to((P, S // r, r)), ALU.mult).then_inc(wk_ready, 1)

        @block.vector
        def _(dve):
            chain = Chain(dve, steps)
            norm.vector(dve, 0, c.x[:, :], c.xn[:, :])
            norm.keep(dve, 0, c.bank(4), c.xT[:, :, :])
            dve.wait_ge(rooted, 1)
            chain(dve.tensor_scalar(ksum[:, :], ksum[:, :], 1e-12, None, ALU.max))
            chain(dve.reciprocal(ksum[:, :], ksum[:, :]))
            for h in range(RH):
                dve.tensor_scalar(kn[:, h * P:(h + 1) * P], c.bank(0)[:, h * P:(h + 1) * P], ksum[:, h:h + 1], None, ALU.mult).then_inc(kn_ready, 1)
            for i, dst in enumerate((qT, vT)):
                dve.wait_ge(proj_made, 2 + i)
                dve.tensor_copy(dst[:, :, :].rearrange("p h s -> p (h s)"), c.bank(1 + i)[:, 0:RH * S]).then_inc(qv_kept, 1)
            dve.wait_ge(k_turned, 1)
            dve.tensor_copy(kT[:, :, :].rearrange("p h s -> p (h s)"), c.bank(4)[:, 0:RH * S]).then_inc(kT_ready, 1)
            dve.wait_ge(a_made, 1)
            for h in range(RH):
                dve.tensor_tensor(am[:, h, :, :], c.bank(3)[:, h * S:(h + 1) * S].unsqueeze(1).broadcast_to((S, LEVELS + 1, S)), masks[:, :, :], ALU.mult).then_inc(am_ready, 1)
            dve.wait_ge(gated, 2 * RH)
            flat = [g[:, :, :].rearrange("p h s -> p (h s)") for g in (gamma, lam, kT)]
            chain(dve.tensor_scalar(flat[1], flat[1], -1.0, 1.0, ALU.mult, ALU.add))
            dve.tensor_tensor(decay[0][:, :], flat[1], flat[0], ALU.mult).then_inc(decay_ready, 1)
            dve.wait_ge(decay_ready, 1)
            chain(dve.tensor_scalar(flat[0], decay[0][:, :], -1.0, 1.0, ALU.mult, ALU.add))
            dve.tensor_tensor(wk[0][:, :], flat[0], flat[2], ALU.mult).then_inc(wk_ready, 1)
            for l in range(1, LEVELS):
                old, new = pair(decay[l - 1][:, :], l - 1), pair(decay[l][:, :], l - 1)
                r = 1 << (l - 1)
                dve.tensor_copy(new[:, :, 0, :], old[:, :, 0, :])
                dve.tensor_tensor(new[:, :, 1, :], old[:, :, 1, :], old[:, :, 0, r - 1:r].broadcast_to((P, S // r, r)), ALU.mult).then_inc(decay_ready, 1)
                dve.wait_ge(decay_ready, l + 1)
            dve.wait_ge(level_made, 1)
            y = yT[:, :, :].rearrange("p h s -> p (h s)")
            tf = t[:, :, :].rearrange("p h s -> p (h s)")
            dve.tensor_copy(y, c.bank(6)[:, 0:RH * S]).then_inc(level_used, 1)
            for l in range(LEVELS):
                dve.wait_ge(level_made, l + 2)
                dve.tensor_tensor(tf, c.bank(6 + (l + 1) % 2)[:, 0:RH * S], decay[l][:, :], ALU.mult).then_inc(level_used, 1)
                dve.wait_ge(level_used, l + 2)
                ins = dve.tensor_tensor(y, y, tf, ALU.add)
                if l < LEVELS - 1:
                    chain(ins)
            ins.then_inc(yT_ready, 1)
            dve.wait_ge(out_made, 1)
            chain(dve.tensor_tensor(c.x[:, :], c.x[:, :], c.bank(5)[:, 0:D], ALU.add))



def lay_out_recurrence(t):
    import numpy as _np
    return {**{f"W{n}": t[f"W{n}"].T for n in "qkvo"}, "masks": level_masks(),
            "gates": _np.stack([t[n].T for n in ("W_gamma", "b_gamma", "W_lambda", "b_lambda")], 1)}


NE = 8
EF = 1024
ET = EF // P
TOP = 2


def experts(nc, c):
    with ExitStack() as ctx:
        def sb(nm, shape):
            return ctx.enter_context(nc.sbuf_tensor(f"moe_{nm}", shape, F32))

        def sem(nm):
            return c.sem(f"moe_{nm}")

        gw, b2 = sb("gate_w", [P, KT, NE]), sb("b2", [NE, D])
        w1 = [sb(f"w1_{i}", [P, KT, EF]) for i in range(2)]
        w2 = [sb(f"w2_{i}", [P, ET, D]) for i in range(2)]
        b1 = [sb(f"b1_{i}", [P, ET]) for i in range(2)]
        hT = [sb(f"hT{i}", [P, ET, S]) for i in range(2)]
        earlier = sb("earlier", [S, NE, NE])
        logit, ex = sb("logit", [S, NE]), sb("ex", [S, NE])
        beats, ties = sb("beats", [S, NE, NE]), sb("ties", [S, NE, NE])
        rank, neg_max, total = sb("rank", [S, NE]), sb("neg_max", [S, 1]), sb("total", [S, 1])
        combine, combT = sb("combine", [S, NE]), sb("combT", [NE, S])
        share = [sb(f"share{i}", [S, 1]) for i in range(2)]
        norm = Norm(c, "moe_norm")
        small_in, filled, earlier_made = sem("small_in"), sem("filled"), sem("earlier_made")
        up_in, down_in = [sem(f"up_in{i}") for i in range(2)], [sem(f"down_in{i}") for i in range(2)]
        logits_made, max_ready, ex_ready, steps = sem("logits_made"), sem("max_ready"), sem("ex_ready"), sem("steps")
        combine_ready, comb_turned, combT_ready, bias_made = sem("combine_ready"), sem("comb_turned"), sem("combT_ready"), sem("bias_made")
        up_made, h_ready, down_made, added, shared = sem("up_made"), sem("h_ready"), sem("down_made"), sem("added"), sem("shared")
        block = ctx.enter_context(nc.Block())

        @block.sync
        def _(sp):
            sp.dma_start(gw[:, :, :], c.moe["gate_w"]).then_inc(small_in, 16)
            sp.dma_start(b2[:, :], c.moe["b2"]).then_inc(small_in, 16)

            def load(e, par):
                def one(w):
                    return w[bass.ds(e, 1)].rearrange("o r n -> (o r) n")
                first = isinstance(e, int) and e < 2
                if not first:
                    sp.wait_ge(h_ready, ET * (e - 1))
                sp.dma_start(w1[par][:, :, :], tiled(one(c.moe["W1"]))).then_inc(up_in[par], 16)
                sp.dma_start(b1[par][:, :], one(c.moe["b1"])).then_inc(up_in[par], 16)
                if not first:
                    sp.wait_ge(down_made, e - 1)
                sp.dma_start(w2[par][:, :, :], tiled(one(c.moe["W2"]))).then_inc(down_in[par], 16)
            for par in range(2):
                load(par, par)
            with sp.Fori(1, NE // 2) as i:
                for par in range(2):
                    load(2 * i + par, par)

        @block.gpsimd
        def _(pool):
            pool.memset(earlier[:, :, :], 1.0).then_inc(filled, 1)
            pool.wait_ge(filled, 1)
            pool.affine_select(out=earlier[:, :, :], in_=earlier[:, :, :], compare_op=ALU.is_gt, fill=0.0,
                               base=0, pattern=[[1, NE], [-1, NE]], channel_multiplier=0).then_inc(earlier_made, 1)

        @block.tensor
        def _(pe):
            norm.turn(pe, 0, c.xn, c.bank(4))
            pe.wait_ge(norm.outT, 1)
            pe.wait_ge(small_in, 32)
            for k in range(KT):
                mm = pe.matmul(c.bank(6)[:, 0:NE], c.xT[:, k, :], gw[:, k, :], start=(k == 0), stop=(k == KT - 1))
            mm.then_inc(logits_made, 1)

            def up(e, par, i):
                pe.wait_ge(up_in[par], 32 * i + 32)
                if not (isinstance(e, int) and e < 2):
                    pe.wait_ge(h_ready, ET * (e - 1))
                for t in range(ET):
                    for k in range(KT):
                        mm = pe.matmul(c.bank(2 * par + t // 4)[:, (t % 4) * S:(t % 4 + 1) * S], w1[par][:, k, t * P:(t + 1) * P], c.xT[:, k, :],
                                       start=(k == 0), stop=(k == KT - 1))
                    if t % 4 == 3:
                        mm.then_inc(up_made, 1)

            def down(e, par, i):
                pe.wait_ge(down_in[par], 16 * i + 16)
                if not (isinstance(e, int) and e < 2):
                    pe.wait_ge(added, e - 1)
                for t in range(ET):
                    pe.wait_ge(h_ready, ET * e + t + 1)
                    mm = pe.matmul(c.bank(4 + par)[:, 0:D], hT[par][:, t, :], w2[par][:, t, :], start=(t == 0), stop=(t == ET - 1))
                mm.then_inc(down_made, 1)

            up(0, 0, 0)
            pe.wait_ge(combine_ready, 1)
            pe.transpose(c.bank(7)[0:NE, 0:S], combine[:, :], c.ident[:, :]).then_inc(comb_turned, 1)
            pe.wait_ge(combT_ready, 1)
            pe.matmul(c.bank(6)[:, D:2 * D], combT[:, :], b2[:, :], start=True, stop=True).then_inc(bias_made, 1)

            def body(i):
                for par in range(2):
                    e = 2 * i + par
                    if not (isinstance(e, int) and e == NE - 1):
                        up(e + 1, 1 - par, i + par)
                    down(e, par, i)
            body(0)
            with pe.Fori(1, NE // 2 - 1) as i:
                body(i)
            body(NE // 2 - 1)

        @block.scalar
        def _(act):
            norm.scalar(act, 0)
            act.wait_ge(max_ready, 1)
            act.activation(ex[:, :], logit[:, :], ACT.Exp, bias=neg_max[:, 0:1]).then_inc(ex_ready, 1)

            def body(i):
                for par in range(2):
                    e = 2 * i + par
                    act.wait_ge(up_in[par], 32 * i + 32)
                    if not (isinstance(e, int) and e < 2):
                        act.wait_ge(down_made, e - 1)
                    for t in range(ET):
                        act.wait_ge(up_made, 2 * e + t // 4 + 1)
                        act.activation(hT[par][:, t, :], c.bank(2 * par + t // 4)[:, (t % 4) * S:(t % 4 + 1) * S], ACT.Gelu,
                                       bias=b1[par][:, t:t + 1]).then_inc(h_ready, 1)
            body(0)
            with act.Fori(1, NE // 2) as i:
                body(i)

        @block.vector
        def _(dve):
            chain = Chain(dve, steps)
            norm.vector(dve, 0, c.x[:, :], c.xn[:, :])
            norm.keep(dve, 0, c.bank(4), c.xT[:, :, :])
            dve.wait_ge(logits_made, 1)
            chain(dve.tensor_copy(logit[:, :], c.bank(6)[:, 0:NE]))
            dve.tensor_reduce(neg_max[:, :], logit[:, :], AX_X, ALU.max, negate=True).then_inc(max_ready, 1)
            other = logit[:, :].unsqueeze(1).broadcast_to((S, NE, NE))
            own = logit[:, :].unsqueeze(2).broadcast_to((S, NE, NE))
            chain(dve.tensor_tensor(beats[:, :, :], other, own, ALU.is_gt))
            chain(dve.tensor_tensor(ties[:, :, :], other, own, ALU.is_equal))
            dve.wait_ge(earlier_made, 1)
            chain(dve.tensor_tensor(ties[:, :, :], ties[:, :, :], earlier[:, :, :], ALU.mult))
            chain(dve.tensor_tensor(beats[:, :, :], beats[:, :, :], ties[:, :, :], ALU.add))
            chain(dve.reduce_sum(rank[:, :], beats[:, :, :], AX_X))
            chain(dve.tensor_scalar(rank[:, :], rank[:, :], float(TOP), None, ALU.is_lt))
            dve.wait_ge(ex_ready, 1)
            chain(dve.tensor_tensor(combine[:, :], ex[:, :], rank[:, :], ALU.mult))
            chain(dve.reduce_sum(total[:, :], combine[:, :], AX_X))
            chain(dve.reciprocal(total[:, :], total[:, :]))
            dve.tensor_scalar(combine[:, :], combine[:, :], total[:, 0:1], None, ALU.mult).then_inc(combine_ready, 1)
            dve.wait_ge(comb_turned, 1)
            dve.tensor_copy(combT[:, :], c.bank(7)[0:NE, 0:S]).then_inc(combT_ready, 1)
            dve.wait_ge(bias_made, 1)
            chain(dve.tensor_tensor(c.x[:, :], c.x[:, :], c.bank(6)[:, D:2 * D], ALU.add))

            def body(i):
                for par in range(2):
                    e = 2 * i + par
                    if not (isinstance(e, int) and e == 0):
                        dve.wait_ge(added, e)
                    dve.tensor_copy(share[par][:, :], combine[:, bass.ds(e, 1)]).then_inc(shared, 1)
                    dve.wait_ge(shared, e + 1)
                    dve.wait_ge(down_made, e + 1)
                    dve.scalar_tensor_tensor(out=c.x[:, :], in0=c.bank(4 + par)[:, 0:D], scalar=share[par][:, 0:1], in1=c.x[:, :],
                                             op0=ALU.mult, op1=ALU.add).then_inc(added, 1)
            body(0)
            with dve.Fori(1, NE // 2) as i:
                body(i)
            dve.wait_ge(added, NE)



def lay_out_experts(t):
    return {"gate_w": t["gate_w"], "W1": t["W1"], "b1": t["b1"].reshape(NE, ET, P).transpose(0, 2, 1), "W2": t["W2"], "b2": t["b2"]}


CF = 1024
CT = CF // P


def biased_feed_forward(nc, c):
    with ExitStack() as ctx:
        def sb(nm, shape):
            return ctx.enter_context(nc.sbuf_tensor(f"cff_{nm}", shape, F32))

        def sem(nm):
            return c.sem(f"cff_{nm}")

        w1, w2 = sb("w1", [P, KT, CF]), sb("w2", [P, CT, D])
        cols, rows = sb("cols", [P, 2 * KT + CT]), sb("rows", [S, 3, D])
        hT = sb("hT", [P, CT, S])
        norm = Norm(c, "cff_norm")
        w_in, up_made, h_ready, down_made, steps = sem("w_in"), sem("up_made"), sem("h_ready"), sem("down_made"), sem("steps")
        block = ctx.enter_context(nc.Block())

        @block.sync
        def _(sp):
            sp.dma_start(cols[:, :], c.cff["cols"]).then_inc(w_in, 16)
            sp.dma_start(rows[:, :, :].rearrange("s l n -> s (l n)"),
                         c.cff["rows"].rearrange("(o l) n -> o (l n)", o=1).broadcast_to((S, 3 * D))).then_inc(w_in, 16)
            sp.dma_start(w1[:, :, :], c.cff["W1"]).then_inc(w_in, 16)
            sp.dma_start(w2[:, :, :], c.cff["W2"]).then_inc(w_in, 16)

        @block.tensor
        def _(pe):
            norm.turn(pe, 0, c.xn, c.bank(4))
            pe.wait_ge(norm.outT, 1)
            pe.wait_ge(w_in, 64)
            for t in range(CT):
                for k in range(KT):
                    mm = pe.matmul(c.bank(t // 4)[:, (t % 4) * S:(t % 4 + 1) * S], w1[:, k, t * P:(t + 1) * P], c.xT[:, k, :],
                                   start=(k == 0), stop=(k == KT - 1))
                if t % 4 == 3:
                    mm.then_inc(up_made, 1)
            for t in range(CT):
                pe.wait_ge(h_ready, t + 1)
                mm = pe.matmul(c.bank(5)[:, 0:D], hT[:, t, :], w2[:, t, :], start=(t == 0), stop=(t == CT - 1))
            mm.then_inc(down_made, 1)

        @block.scalar
        def _(act):
            norm.scalar(act, 0)
            act.wait_ge(w_in, 64)
            for t in range(CT):
                act.wait_ge(up_made, t // 4 + 1)
                act.activation(hT[:, t, :], c.bank(t // 4)[:, (t % 4) * S:(t % 4 + 1) * S], ACT.Gelu,
                               bias=cols[:, 2 * KT + t:2 * KT + t + 1]).then_inc(h_ready, 1)
            norm.scalar(act, 1)

        @block.vector
        def _(dve):
            chain = Chain(dve, steps)
            norm.vector(dve, 0, c.z[:, :], c.xn[:, :])
            dve.wait_ge(w_in, 64)
            dve.wait_ge(norm.turned, 1)
            for k in range(KT):
                ins = dve.tensor_scalar(c.xT[:, k, :], c.bank(4)[:, k * S:(k + 1) * S], cols[:, k:k + 1], cols[:, KT + k:KT + k + 1], ALU.mult, ALU.add)
            ins.then_inc(norm.outT, 1)
            chain(dve.tensor_tensor(c.z[:, :], c.z[:, :], rows[:, 0, :], ALU.add))
            dve.wait_ge(down_made, 1)
            chain(dve.tensor_tensor(c.z[:, :], c.z[:, :], c.bank(5)[:, 0:D], ALU.add))
            norm.vector(dve, 1, c.z[:, :], c.xn[:, :])
            dve.wait_ge(norm.out, 2)
            chain(dve.tensor_tensor(c.xn[:, :], c.xn[:, :], rows[:, 1, :], ALU.mult))
            chain(dve.tensor_tensor(c.xn[:, :], c.xn[:, :], rows[:, 2, :], ALU.add))
            chain(dve.tensor_tensor(c.x[:, :], c.x[:, :], c.xn[:, :], ALU.add))


def program(nc, a, out):
    with ExitStack() as ctx:
        c = Core(nc, ctx)
        c.x_dram, c.ctxT = a["x"], a["ctxT"]
        c.T = c.ctxT.shape[1]
        c.z = c.sb("z_rows", [S, D])
        c.wkA, c.wkD, c.wvA, c.wvD = (tiled(a[k]) for k in ("wkA", "wkD", "wvA", "wvD"))
        c.k1_dram = nc.dram_tensor("keys1_scratch", (SPLIT, KVA, c.T), F32).ap()
        c.k2_dram = nc.dram_tensor("keys2_scratch", (SPLIT, D, c.T), F32).ap()
        c.v_dram = nc.dram_tensor("values_scratch", (NKV + NH, P, c.T // P, HD), F32).ap()

        def part(prefix, matrices):
            return {k[len(prefix):]: (tiled(v) if k[len(prefix):] in matrices else v) for k, v in a.items() if k.startswith(prefix)}

        c.rel = part("rel_", ("W_q", "W_k", "W_v", "W_o"))
        c.loc = part("loc_", ())
        c.cff = part("cff_", ("W1", "W2"))
        c.rec = part("rec_", ("Wq", "Wk", "Wv", "Wo"))
        c.moe = part("moe_", ("gate_w",))

        def cross(name, wq, groups, v_dram, heads_per_v, bias, keys_dram, wo, base, dst):
            with ExitStack() as mem:
                c.qm = mem.enter_context(nc.sbuf_tensor(f"{name}_queries", [P, NH, S], F32R))
                c.attn = mem.enter_context(nc.sbuf_tensor(f"{name}_attn", [S, D], F32))
                c.scores = [mem.enter_context(nc.sbuf_tensor(f"{name}_scores{i}", [P, c.T], F32)) for i in range(2)]
                c.keys = mem.enter_context(nc.sbuf_tensor(f"{name}_keys", [P, c.T], F32R))
                c.run(queries, name, wq, groups, keys_dram)
                c.run(attention, name, v_dram, heads_per_v, bias, keys_dram)
                c.run(project_out, name, wo, base, dst)

        c.run(consts)
        c.run(context_products)
        cross("gqa", tiled(a["wqA"]), True, c.v_dram[0:NKV], GRP, None, c.k1_dram, tiled(a["woA"]), c.x, c.x)
        c.run(relative_attention)
        c.run(local_transformer)
        cross("biased", tiled(a["wqD"]), False, c.v_dram[NKV:], 1, a["bias"], c.k2_dram, tiled(a["woD"]), c.xn, c.z)
        c.run(biased_feed_forward)
        c.run(gated_recurrence)
        c.run(experts)
        c.run(store_x, out)


def lay_out(i):
    import numpy as _np
    t = {k: _np.asarray(v) for k, v in i.items()}

    def repeated(w):
        return _np.repeat(w.reshape(D, NH // KG, 1, KR), KREP, axis=2).reshape(D, -1)

    def part(prefix):
        return {k[len(prefix):]: v for k, v in t.items() if k.startswith(prefix)}

    gqa, rel, bia = part("L0_xattn_"), part("L0_attn_"), part("L1_xattn_")
    out = {
        "x": t["x"][0], "ctxT": t["ctx_1024"][0].T, "bias": t["fside_Bx16xSxS2_0"][0],
        "wqA": repeated(gqa["Wq"].reshape(NKV // KG, KG, GRP, HD, D).transpose(4, 0, 2, 1, 3)),
        "wkA": gqa["Wk"].T, "wvA": gqa["Wv"].T, "woA": gqa["Wo"].T,
        "wqD": repeated(bia["Wq"].T), "wkD": bia["Wk"].T, "wvD": bia["Wv"].T, "woD": bia["Wo"].T,
    }
    for n in "qk":
        rel[f"b_{n}"] = rel[f"b_{n}"].reshape(KT, P).T
    rel["rel_kT"] = rel.pop("rel_k_table").T
    cff = {"W1": bia["W1"].T, "W2": bia["W2"].T, "rows": _np.stack([bia["b2"], bia["g2"], bia["be2"]]),
           "cols": _np.concatenate([bia["g1"].reshape(KT, P).T, bia["be1"].reshape(KT, P).T, bia["b1"].reshape(CT, P).T], 1)}
    parts = {"rel_": rel, "loc_": lay_out_local(part("L0_ffn_")), "cff_": cff,
             "rec_": lay_out_recurrence(part("L1_attn_")), "moe_": lay_out_experts(part("L1_ffn_"))}
    for prefix, p in parts.items():
        out.update({prefix + k: v for k, v in p.items()})
    return out


def kernel(**inputs):
    import numpy as _np
    import concourse.bacc as _bacc
    from concourse import mybir as _mybir
    from concourse.bass_utils import run_bass_kernel_spmd as _run

    nc = _bacc.Bacc("TRN2", target_bir_lowering=False, num_devices=1)
    arrays, aps = {}, {}
    for name, a in lay_out(inputs).items():
        a = _np.ascontiguousarray(a)
        arrays[f"in_{name}"] = a
        aps[name] = nc.dram_tensor(f"in_{name}", a.shape, _mybir.dt.from_np(a.dtype), kind="ExternalInput").ap()
    out = nc.dram_tensor("out_x", (1, S, D), F32, kind="ExternalOutput").ap()
    program(nc, aps, out)
    r = _run(nc, [arrays], core_ids=[0])
    return r.results[0]["out_x"]
```
